# Optimizing a Trainium2 kernel written in Bass

```python
import numpy as np
import jax
import jax.numpy as jnp

def _softmax(x, axis=-1):
    return jax.nn.softmax(x, axis=axis)

def _gelu(x):
    return jax.nn.gelu(x, approximate=True)

def _silu(x):
    return jax.nn.silu(x)

def _sigmoid(x):
    return jax.nn.sigmoid(x)

def _layernorm(x, axis=-1, eps=1e-05):
    m = jnp.mean(x, axis=axis, keepdims=True)
    v = jnp.var(x, axis=axis, keepdims=True)
    return (x - m) / jnp.sqrt(v + eps)

def _scatter_add(tgt, idx, src, axis=0):
    return tgt.at[idx].add(src)

def _segment_sum(src, seg, n):
    return jax.ops.segment_sum(src, seg, n)
kernel_name = 'mk_macaron_d1_jaxref_r4_8cde1e'

def setup_inputs(seed: int=0):
    np.random.seed(seed)
    _w = jnp.asarray

    def _L0_attn_setup():
        import jax, jax.numpy as jnp
        import numpy as np
        D_MODEL, D_INNER, D_STATE, D_CONV, DT_RANK = (256, 512, 16, 4, 64)
        B, T = (2, 512)

        def rmsnorm(x):
            eps = jnp.asarray(jnp.finfo(x.dtype).eps, x.dtype)
            return x * jax.lax.rsqrt(jnp.mean(jnp.square(x), axis=-1, keepdims=True) + eps)

        def silu(x):
            return x * jax.nn.sigmoid(x)

        def mamba(xn, in_proj_w, conv_w, conv_b, x_proj_w, dt_proj_w, dt_proj_b, A_log, D, out_proj_w):
            b, t, _ = xn.shape
            xz = jnp.einsum('btd,ed->bte', xn, in_proj_w)
            x_in, z = jnp.split(xz, 2, axis=-1)
            x_pad = jnp.pad(x_in, ((0, 0), (D_CONV - 1, 0), (0, 0)))
            x_conv = sum((conv_w[:, k] * x_pad[:, k:k + t, :] for k in range(D_CONV))) + conv_b
            x_conv = silu(x_conv)
            x_dbl = jnp.einsum('bte,fe->btf', x_conv, x_proj_w)
            dt_low = x_dbl[..., :DT_RANK]
            B_ssm = x_dbl[..., DT_RANK:DT_RANK + D_STATE]
            C_ssm = x_dbl[..., DT_RANK + D_STATE:]
            dt = jax.nn.softplus(jnp.einsum('btr,er->bte', dt_low, dt_proj_w) + dt_proj_b)
            A = -jnp.exp(A_log)

            def step(h, inp):
                dt_t, B_t, C_t, u_t = inp
                dA = jnp.exp(dt_t[..., None] * A)
                h = h * dA + (dt_t * u_t)[..., None] * B_t[:, None, :]
                y = jnp.einsum('bes,bs->be', h, C_t)
                return (h, y)
            tm = lambda a: jnp.swapaxes(a, 0, 1)
            h0 = jnp.zeros((b, D_INNER, D_STATE), xn.dtype)
            _, ys = jax.lax.scan(step, h0, (tm(dt), tm(B_ssm), tm(C_ssm), tm(x_conv)))
            y = tm(ys) + x_conv * D
            y = y * silu(z)
            return jnp.einsum('bte,de->btd', y, out_proj_w)
        key = jax.random.key(seed)
        ks = jax.random.split(key, 12)
        s = 0.02
        A_log = jnp.log(jnp.broadcast_to(jnp.arange(1, D_STATE + 1, dtype=jnp.float32), (D_INNER, D_STATE)))
        return {'x': jax.random.normal(ks[0], (B, T, D_MODEL), jnp.float32), 'in_proj_w': jax.random.normal(ks[1], (2 * D_INNER, D_MODEL), jnp.float32) * s, 'conv_w': jax.random.normal(ks[2], (D_INNER, D_CONV), jnp.float32) * 0.2, 'conv_b': jax.random.normal(ks[3], (D_INNER,), jnp.float32) * s, 'x_proj_w': jax.random.normal(ks[4], (DT_RANK + 2 * D_STATE, D_INNER), jnp.float32) * s, 'dt_proj_w': jax.random.normal(ks[5], (D_INNER, DT_RANK), jnp.float32) * 0.1, 'dt_proj_b': jax.random.normal(ks[6], (D_INNER,), jnp.float32) * 0.1 - 4.0, 'A_log': A_log, 'D': jax.random.normal(ks[7], (D_INNER,), jnp.float32) * s, 'out_proj_w': jax.random.normal(ks[8], (D_MODEL, D_INNER), jnp.float32) * s, 'c_fc_w': jax.random.normal(ks[9], (2 * D_MODEL, D_MODEL), jnp.float32) * s, 'c_proj_w': jax.random.normal(ks[10], (D_MODEL, 2 * D_MODEL), jnp.float32) * s}
    _L0_attn_in = _L0_attn_setup()

    def _L0_ffn_setup():
        import math
        import jax, jax.numpy as jnp
        import numpy as np
        B, L, D, FF, E, K = (4, 512, 256, 1024, 8, 2)
        CAPACITY_FACTOR = 1.25
        T = B * L
        CAP = math.ceil(CAPACITY_FACTOR * T * K / E)
        key = jax.random.key(seed)
        ks = jax.random.split(key, 7)
        return {'h': jax.random.normal(ks[0], (B, L, D), dtype=jnp.float32), 'gate_w': 0.02 * jax.random.normal(ks[1], (E, D), dtype=jnp.float32), 'gate_b': jnp.zeros((E,), dtype=jnp.float32), 'W1': 0.02 * jax.random.normal(ks[2], (E, D, FF), dtype=jnp.float32), 'b1': jnp.zeros((E, FF), dtype=jnp.float32), 'W2': 0.02 * jax.random.normal(ks[3], (E, FF, D), dtype=jnp.float32), 'b2': jnp.zeros((E, D), dtype=jnp.float32)}
    _L0_ffn_in = _L0_ffn_setup()
    _d = {'L0_attn_x': _L0_attn_in['x'], 'L0_attn_in_proj_w': _L0_attn_in['in_proj_w'], 'L0_attn_conv_w': _L0_attn_in['conv_w'], 'L0_attn_conv_b': _L0_attn_in['conv_b'], 'L0_attn_x_proj_w': _L0_attn_in['x_proj_w'], 'L0_attn_dt_proj_w': _L0_attn_in['dt_proj_w'], 'L0_attn_dt_proj_b': _L0_attn_in['dt_proj_b'], 'L0_attn_A_log': _L0_attn_in['A_log'], 'L0_attn_D': _L0_attn_in['D'], 'L0_attn_out_proj_w': _L0_attn_in['out_proj_w'], 'L0_attn_c_fc_w': _L0_attn_in['c_fc_w'], 'L0_attn_c_proj_w': _L0_attn_in['c_proj_w'], 'L0_ffn_gate_w': _L0_ffn_in['gate_w'], 'L0_ffn_gate_b': _L0_ffn_in['gate_b'], 'L0_ffn_W1': _L0_ffn_in['W1'], 'L0_ffn_b1': _L0_ffn_in['b1'], 'L0_ffn_W2': _L0_ffn_in['W2'], 'L0_ffn_b2': _L0_ffn_in['b2']}
    _x0 = _d['L0_attn_x']
    _d['L0_attn_x'] = jax.random.normal(jax.random.fold_in(jax.random.key(seed), 1), (2, 2048, 256), dtype=_x0.dtype)
    del _x0
    return _d

def reference(L0_attn_x, L0_attn_in_proj_w, L0_attn_conv_w, L0_attn_conv_b, L0_attn_x_proj_w, L0_attn_dt_proj_w, L0_attn_dt_proj_b, L0_attn_A_log, L0_attn_D, L0_attn_out_proj_w, L0_attn_c_fc_w, L0_attn_c_proj_w, L0_ffn_gate_w, L0_ffn_gate_b, L0_ffn_W1, L0_ffn_b1, L0_ffn_W2, L0_ffn_b2):

    def _L0_attn_ref(x, in_proj_w, conv_w, conv_b, x_proj_w, dt_proj_w, dt_proj_b, A_log, D, out_proj_w, c_fc_w, c_proj_w):
        import jax, jax.numpy as jnp
        import numpy as np
        D_MODEL, D_INNER, D_STATE, D_CONV, DT_RANK = (256, 512, 16, 4, 64)
        B, T = (2, 512)

        def rmsnorm(x):
            eps = jnp.asarray(jnp.finfo(x.dtype).eps, x.dtype)
            return x * jax.lax.rsqrt(jnp.mean(jnp.square(x), axis=-1, keepdims=True) + eps)

        def silu(x):
            return x * jax.nn.sigmoid(x)

        def mamba(xn, in_proj_w, conv_w, conv_b, x_proj_w, dt_proj_w, dt_proj_b, A_log, D, out_proj_w):
            b, t, _ = xn.shape
            xz = jnp.einsum('btd,ed->bte', xn, in_proj_w)
            x_in, z = jnp.split(xz, 2, axis=-1)
            x_pad = jnp.pad(x_in, ((0, 0), (D_CONV - 1, 0), (0, 0)))
            x_conv = sum((conv_w[:, k] * x_pad[:, k:k + t, :] for k in range(D_CONV))) + conv_b
            x_conv = silu(x_conv)
            x_dbl = jnp.einsum('bte,fe->btf', x_conv, x_proj_w)
            dt_low = x_dbl[..., :DT_RANK]
            B_ssm = x_dbl[..., DT_RANK:DT_RANK + D_STATE]
            C_ssm = x_dbl[..., DT_RANK + D_STATE:]
            dt = jax.nn.softplus(jnp.einsum('btr,er->bte', dt_low, dt_proj_w) + dt_proj_b)
            A = -jnp.exp(A_log)

            def step(h, inp):
                dt_t, B_t, C_t, u_t = inp
                dA = jnp.exp(dt_t[..., None] * A)
                h = h * dA + (dt_t * u_t)[..., None] * B_t[:, None, :]
                y = jnp.einsum('bes,bs->be', h, C_t)
                return (h, y)
            tm = lambda a: jnp.swapaxes(a, 0, 1)
            h0 = jnp.zeros((b, D_INNER, D_STATE), xn.dtype)
            _, ys = jax.lax.scan(step, h0, (tm(dt), tm(B_ssm), tm(C_ssm), tm(x_conv)))
            y = tm(ys) + x_conv * D
            y = y * silu(z)
            return jnp.einsum('bte,de->btd', y, out_proj_w)
        x = x + mamba(rmsnorm(x), in_proj_w, conv_w, conv_b, x_proj_w, dt_proj_w, dt_proj_b, A_log, D, out_proj_w)
        h = rmsnorm(x)
        h = jnp.square(jax.nn.relu(jnp.einsum('btd,ed->bte', h, c_fc_w)))
        x = x + jnp.einsum('bte,de->btd', h, c_proj_w)
        return x

    def _L0_ffn_ref(h, gate_w, gate_b, W1, b1, W2, b2):
        import math
        import jax, jax.numpy as jnp
        import numpy as np
        B, L, D, FF, E, K = (4, 512, 256, 1024, 8, 2)
        CAPACITY_FACTOR = 1.25
        T = B * L
        CAP = math.ceil(CAPACITY_FACTOR * T * K / E)
        Bb, Ll, Dm = h.shape
        Tt = Bb * Ll
        x = h.reshape(Tt, Dm)
        logits = x @ gate_w.T + gate_b
        probs = jax.nn.softmax(logits, axis=-1)
        topk_prob, topk_idx = jax.lax.top_k(probs, K)
        y = jnp.zeros((Tt, Dm), dtype=h.dtype)
        n_slots = E * CAP
        for c in range(K):
            idx = topk_idx[:, c]
            prb = topk_prob[:, c]
            oh = jax.nn.one_hot(idx, E, dtype=jnp.int32)
            pos = jnp.take_along_axis(jnp.cumsum(oh, axis=0) - 1, idx[:, None], axis=1)[:, 0]
            keep = pos < CAP
            buf_idx = jnp.where(keep, idx * CAP + pos, n_slots)
            xbuf = jnp.zeros((n_slots, Dm), x.dtype).at[buf_idx].set(x, mode='drop')
            xb = xbuf.reshape(E, CAP, Dm)
            hmid = jax.nn.relu(jnp.einsum('ecd,edf->ecf', xb, W1) + b1[:, None, :])
            yb = jnp.einsum('ecf,efd->ecd', hmid, W2) + b2[:, None, :]
            ytok = yb.reshape(n_slots, Dm)[jnp.clip(buf_idx, 0, n_slots - 1)]
            y = y + ytok * (prb * keep.astype(prb.dtype))[:, None]
        return y.reshape(Bb, Ll, Dm)
    x = L0_attn_x
    x = x + 0.5 * _L0_ffn_ref(_layernorm(x, axis=-1), L0_ffn_gate_w, L0_ffn_gate_b, L0_ffn_W1, L0_ffn_b1, L0_ffn_W2, L0_ffn_b2)
    x = x + _L0_attn_ref(_layernorm(x, axis=-1), L0_attn_in_proj_w, L0_attn_conv_w, L0_attn_conv_b, L0_attn_x_proj_w, L0_attn_dt_proj_w, L0_attn_dt_proj_b, L0_attn_A_log, L0_attn_D, L0_attn_out_proj_w, L0_attn_c_fc_w, L0_attn_c_proj_w)
    x = x + 0.5 * _L0_ffn_ref(_layernorm(x, axis=-1), L0_ffn_gate_w, L0_ffn_gate_b, L0_ffn_W1, L0_ffn_b1, L0_ffn_W2, L0_ffn_b2)
    return x

_drawn_inputs = setup_inputs


def setup_inputs(seed=0):
    import zlib

    import numpy as np

    out = dict(_drawn_inputs(seed))
    spreads = {'L0_ffn_gate_b': (0.0, 0.1), 'L0_ffn_b1': (0.0, 0.1), 'L0_ffn_b2': (0.0, 0.1)}
    factors = {}
    for name, (base, spread) in spreads.items():
        noise = np.random.default_rng([zlib.crc32(name.encode()), seed]).standard_normal(out[name].shape)
        drawn = base * np.exp(spread * noise) if base else spread * noise
        out[name] = jnp.asarray(drawn.astype(out[name].dtype))
    for name, factor in factors.items():
        out[name] = (out[name] * factor).astype(out[name].dtype)
    return out
```

```python
import concourse.bass as bass
from concourse import mybir
from contextlib import ExitStack

FP32 = mybir.dt.float32
FP32R = mybir.dt.float32r
BF16 = mybir.dt.bfloat16
U32 = mybir.dt.uint32
ALU = mybir.AluOpType
ACT = mybir.ActivationFunctionType
AX = mybir.AxisListType

P = 128
TOKENS, D = 4096, 256
BATCH = 2
TT = TOKENS // P
DK = D // P
EXPERTS, FF, TOPK = 8, 1024, 2
CAP = 640
ROWS_E = TOPK * CAP
ROWS = EXPERTS * ROWS_E
CH = 256
CPE = ROWS_E // CH
CHT = CH // P
NCHUNK = EXPERTS * CPE
FK = FF // P
FP = FK // 2
DROPPED = 20000
LN_EPS = 1e-5
RMS_EPS = 1.1920928955078125e-07

DI, DS, DC, DR = 512, 16, 4, 64
EK = DI // P
CT = 512
CTT = CT // P
MCH = TOKENS // CT
XPR = DR + 2 * DS
W_IN, W_XP = 0, DK * 2 * DI
W_DT = W_XP + EK * XPR
W_OUT = W_DT + DI
W_FC = W_OUT + EK * D
W_PJ = W_FC + DK * 2 * D
W_ALL = W_PJ + EK * D
C_CW, C_CB, C_DB, C_D, C_AL, C_ALL = 0, 4, 5, 6, 7, 7 + DS


def sem_maker(nc, C, tag):
    def get(name, own=False):
        full = f"{tag}_{name}" if own else f"{tag[0]}_{name}"
        if full not in C["sems"]:
            C["sems"][full] = C["whole"].enter_context(nc.semaphore(full))
        return C["sems"][full]

    return get


def buf_maker(nc, ctx, tag):
    return lambda name, shape, dt=FP32: ctx.enter_context(nc.sbuf_tensor(f"{tag}_{name}", shape, dt))


def chain(eng, sem):
    count = [0]

    def link(instruction):
        count[0] += 1
        instruction.then_inc(sem, 1)
        eng.wait_ge(sem, count[0])

    return link


def route(nc, tag, X, C, PS, R, xrows, x_dram, zero_rows):
    ctx = ExitStack()
    with ctx:
        sem, sb = sem_maker(nc, C, tag), buf_maker(nc, ctx, tag)
        st = sb("stats", [P, TT, 6])
        small = sb("small", [P, 6, TT])
        mean, rstd, dif, mhalf = small[:, 0, :], small[:, 1, :], small[:, 2, :], small[:, 3, :]
        xn = sb("xn", [P, 2, 4, D])
        xnT = sb("xnT", [P, 2, DK, 4 * P])
        lg = sb("lg", [P, TT, EXPERTS])
        pr = sb("pr", [P, TT, EXPERTS])
        w1 = sb("w1", [P, TT, EXPERTS])
        w2 = sb("w2", [P, TT, EXPERTS])
        red = sb("red", [P, 4, TT])
        oh = sb("oh", [P, TOPK, TT, EXPERTS])
        ohb = sb("ohb", [P, TOPK, TT, EXPERTS], BF16)
        pos = sb("pos", [P, TOPK, TT, EXPERTS])
        tot = sb("tot", [P, TOPK, TT, EXPERTS])
        inc = sb("inc", [P, TOPK, TT, EXPERTS])
        zcol = sb("zcol", [P, TT])
        base = sb("base", [P, TOPK, EXPERTS])
        slot = sb("slot", [P, TOPK, TT])
        xs = sb("xs", [P, 4, D])
        ixs = sb("ixs", [P, 4, TOPK], U32)
        zrow = sb("zrow", [P, 2048])

        x_in = [sem(f"x_in{q}") for q in range(4)]
        zero_set, zeroed = sem("zero_set"), sem("zeroed")
        dch, var_ok, rstd_ok = sem("dch"), sem("var_ok"), sem("rstd_ok")
        xn_ok, tp_ok, xnT_ok, lgp_ok, lg_ok = sem("xn_ok"), sem("tp_ok"), sem("xnT_ok"), sem("lgp_ok"), sem("lg_ok")
        sh_ok, ex_ok, ohb_ok, cum_ok = sem("sh_ok"), sem("ex_ok"), sem("ohb_ok"), sem("cum_ok")
        xs_ok, turned = sem("xs_ok"), sem("turned")
        sent = [[sem(f"sent{b}_{c}", own=True) for c in range(TOPK)] for b in range(4)]
        block = ctx.enter_context(nc.Block())
        Q = TT // 4

        @block.sync
        def _(sp):
            if x_dram is not None:
                for q in range(4):
                    sp.dma_start(X[:, q * Q:(q + 1) * Q, :],
                                 x_dram[q * Q * P:(q + 1) * Q * P, :].rearrange("(t p) d -> p t d", p=P)).then_inc(x_in[q], 16)
            if zero_rows:
                sp.wait_ge(zero_set, 1)
                rows = 8 * P
                for r in range(ROWS // rows):
                    sp.dma_start(xrows[r * rows:(r + 1) * rows, :].rearrange("(p a) d -> p (a d)", p=P),
                                 zrow[:, :]).then_inc(zeroed, 16)

        @block.vector
        def _(dve):
            V = nc.vector
            link = chain(dve, dch)
            V.memset(zrow[:, :], 0.0).then_inc(zero_set, 1)
            V.memset(mhalf, -0.5)
            V.memset(zcol[:, :], 1.0)
            for q in range(4):
                if x_dram is not None:
                    dve.wait_ge(x_in[q], 16)
                with dve.Fori(q * Q, (q + 1) * Q, 1) as t:
                    V.bn_stats(st[:, bass.ds(t, 1), :].rearrange("p o s -> p (o s)"),
                               X[:, bass.ds(t, 1), :].rearrange("p o d -> p (o d)"))
            link(V.memset(red[:, 0, :], 0.0))
            link(V.tensor_tensor(mean, st[:, :, 1], st[:, :, 4], ALU.add))
            V.tensor_tensor(dif, st[:, :, 1], st[:, :, 4], ALU.subtract)
            link(V.tensor_tensor(rstd, st[:, :, 2], st[:, :, 5], ALU.add))
            link(V.tensor_scalar(mean, mean, 0.5, None, ALU.mult))
            link(V.tensor_tensor(dif, dif, dif, ALU.mult))
            link(V.tensor_scalar(dif, dif, 0.25, LN_EPS, ALU.mult, ALU.add))
            V.scalar_tensor_tensor(rstd, rstd, 1.0 / D, dif, ALU.mult, ALU.add).then_inc(var_ok, 1)
            dve.wait_ge(rstd_ok, 1)

            def normed(out, t):
                return V.tensor_scalar(out, X[:, bass.ds(t, 1), :].rearrange("p o d -> p (o d)"),
                                       mean[:, bass.ds(t, 1)], rstd[:, bass.ds(t, 1)], ALU.subtract, ALU.mult)

            with dve.Fori(0, TT // 8, 1) as i:
                for g in range(2):
                    for a in range(4):
                        last = normed(xn[:, g, a, :], i * 8 + (g * 4 + a))
                    last.then_inc(xn_ok, 1)
                for g in range(2):
                    dve.wait_ge(lgp_ok, i * 2 + (g + 1))
                    V.tensor_tensor(lg[:, bass.ds(i * 8 + g * 4, 4), :],
                                    PS[:, 4 + g, 0:4 * EXPERTS].rearrange("p (t e) -> p t e", e=EXPERTS),
                                    C["gb"][:, :].unsqueeze(1).to_broadcast([P, 4, EXPERTS]), ALU.add).then_inc(lg_ok, 1)
            dve.wait_ge(lg_ok, TT // 4)
            bc = lambda a: a.unsqueeze(2).to_broadcast([P, TT, EXPERTS])
            link(V.tensor_reduce(red[:, 0, :], lg[:, :, :], AX.X, ALU.max))
            V.tensor_tensor(lg[:, :, :], lg[:, :, :], bc(red[:, 0, :]), ALU.subtract).then_inc(sh_ok, 1)
            dve.wait_ge(ex_ok, 1)
            link(V.tensor_reduce(red[:, 1, :], lg[:, :, :], AX.X, ALU.add))
            link(V.reciprocal(red[:, 1, :], red[:, 1, :]))
            link(V.tensor_tensor(pr[:, :, :], lg[:, :, :], bc(red[:, 1, :]), ALU.mult))
            rank = C["rank"][:, :].unsqueeze(1).to_broadcast([P, TT, EXPERTS])
            for c in range(TOPK):
                wc = R["w"][:, c, :]
                link(V.tensor_reduce(wc, pr[:, :, :], AX.X, ALU.max))
                link(V.tensor_tensor(w1[:, :, :], pr[:, :, :], bc(wc), ALU.is_equal))
                link(V.tensor_tensor(w1[:, :, :], w1[:, :, :], rank, ALU.mult))
                link(V.tensor_reduce(red[:, 2, :], w1[:, :, :], AX.X, ALU.max))
                link(V.tensor_tensor(oh[:, c, :, :], w1[:, :, :], bc(red[:, 2, :]), ALU.is_equal))
                if c == 0:
                    link(V.scalar_tensor_tensor(pr[:, :, :], oh[:, 0, :, :], -2.0, pr[:, :, :], ALU.mult, ALU.add))
            V.tensor_copy(ohb[:, :, :, :], oh[:, :, :, :]).then_inc(ohb_ok, 1)
            dve.wait_ge(cum_ok, 1)
            f = lambda a: a[:, :, :, :].rearrange("p c t e -> p (c t e)")
            link(V.tensor_copy(f(tot), PS[:, 1, :]))
            for c in range(TOPK):
                for e in range(EXPERTS):
                    last = V.tensor_tensor_scan(inc[:, c, :, e], zcol[:, :], tot[:, c, :, e], 0.0, ALU.mult, ALU.add)
            link(last)
            link(V.tensor_tensor(f(pos), PS[:, 0, :], f(inc), ALU.add))
            link(V.scalar_tensor_tensor(f(pos), f(pos), -1.0, f(tot), ALU.add, ALU.subtract))
            link(V.scalar_tensor_tensor(f(oh), f(pos), float(CAP), f(oh), ALU.is_lt, ALU.mult))
            V.tensor_scalar(base[:, 0, :], C["region"][:, :], -float(DROPPED), None, ALU.add)
            link(V.tensor_scalar(base[:, 1, :], inc[:, 0, TT - 1, :], float(CAP), -float(DROPPED), ALU.min, ALU.add))
            link(V.tensor_tensor(base[:, 1, :], base[:, 1, :], C["region"][:, :], ALU.add))
            for c in range(TOPK):
                link(V.tensor_tensor(w1[:, :, :], pos[:, c, :, :],
                                     base[:, c, :].unsqueeze(1).to_broadcast([P, TT, EXPERTS]), ALU.add))
                link(V.tensor_tensor(w1[:, :, :], w1[:, :, :], oh[:, c, :, :], ALU.mult))
                link(V.tensor_reduce(slot[:, c, :], w1[:, :, :], AX.X, ALU.add))
                V.tensor_reduce(red[:, 2 + c, :], oh[:, c, :, :], AX.X, ALU.add)
            link(V.tensor_scalar(slot[:, :, :], slot[:, :, :], float(DROPPED), None, ALU.add))
            link(V.tensor_copy(R["idx"][:, :, :], slot[:, :, :]))
            link(V.scalar_tensor_tensor(R["w"][:, :, :], R["w"][:, :, :], 0.5, red[:, 2:4, :], ALU.mult, ALU.mult))
            def fill(i, first=False):
                for b in range(4):
                    if not first:
                        for c in range(TOPK):
                            dve.wait_ge(sent[b][c], i * 16)
                    normed(xs[:, b, :], i * 4 + b)
                    V.tensor_copy(ixs[:, b, :], R["idx"][:, :, bass.ds(i * 4 + b, 1)].rearrange("p c o -> p (c o)")).then_inc(xs_ok, 1)

            fill(0, first=True)
            with dve.Fori(1, TT // 4, 1) as i:
                fill(i)

        @block.gpsimd
        def _(gp):
            G = nc.gpsimd
            gp.wait_ge(var_ok, 1)
            G.tensor_tensor(rstd, rstd, mhalf, ALU.pow).then_inc(rstd_ok, 1)
            bound = gp.to_reg(ROWS - 1)
            if zero_rows:
                gp.wait_ge(zeroed, 16 * (ROWS // (8 * P)))
            with gp.Fori(0, TT // 4, 1) as i:
                for b in range(4):
                    gp.wait_ge(xs_ok, i * 4 + (b + 1))
                    gp.sem_inc(turned, 1)
                    for c in range(TOPK):
                        G.indirect_dma_start(out=xrows, out_offset=bass.IndirectOffsetOnAxis(ap=ixs[:, b, c:c + 1], axis=0),
                                             in_=xs[:, b, :], in_offset=None, bounds_check=bound,
                                             oob_is_err=False).then_inc(sent[b][c], 16)
            for b in range(4):
                for c in range(TOPK):
                    gp.wait_ge(sent[b][c], 16 * (TT // 4))

        @block.scalar
        def _(act):
            with act.Fori(0, TT // 8, 1) as i:
                for g in range(2):
                    act.wait_ge(tp_ok, i * 2 + (g + 1))
                    nc.scalar.activation(xnT[:, g, :, :], PS[:, 2 * g:2 * g + 2, :], ACT.Copy).then_inc(xnT_ok, 1)
            act.wait_ge(sh_ok, 1)
            nc.scalar.activation(lg[:, :, :], lg[:, :, :], ACT.Exp).then_inc(ex_ok, 1)

        @block.tensor
        def _(pe):
            with pe.Fori(0, TT // 8, 1) as i:
                for g in range(2):
                    pe.wait_ge(xn_ok, i * 2 + (g + 1))
                    for k in range(DK):
                        for a in range(4):
                            last = nc.tensor.transpose(PS[:, 2 * g + k, a * P:(a + 1) * P], xn[:, g, a, k * P:(k + 1) * P],
                                                       C["ident"][:, :])
                    last.then_inc(tp_ok, 1)
                for g in range(2):
                    pe.wait_ge(xnT_ok, i * 2 + (g + 1))
                    for a in range(4):
                        for k in range(DK):
                            last = nc.tensor.matmul(PS[:, 4 + g, a * EXPERTS:(a + 1) * EXPERTS],
                                                    xnT[:, g, k, a * P:(a + 1) * P], C["gate"][:, k, :],
                                                    start=(k == 0), stop=(k == DK - 1))
                    last.then_inc(lgp_ok, 1)
            pe.wait_ge(lg_ok, TT // 4)
            pe.wait_ge(ohb_ok, 1)
            ohf = ohb[:, :, :, :].rearrange("p c t e -> p (c t e)")
            nc.tensor.matmul(PS[:, 0, :], C["upper"][:, :], ohf, start=True, stop=True)
            nc.tensor.matmul(PS[:, 1, :], C["onesb"][:, :], ohf, start=True, stop=True).then_inc(cum_ok, 1)


def experts(nc, tag, C, PS, xrows, yrows, W1, W2, b2):
    ctx = ExitStack()
    with ctx:
        sem, sb = sem_maker(nc, C, tag), buf_maker(nc, ctx, tag)
        raw = sb("raw", [P, 4, FF])
        wh = sb("wh", [P, 2, 4, FF], FP32R)
        wl = sb("wl", [P, 2, 4, FF], FP32R)
        xin = sb("xin", [P, 2, CHT, D])
        xh = sb("xh", [P, 2, DK, CH], FP32R)
        xl = sb("xl", [P, 2, DK, CH], FP32R)
        u = sb("u", [P, FP, 2, CH])
        hh = sb("hh", [P, 2, FK, CH], FP32R)
        hl = sb("hl", [P, 2, FK, CH], FP32R)
        ysb = sb("ysb", [P, 2, CHT, D])
        b2_all = sb("b2", [P, EXPERTS, D])
        b2_in = sem("b2_in")
        wraw = [sem(f"wraw{q}") for q in range(4)]
        wh_ok, wl_ok = sem("wh_ok"), sem("wl_ok")
        xin_ok = [sem(f"xin{b}") for b in range(2)]
        xT_ok, xh_ok, xl_ok = sem("xT_ok"), sem("xh_ok"), sem("xl_ok")
        s1_ok, u_ok, hh_ok, hl_ok = sem("s1_ok"), sem("u_ok"), sem("hh_ok"), sem("hl_ok")
        y_ok, yb_ok = sem("y_ok"), sem("yb_ok")
        stored, ysb_free = [sem(f"stored{b}", own=True) for b in range(2)], sem("ysb_free")
        block = ctx.enter_context(nc.Block())
        B_XT, B_S1, B_Y = 0, 1, 5
        TURN = 2 * CPE
        Y0, YB0, YF0 = 1, 2, 2

        def chunks(eng, step):
            with eng.Fori(0, EXPERTS // 2 - 1, 1) as i:
                for c in range(TURN):
                    step(i, c, False)
            for c in range(TURN):
                step(EXPERTS // 2 - 1, c, True)

        @block.sync
        def _(sp):
            def load_x(i, c):
                sp.dma_start(xin[:, c % 2, :, :],
                             xrows[bass.ds(i * (TURN * CH) + c * CH, CH), :].rearrange("(t p) d -> p t d", p=P)).then_inc(xin_ok[c % 2], 16)

            def load_w(e, q):
                if q < 2:
                    src = W1[bass.ds(e, 1), q * P:(q + 1) * P, :].rearrange("o p f -> p (o f)")
                    sp.dma_start(raw[:, q, :], src).then_inc(wraw[q], 16)
                else:
                    src = W2[bass.ds(e, 1), (q - 2) * 4 * P:(q - 1) * 4 * P, :].rearrange("o (j p) d -> p (o j) d", p=P)
                    sp.dma_start(raw[:, q, :].rearrange("p (j d) -> p j d", d=D), src).then_inc(wraw[q], 16)

            load_x(0, 0)
            load_x(0, 1)
            for q in range(4):
                load_w(0, q)
            sp.dma_start(b2_all[:, :, :].rearrange("p e d -> p (e d)"), b2.to_broadcast([P, EXPERTS * D])).then_inc(b2_in, 16)

            def step(i, c, last):
                e2, j = divmod(c, CPE)
                if j < 4 and not (last and e2 == 1):
                    sp.wait_ge(wl_ok, i * 8 + (4 * e2 + j + 1))
                    load_w(i * 2 + (e2 + 1), j)
                if not (last and c + 2 >= TURN):
                    sp.wait_ge(xT_ok, i * TURN + (c + 1))
                    load_x(i, c + 2)

            chunks(sp, step)

        @block.gpsimd
        def _(gp):
            def step(i, c, last):
                gp.wait_ge(yb_ok, i * TURN + (c + 1 + YB0))
                gp.dma_start(yrows[bass.ds(i * (TURN * CH) + c * CH, CH), :].rearrange("(t p) d -> p t d", p=P),
                             ysb[:, c % 2, :, :]).then_inc(stored[c % 2], 16)
                gp.wait_ge(stored[c % 2], i * (16 * CPE) + 16 * (c // 2 + 1))
                gp.sem_inc(ysb_free, 1)

            chunks(gp, step)

        @block.tensor
        def _(pe):
            M = nc.tensor.matmul
            pe.sem_inc(y_ok, Y0)

            def turn(i, c, first=False):
                pe.wait_ge(xin_ok[c % 2], i * (16 * CPE) + 16 * (c // 2 + 1))
                if not first:
                    pe.wait_ge(xl_ok, i * TURN + c)
                for k in range(DK):
                    for t in range(CHT):
                        last = nc.tensor.transpose(PS[:, B_XT, k * CH + t * P:k * CH + (t + 1) * P],
                                                   xin[:, c % 2, t, k * P:(k + 1) * P], C["ident"][:, :])
                last.then_inc(xT_ok, 1)

            def up(i, c, first=False):
                e2, j = divmod(c, CPE)
                w = e2 % 2
                if j == 0:
                    pe.wait_ge(wl_ok, i * 8 + (4 * e2 + 2))
                pe.wait_ge(xl_ok, i * TURN + (c + 1))
                for pair in range(FP):
                    if not first:
                        pe.wait_ge(u_ok, i * (TURN * FP) + ((c - 1) * FP + pair + 1))
                    for m in range(2):
                        f = slice((2 * pair + m) * P, (2 * pair + m + 1) * P)
                        terms = [(wx[:, w, k, f], rx[:, c % 2, k, :]) for k in range(DK)
                                 for wx, rx in ((wh, xh), (wh, xl), (wl, xh))]
                        for n, (a, r) in enumerate(terms):
                            last = M(PS[:, B_S1 + pair, m * CH:(m + 1) * CH], a, r, start=(n == 0), stop=(n == len(terms) - 1))
                    last.then_inc(s1_ok, 1)

            def down(i, c):
                e2, j = divmod(c, CPE)
                w = e2 % 2
                if j == 0:
                    pe.wait_ge(wl_ok, i * 8 + (4 * e2 + 4))
                pe.wait_ge(hl_ok, i * (TURN * FP) + (c + 1) * FP)
                pe.wait_ge(yb_ok, i * TURN + (c - 1 + YB0))
                for t in range(CHT):
                    ts = slice(t * P, (t + 1) * P)
                    terms = [(hx[:, c % 2, f, ts], wx[:, w, 2 + f // 4, (f % 4) * D:(f % 4 + 1) * D])
                             for f in range(FK) for hx, wx in ((hh, wh), (hl, wh), (hh, wl))]
                    for n, (a, r) in enumerate(terms):
                        last = M(PS[:, B_Y + c % 2, t * D:(t + 1) * D], a, r, start=(n == 0), stop=(n == len(terms) - 1))
                last.then_inc(y_ok, 1)

            turn(0, 0, first=True)
            turn(0, 1)
            up(0, 0, first=True)

            def step(i, c, last):
                if not (last and c + 2 >= TURN):
                    turn(*((i, c + 2) if c + 2 < TURN else (i + 1, c + 2 - TURN)))
                if not (last and c + 1 >= TURN):
                    up(*((i, c + 1) if c + 1 < TURN else (i + 1, c + 1 - TURN)))
                down(i, c)

            chunks(pe, step)

        @block.scalar
        def _(act):
            A = nc.scalar.activation

            def split_w(e2, i, q):
                act.wait_ge(wraw[q], i * 32 + 16 * (e2 + 1))
                A(wh[:, e2 % 2, q, :], raw[:, q, :], ACT.Copy).then_inc(wh_ok, 1)

            def rows(i, c):
                act.wait_ge(xT_ok, i * TURN + (c + 1))
                A(xh[:, c % 2, :, :].rearrange("p k c -> p (k c)"), PS[:, B_XT, :], ACT.Copy).then_inc(xh_ok, 1)

            def hidden(i, c):
                for pair in range(FP):
                    act.wait_ge(u_ok, i * (TURN * FP) + (c * FP + pair + 1))
                    A(hh[:, c % 2, 2 * pair:2 * pair + 2, :], u[:, pair, :, :], ACT.Relu).then_inc(hh_ok, 1)

            rows(0, 0)
            rows(0, 1)
            for q in range(4):
                split_w(0, 0, q)
            hidden(0, 0)

            def step(i, c, last):
                e2, j = divmod(c, CPE)
                if not (last and c + 2 >= TURN):
                    act.wait_ge(s1_ok, i * (TURN * FP) + (c + 1) * FP)
                    rows(*((i, c + 2) if c + 2 < TURN else (i + 1, c + 2 - TURN)))
                act.wait_ge(y_ok, i * TURN + (c + Y0))
                if not (last and c + 1 >= TURN):
                    hidden(*((i, c + 1) if c + 1 < TURN else (i + 1, c + 1 - TURN)))
                if j >= 1 and not (last and e2 == 1):
                    split_w(*((1, i) if e2 == 0 else (0, i + 1)), j - 1)

            chunks(act, step)

        @block.vector
        def _(dve):
            V = nc.vector
            dve.sem_inc(yb_ok, YB0)
            dve.sem_inc(ysb_free, YF0)

            def split_w(e2, i, q):
                dve.wait_ge(wh_ok, i * 8 + (4 * e2 + q + 1))
                V.tensor_tensor(wl[:, e2 % 2, q, :], raw[:, q, :], wh[:, e2 % 2, q, :].bitcast(FP32), ALU.subtract).then_inc(wl_ok, 1)

            def rows(i, c):
                dve.wait_ge(xh_ok, i * TURN + (c + 1))
                V.tensor_tensor(xl[:, c % 2, :, :].rearrange("p k c -> p (k c)"), PS[:, B_XT, :],
                                xh[:, c % 2, :, :].rearrange("p k c -> p (k c)").bitcast(FP32), ALU.subtract).then_inc(xl_ok, 1)

            def hidden(i, c):
                e2 = c // CPE

                def bias(pair):
                    dve.wait_ge(s1_ok, i * (TURN * FP) + (c * FP + pair + 1))
                    b1 = C["b1"][:, bass.ds(i * (2 * FK) + (e2 * FK + 2 * pair), 2)]
                    V.tensor_tensor(u[:, pair, :, :], PS[:, B_S1 + pair, :].rearrange("p (m c) -> p m c", m=2),
                                    b1.unsqueeze(2).to_broadcast([P, 2, CH]), ALU.add).then_inc(u_ok, 1)

                def low(pair):
                    dve.wait_ge(hh_ok, i * (TURN * FP) + (c * FP + pair + 1))
                    V.scalar_tensor_tensor(hl[:, c % 2, 2 * pair:2 * pair + 2, :], u[:, pair, :, :], 0.0,
                                           hh[:, c % 2, 2 * pair:2 * pair + 2, :].bitcast(FP32), ALU.max, ALU.subtract).then_inc(hl_ok, 1)

                bias(0)
                for pair in range(1, FP):
                    bias(pair)
                    low(pair - 1)
                low(FP - 1)

            def out(i, c):
                e2 = c // CPE
                dve.wait_ge(y_ok, i * TURN + (c + 1 + Y0))
                dve.wait_ge(ysb_free, i * TURN + (c - 1 + YF0))
                b2 = b2_all[:, bass.ds(i * 2 + e2, 1), :].rearrange("p o d -> p (o d)")
                V.tensor_tensor(ysb[:, c % 2, :, :], PS[:, B_Y + c % 2, :].rearrange("p (t d) -> p t d", t=CHT),
                                b2.unsqueeze(1).to_broadcast([P, CHT, D]), ALU.add).then_inc(yb_ok, 1)

            rows(0, 0)
            rows(0, 1)
            for q in range(4):
                split_w(0, 0, q)
            hidden(0, 0)
            dve.wait_ge(b2_in, 16)

            def step(i, c, last):
                e2, j = divmod(c, CPE)
                if not (last and c + 2 >= TURN):
                    dve.wait_ge(s1_ok, i * (TURN * FP) + (c + 1) * FP)
                    rows(*((i, c + 2) if c + 2 < TURN else (i + 1, c + 2 - TURN)))
                dve.wait_ge(y_ok, i * TURN + (c + Y0))
                if not (last and c + 1 >= TURN):
                    hidden(*((i, c + 1) if c + 1 < TURN else (i + 1, c + 1 - TURN)))
                out(i, c)
                if j >= 1 and not (last and e2 == 1):
                    split_w(*((1, i) if e2 == 0 else (0, i + 1)), j - 1)

            chunks(dve, step)


def combine(nc, tag, C, X, R, yrows, out_dram):
    ctx = ExitStack()
    with ctx:
        sem, sb = sem_maker(nc, C, tag), buf_maker(nc, ctx, tag)
        NB = 8
        got = sb("got", [P, NB, TOPK, D])
        ix = sb("ix", [P, NB, TOPK], U32)
        cleared, ix_ok, added, done, turned = sem("cleared"), sem("ix_ok"), sem("added"), sem("done"), sem("turned")
        landed = [[sem(f"landed{b}_{c}", own=True) for c in range(TOPK)] for b in range(NB)]
        block = ctx.enter_context(nc.Block())

        @block.gpsimd
        def _(gp):
            G = nc.gpsimd
            G.memset(got[:, :, :, :], 0.0).then_inc(cleared, 1)
            gp.wait_ge(cleared, 1)
            bound = gp.to_reg(ROWS - 1)
            with gp.Fori(0, TT // NB, 1) as i:
                for b in range(NB):
                    gp.wait_ge(added, i * NB + (b + 1))
                    G.tensor_copy(ix[:, b, :], R["idx"][:, :, bass.ds(i * NB + b, 1)].rearrange("p c o -> p (c o)")).then_inc(ix_ok, 1)
                    gp.wait_ge(ix_ok, i * NB + (b + 1))
                    gp.sem_inc(turned, 1)
                    for c in range(TOPK):
                        G.indirect_dma_start(out=got[:, b, c, :], out_offset=None, in_=yrows,
                                             in_offset=bass.IndirectOffsetOnAxis(ap=ix[:, b, c:c + 1], axis=0),
                                             bounds_check=bound, oob_is_err=False).then_inc(landed[b][c], 16)

        @block.vector
        def _(dve):
            V = nc.vector
            dve.sem_inc(added, NB)
            with dve.Fori(0, TT // NB, 1) as i:
                for b in range(NB):
                    x = X[:, bass.ds(i * NB + b, 1), :].rearrange("p o d -> p (o d)")
                    for c in range(TOPK):
                        dve.wait_ge(landed[b][c], i * 16 + 16)
                        w = R["w"][:, c, bass.ds(i * NB + b, 1)]
                        last = V.scalar_tensor_tensor(x, got[:, b, c, :], w, x, ALU.mult, ALU.add)
                        if c == 0:
                            last.then_inc(done, 1)
                            dve.wait_ge(done, i * NB + (b + 1))
                    last.then_inc(added, 1)

        if out_dram is not None:
            @block.sync
            def _(sp):
                stored = sem("stored")
                Q = TT // 4
                for q in range(4):
                    sp.wait_ge(added, NB + (q + 1) * Q)
                    sp.dma_start(out_dram[q * Q * P:(q + 1) * Q * P, :].rearrange("(t p) d -> p t d", p=P),
                                 X[:, q * Q:(q + 1) * Q, :]).then_inc(stored, 16)
                sp.wait_ge(stored, 64)


def mamba(nc, X, C, PS, mamba_w, mamba_c, bc_dram):
    ctx = ExitStack()
    with ctx:
        sem, sb = sem_maker(nc, C, "m"), buf_maker(nc, ctx, "m")
        MW = sb("MW", [P, W_ALL])
        mc = sb("mc", [P, EK, C_ALL])
        A = sb("A", [P, EK, DS])
        taps = sb("taps", [P, EK, DC, P])
        skip = sb("skip", [P, EK, P])
        mask = sb("mask", [P, MCH + 1], U32)
        st = sb("st", [P, TT, 6])
        tk = sb("tk", [P, 5, TT])
        mean, rstd, rrms, var, mhalf = (tk[:, n, :] for n in range(5))
        XI = sb("XI", [P, EK, DC - 1 + CT])
        U = sb("U", [P, EK, CT])
        T3 = sb("T3", [P, EK, CT])
        xrT = sb("xrT", [P, DK, CT])
        hT = sb("hT", [P, DK, CT])
        XR = sb("XR", [P, CTT, D])
        XP = sb("XP", [P, CTT, D])
        ssq = sb("ssq", [P, CTT])
        SZ = sb("SZ", [P, 2, EK, CT])
        DT = sb("DT", [P, 2, EK, CT])
        DTU = sb("DTU", [P, 2, EK, CT])
        dA = sb("dA", [P, EK, CT])
        dB = sb("dB", [P, EK, CT])
        H = sb("H", [P, EK, CT])
        G = sb("G", [P, EK, CT])
        ST = sb("ST", [P, DS, EK])
        NBC = 2
        BC = sb("BC", [P, NBC, 2, CT])
        sp1 = sb("sp1", [P, 2, CT])
        XD = sb("XD", [P, CT])

        w_in, c_in, dch, a_raw, a_ok, diag_ok = (sem(n) for n in ("w_in", "c_in", "dch", "a_raw", "a_ok", "diag_ok"))
        var_ok, rstd_ok, ms_ok, rrms_ok = (sem(n) for n in ("var_ok", "rstd_ok", "ms_ok", "rrms_ok"))
        f_w, f_r = sem("f_w"), sem("f_r")
        k_w, k_r = sem("k_w"), sem("k_r")
        xr_ok, tail_ok, u_ok, sz_ok = sem("xr_ok"), sem("tail_ok"), sem("u_ok"), sem("sz_ok")
        sp_abs, sp_exp, sp_ln, dt_ok, dtu_ok = (sem(n) for n in ("sp_abs", "sp_exp", "sp_ln", "dt_ok", "dtu_ok"))
        bc_out = sem("bc_out")
        bc_in = [sem(f"bc_in{b}") for b in range(NBC)]
        dA_ok, dB_ok, scanned, g_ok, g_read, kept = (sem(n) for n in ("dA_ok", "dB_ok", "scanned", "g_ok", "g_read", "kept"))
        yz_ok, xn_ok, sq_ok, v_ok, rs_ok, hr_ok, q_ok, xa_ok = (sem(n) for n in (
            "yz_ok", "xn_ok", "sq_ok", "v_ok", "rs_ok", "hr_ok", "q_ok", "xa_ok"))
        block = ctx.enter_context(nc.Block())

        B_F, B_K, B_Y = 0, 2, 4
        F_USE = {use: n for n, use in enumerate(
            [("T", 0), ("T", 1), ("x", 0), ("x", 1), ("x", 2), ("x", 3), ("z", 0), ("z", 1), ("conv", 0), ("conv", 1),
             ("conv", 2), ("conv", 3), ("z", 2), ("z", 3), ("xp", 0), ("dt", 0), ("dt", 1), ("dt", 2), ("dt", 3)])}
        K_USE = {use: n for n, use in enumerate(
            [("out", 0), ("out", 1), ("T", 0), ("T", 1), ("fc", 0), ("fc", 1), ("fc", 2), ("fc", 3), ("pj", 0), ("pj", 1)])}
        NF, NK = len(F_USE), len(K_USE)
        KR0 = 2
        ITEMS = {
            0: ["F_xr", "F_T"], 1: ["F_x01"], 2: ["F_x23"], 3: ["K_out"], 4: ["F_z01", "K_sq"], 5: ["F_c0", "K_v"],
            6: ["F_c1", "K_hr"], 7: ["K_T", "F_c2"], 8: ["F_c3"], 9: ["F_z23", "F_silu"], 10: ["K_fc01"], 11: ["K_fc23"],
            12: ["F_xp"], 13: ["F_dt"], 14: ["K_pj"],
        }
        FRONT = [p for s in sorted(ITEMS) for p in ITEMS[s] if p[0] == "F"]
        BACK = [p for s in sorted(ITEMS) for p in ITEMS[s] if p[0] == "K"]

        def run(eng, turn, front, back):
            for p in FRONT:
                front(p, 0, 0)
            turn(0, 0, True, False)
            with eng.Fori(0, MCH // 2 - 1, 1) as i:
                turn(i * 2 + 1, 1, True, True)
                turn(i * 2 + 2, 0, True, True)
            turn(MCH - 1, 1, False, True)
            for p in ["K_yz"] + BACK:
                back(p, MCH - 1, 1)

        def items(s, k, par, has_front, has_back, front, back):
            for p in ITEMS.get(s, []):
                if p[0] == "F" and has_front:
                    front(p, k + 1, 1 - par)
                if p[0] == "K" and has_back:
                    back(p, k - 1, 1 - par)

        def is_first(k):
            return isinstance(k, int) and k == 0

        def f_bank(use, rows=P):
            return PS[0:rows, B_F + F_USE[use] % 2, :]

        def k_bank(use):
            return PS[:, B_K + K_USE[use] % 2, :]

        def weights(at, width, tile, lo, n):
            return MW[:, at + tile * width + lo:at + tile * width + lo + n]

        @block.sync
        def _(sp):
            sp.dma_start(mc[:, :, :], mamba_c).then_inc(c_in, 16)
            sp.dma_start(MW[:, :], mamba_w).then_inc(w_in, 16)

            def load(k, s):
                src = bc_dram[bass.ds(k, 1), :, s:s + 1, :].rearrange("o j q t -> (o q) j t")
                sp.dma_start(BC[:, s % NBC, :, :], src.to_broadcast([P, 2, CT])).then_inc(bc_in[s % NBC], 16)

            def front(p, k, par):
                if p == "F_xp":
                    sp.wait_ge(f_r, k * NF + (F_USE["xp", 0] + 1))
                    sp.dma_start(bc_dram[bass.ds(k, 1), :, :, :].rearrange("o j s t -> (o j s) t"),
                                 XD[DR:XPR, :]).then_inc(bc_out, 16)

            def back(p, k, par):
                pass

            def turn(k, par, has_front, has_back):
                sp.wait_ge(bc_out, k * 16 + 16)
                for s in range(DS):
                    if s >= NBC or not is_first(k):
                        sp.wait_ge(g_ok, k * (2 * DS) + 2 * (s - NBC + 1))
                    load(k, s)
                    if s == 14 and has_front:
                        front("F_xp", k + 1, 1 - par)

            run(sp, turn, front, back)

        @block.tensor
        def _(pe):
            M = nc.tensor.matmul
            pe.sem_inc(k_r, KR0)
            pe.wait_ge(w_in, 16)
            pe.wait_ge(diag_ok, 1)

            def front(p, k, par):
                def bank_free(use):
                    if not (is_first(k) and F_USE[use] < 2):
                        pe.wait_ge(f_r, k * NF + (F_USE[use] - 1))

                if p == "F_T":
                    pe.wait_ge(xr_ok, k + 1)
                    for d in range(DK):
                        bank_free(("T", d))
                        for t in range(CTT):
                            last = nc.tensor.transpose(f_bank(("T", d))[:, t * P:(t + 1) * P], XR[:, t, d * P:(d + 1) * P], C["ident"][:, :])
                        last.then_inc(f_w, 1)
                elif p[:3] in ("F_x", "F_z") and p[3:] in ("01", "23"):
                    for n in (int(p[3]), int(p[4])):
                        use = (p[2], n)
                        pe.wait_ge(f_r, k * NF + 2)
                        bank_free(use)
                        for d in range(DK):
                            last = M(f_bank(use), weights(W_IN, 2 * DI, d, (0 if p[2] == "x" else DI) + n * P, P), xrT[:, d, :],
                                     start=(d == 0), stop=(d == DK - 1))
                        last.then_inc(f_w, 1)
                elif p[:3] == "F_c":
                    use = ("conv", int(p[3]))
                    pe.wait_ge(f_r, k * NF + (F_USE["x", 3] + 1))
                    bank_free(use)
                    for tap in range(DC):
                        last = M(f_bank(use), taps[:, use[1], tap, :], XI[:, use[1], tap:tap + CT], start=(tap == 0), stop=(tap == DC - 1))
                    last.then_inc(f_w, 1)
                elif p == "F_xp":
                    use = ("xp", 0)
                    pe.wait_ge(u_ok, k + 1)
                    bank_free(use)
                    for e in range(EK):
                        last = M(f_bank(use, XPR), weights(W_XP, XPR, e, 0, XPR), U[:, e, :], start=(e == 0), stop=(e == EK - 1))
                    last.then_inc(f_w, 1)
                elif p == "F_dt":
                    pe.wait_ge(f_r, k * NF + (F_USE["xp", 0] + 1))
                    for n in range(EK):
                        bank_free(("dt", n))
                        M(f_bank(("dt", n)), MW[0:DR, W_DT + n * P:W_DT + (n + 1) * P], XD[0:DR, :], start=True, stop=True).then_inc(f_w, 1)

            def back(p, k, par):
                def bank_free(use):
                    pe.wait_ge(k_r, k * NK + (K_USE[use] - 1 + KR0))

                if p in ("K_out", "K_pj"):
                    kind, at = ("out", W_OUT) if p == "K_out" else ("pj", W_PJ)
                    pe.wait_ge(*((yz_ok, k * 2 + 2) if p == "K_out" else (q_ok, k * 2 + 2)))
                    for a in range(2):
                        bank_free((kind, a))
                        for t in (2 * a, 2 * a + 1):
                            for e in range(EK):
                                last = M(k_bank((kind, a))[:, (t % 2) * D:(t % 2 + 1) * D], T3[:, e, t * P:(t + 1) * P],
                                         weights(at, D, e, 0, D), start=(e == 0), stop=(e == EK - 1))
                        last.then_inc(k_w, 1)
                elif p == "K_T":
                    pe.wait_ge(hr_ok, k + 1)
                    for d in range(DK):
                        bank_free(("T", d))
                        for t in range(CTT):
                            last = nc.tensor.transpose(k_bank(("T", d))[:, t * P:(t + 1) * P], XR[:, t, d * P:(d + 1) * P], C["ident"][:, :])
                        last.then_inc(k_w, 1)
                elif p[:4] == "K_fc":
                    pe.wait_ge(k_r, k * NK + (K_USE["T", 1] + 1 + KR0))
                    for n in (int(p[4]), int(p[5])):
                        bank_free(("fc", n))
                        for d in range(DK):
                            last = M(k_bank(("fc", n)), weights(W_FC, 2 * D, d, n * P, P), hT[:, d, :], start=(d == 0), stop=(d == DK - 1))
                        last.then_inc(k_w, 1)

            def turn(k, par, has_front, has_back):
                pe.wait_ge(u_ok, k + 1)
                for e in range(EK):
                    if has_back:
                        pe.wait_ge(yz_ok, k * 2 + (e // 2 - 1))
                    M(PS[:, B_Y + e, :], skip[:, e, :], U[:, e, :], start=True, stop=False)
                for s in range(DS):
                    items(s, k, par, has_front, has_back, front, back)
                    for pair in range(2):
                        pe.wait_ge(g_ok, k * (2 * DS) + (2 * s + pair + 1))
                        for e in (2 * pair, 2 * pair + 1):
                            last = M(PS[:, B_Y + e, :], C["ident"][:, :], G[:, e, :], start=False, stop=(s == DS - 1))
                        last.then_inc(g_read, 1)

            run(pe, turn, front, back)

        @block.scalar
        def _(act):
            def F(out, in_, func, **kw):
                return nc.scalar.activation(out, in_, func, **kw)

            def exp_set():
                act.preload_act_table_set("natural_log_exp_and_others")

            act.wait_ge(c_in, 16)
            exp_set()
            F(A[:, :, :], mc[:, :, C_AL:C_AL + DS], ACT.Exp).then_inc(a_raw, 1)
            act.wait_ge(a_ok, 1)

            def evac(use, k, out, **kw):
                act.wait_ge(f_w, k * NF + (F_USE[use] + 1))
                F(out, f_bank(use), kw.pop("func", ACT.Copy), **kw).then_inc(f_r, 1)

            def front(p, k, par):
                if p == "F_T":
                    for d in range(DK):
                        evac(("T", d), k, xrT[:, d, :])
                elif p in ("F_x01", "F_x23"):
                    act.wait_ge(tail_ok, k + 1)
                    for n in (int(p[3]), int(p[4])):
                        evac(("x", n), k, XI[:, n, DC - 1:])
                elif p in ("F_z01", "F_z23"):
                    if not (isinstance(k, int) and k < 2):
                        act.wait_ge(yz_ok, k * 2 - 2)
                    for n in (int(p[3]), int(p[4])):
                        evac(("z", n), k, SZ[:, par, n, :])
                elif p[:3] == "F_c":
                    if not is_first(k):
                        act.wait_ge(dtu_ok, k * 2)
                    n = int(p[3])
                    evac(("conv", n), k, U[:, n, :], func=ACT.Identity, bias=mc[:, n, C_CB:C_CB + 1])
                elif p == "F_silu":
                    act.wait_ge(f_r, k * NF + (F_USE["z", 3] + 1))
                    F(U[:, :, :], U[:, :, :], ACT.Silu).then_inc(u_ok, 1)
                    F(SZ[:, par, :, :], SZ[:, par, :, :], ACT.Silu).then_inc(sz_ok, 1)
                    exp_set()
                elif p == "F_xp":
                    if not is_first(k):
                        act.wait_ge(bc_out, k * 16)
                    act.wait_ge(f_w, k * NF + (F_USE["xp", 0] + 1))
                    F(XD[0:XPR, :], f_bank(("xp", 0), XPR), ACT.Copy).then_inc(f_r, 1)
                elif p == "F_dt":
                    for pair in range(2):
                        if not (is_first(k) and pair == 0):
                            act.wait_ge(dt_ok, k * 2 + pair)
                        for n in (2 * pair, 2 * pair + 1):
                            act.wait_ge(f_w, k * NF + (F_USE["dt", n] + 1))
                            bias = mc[:, n, C_DB:C_DB + 1]
                            F(DT[:, par, n, :], f_bank(("dt", n)), ACT.Relu, bias=bias)
                            F(sp1[:, n % 2, :], f_bank(("dt", n)), ACT.Abs, bias=bias).then_inc(f_r, 1)
                        act.wait_ge(f_r, k * NF + (F_USE["dt", 2 * pair + 1] + 1))
                        F(sp1[:, :, :], sp1[:, :, :], ACT.Exp, scale=-1.0).then_inc(sp_exp, 1)
                        act.wait_ge(sp_exp, k * 2 + (pair + 1))
                        F(sp1[:, :, :], sp1[:, :, :], ACT.Ln, bias=1.0).then_inc(sp_ln, 1)

            def back(p, k, par):
                if p == "K_sq":
                    act.wait_ge(k_r, k * NK + 2 + KR0)
                    for t in range(CTT):
                        last = F(XR[:, t, :], XP[:, t, :], ACT.Square, accum_out=ssq[:, t:t + 1])
                    last.then_inc(sq_ok, 1)
                elif p == "K_T":
                    for d in range(DK):
                        act.wait_ge(k_w, k * NK + (K_USE["T", d] + 1))
                        F(hT[:, d, :], k_bank(("T", d)), ACT.Copy).then_inc(k_r, 1)
                elif p[:4] == "K_fc":
                    for n in (int(p[4]), int(p[5])):
                        act.wait_ge(k_w, k * NK + (K_USE["fc", n] + 1))
                        F(T3[:, n, :], k_bank(("fc", n)), ACT.Copy).then_inc(k_r, 1)

            def decay(k, par, s):
                if s == 0:
                    act.wait_ge(dt_ok, k * 2 + 2)
                for e in range(EK):
                    if not (is_first(k) and s == 0):
                        act.wait_ge(scanned, k * (DS * EK) + ((s - 1) * EK + e + 1))
                    F(dA[:, e, :], DT[:, par, e, :], ACT.Exp, scale=A[:, e, s:s + 1]).then_inc(dA_ok, 1)

            def turn(k, par, has_front, has_back):
                decay(k, par, 0)
                for s in range(DS):
                    if s + 1 < DS:
                        decay(k, par, s + 1)
                    items(s, k, par, has_front, has_back, front, back)

            run(act, turn, front, back)

        @block.gpsimd
        def _(gp):
            G_ = nc.gpsimd
            gp.wait_ge(var_ok, 1)
            G_.tensor_tensor(rstd, rstd, mhalf, ALU.pow).then_inc(rstd_ok, 1)
            gp.wait_ge(ms_ok, 1)
            G_.tensor_tensor(rrms, rrms, mhalf, ALU.pow).then_inc(rrms_ok, 1)

            def front(p, k, par):
                pass

            def back(p, k, par):
                if p == "K_v":
                    gp.wait_ge(v_ok, k + 1)
                    G_.tensor_tensor(ssq[:, :], ssq[:, :], mhalf[:, 0:CTT], ALU.pow).then_inc(rs_ok, 1)

            def turn(k, par, has_front, has_back):
                gp.wait_ge(dtu_ok, k * 2 + 2)
                for s in range(DS):
                    gp.wait_ge(bc_in[s % NBC], k * (16 * DS // NBC) + 16 * (s // NBC + 1))
                    for pair in range(2):
                        if not (is_first(k) and s == 0):
                            gp.wait_ge(scanned, k * (DS * EK) + ((s - 1) * EK + 2 * pair + 2))
                        es = slice(2 * pair, 2 * pair + 2)
                        G_.tensor_tensor(dB[:, es, :], DTU[:, par, es, :], BC[:, s % NBC, 0:1, :].to_broadcast([P, 2, CT]),
                                         ALU.mult).then_inc(dB_ok, 1)
                    items(s, k, par, has_front, has_back, front, back)

            run(gp, turn, front, back)

        @block.vector
        def _(dve):
            V = nc.vector
            link = chain(dve, dch)
            V.memset(mhalf, -0.5)
            link(V.memset(mask[:, :].bitcast(mybir.dt.int32), -1))
            V.memset(ST[:, :, :], 0.0)
            V.memset(XI[:, :, 0:DC - 1], 0.0).then_inc(tail_ok, 1)
            with dve.Fori(0, TT, 1) as t:
                V.bn_stats(st[:, bass.ds(t, 1), :].rearrange("p o s -> p (o s)"),
                           X[:, bass.ds(t, 1), :].rearrange("p o d -> p (o d)"))
            for k in range(0, MCH, MCH // BATCH):
                link(V.memset(mask[:, k:k + 1].bitcast(mybir.dt.int32), 0))
            dve.wait_ge(c_in, 16)
            for e in range(EK):
                for tap in range(DC):
                    V.tensor_scalar(taps[:, e, tap, :], C["ident"][:, :], mc[:, e, C_CW + tap:C_CW + tap + 1], None, ALU.mult)
                last = V.tensor_scalar(skip[:, e, :], C["ident"][:, :], mc[:, e, C_D:C_D + 1], None, ALU.mult)
            last.then_inc(diag_ok, 1)
            link(V.tensor_tensor(mean, st[:, :, 1], st[:, :, 4], ALU.add))
            V.tensor_tensor(var, st[:, :, 1], st[:, :, 4], ALU.subtract)
            link(V.tensor_tensor(rstd, st[:, :, 2], st[:, :, 5], ALU.add))
            link(V.tensor_scalar(mean, mean, 0.5, None, ALU.mult))
            link(V.tensor_tensor(var, var, var, ALU.mult))
            link(V.tensor_scalar(var, var, 0.25, None, ALU.mult))
            link(V.scalar_tensor_tensor(var, rstd, 1.0 / D, var, ALU.mult, ALU.add))
            V.tensor_scalar(rstd, var, LN_EPS, None, ALU.add).then_inc(var_ok, 1)
            dve.wait_ge(a_raw, 1)
            V.tensor_scalar(A[:, :, :], A[:, :, :], -1.0, None, ALU.mult).then_inc(a_ok, 1)
            dve.wait_ge(rstd_ok, 1)
            link(V.tensor_tensor(rrms, rstd, rstd, ALU.mult))
            link(V.tensor_tensor(rrms, rrms, var, ALU.mult))
            V.tensor_scalar(rrms, rrms, RMS_EPS, None, ALU.add).then_inc(ms_ok, 1)
            dve.wait_ge(rrms_ok, 1)
            link(V.tensor_tensor(rrms, rrms, rstd, ALU.mult))

            def tile(k, t, n=1):
                x = X[:, bass.ds(k * CTT + t, n), :]
                return x.rearrange("p o d -> p (o d)") if n == 1 else x

            def col(a, k, t):
                return a[:, bass.ds(k * CTT + t, 1)]

            def front(p, k, par):
                if p == "F_xr":
                    for t in range(CTT):
                        last = V.tensor_scalar(XR[:, t, :], tile(k, t), col(mean, k, t), col(rrms, k, t), ALU.subtract, ALU.mult)
                    last.then_inc(xr_ok, 1)
                    if not is_first(k):
                        dve.wait_ge(f_r, k * NF)
                        V.tensor_tensor(XI[:, :, 0:DC - 1].bitcast(U32), XI[:, :, CT:].bitcast(U32),
                                        mask[:, bass.ds(k, 1)].unsqueeze(2).to_broadcast([P, EK, DC - 1]),
                                        ALU.bitwise_and).then_inc(tail_ok, 1)
                elif p == "F_dt":
                    for pair in range(2):
                        es = slice(2 * pair, 2 * pair + 2)
                        dve.wait_ge(sp_ln, k * 2 + (pair + 1))
                        V.tensor_tensor(DT[:, par, es, :], DT[:, par, es, :], sp1[:, :, :], ALU.add).then_inc(dt_ok, 1)
                        dve.wait_ge(dt_ok, k * 2 + (pair + 1))
                        V.tensor_tensor(DTU[:, par, es, :], DT[:, par, es, :], U[:, es, :], ALU.mult).then_inc(dtu_ok, 1)

            def back(p, k, par):
                if p == "K_yz":
                    dve.wait_ge(sz_ok, k + 1)
                    for pair in range(2):
                        es = slice(2 * pair, 2 * pair + 2)
                        dve.wait_ge(g_read, k * (2 * DS) + (2 * DS - 1 + pair))
                        V.tensor_tensor(T3[:, es, :], PS[:, B_Y + 2 * pair:B_Y + 2 * pair + 2, :], SZ[:, par, es, :], ALU.mult).then_inc(yz_ok, 1)
                elif p == "K_out":
                    for t in range(CTT):
                        last = V.tensor_scalar(XP[:, t, :], tile(k, t), col(mean, k, t), col(rstd, k, t), ALU.subtract, ALU.mult)
                    last.then_inc(xn_ok, 1)
                    dve.wait_ge(xn_ok, k + 1)
                    for a in range(2):
                        dve.wait_ge(k_w, k * NK + (K_USE["out", a] + 1))
                        xp = XP[:, 2 * a:2 * a + 2, :]
                        V.tensor_tensor(xp, xp, k_bank(("out", a)).rearrange("p (t d) -> p t d", t=2), ALU.add).then_inc(k_r, 1)
                elif p == "K_v":
                    dve.wait_ge(sq_ok, k + 1)
                    V.tensor_scalar(ssq[:, :], ssq[:, :], 1.0 / D, RMS_EPS, ALU.mult, ALU.add).then_inc(v_ok, 1)
                elif p == "K_hr":
                    dve.wait_ge(rs_ok, k + 1)
                    for t in range(CTT):
                        last = V.tensor_scalar(XR[:, t, :], XP[:, t, :], ssq[:, t:t + 1], None, ALU.mult)
                    last.then_inc(hr_ok, 1)
                elif p[:4] == "K_fc":
                    pair = int(p[4]) // 2
                    es = slice(2 * pair, 2 * pair + 2)
                    dve.wait_ge(k_r, k * NK + (K_USE["fc", 2 * pair + 1] + 1 + KR0))
                    V.scalar_tensor_tensor(T3[:, es, :], T3[:, es, :], 0.0, T3[:, es, :], ALU.max, ALU.mult).then_inc(q_ok, 1)
                elif p == "K_pj":
                    V.tensor_tensor(tile(k, 0, CTT), tile(k, 0, CTT), XP[:, :, :], ALU.add).then_inc(xa_ok, 1)
                    dve.wait_ge(xa_ok, k + 1)
                    for a in range(2):
                        dve.wait_ge(k_w, k * NK + (K_USE["pj", a] + 1))
                        V.tensor_tensor(tile(k, 2 * a, 2), tile(k, 2 * a, 2),
                                        k_bank(("pj", a)).rearrange("p (t d) -> p t d", t=2), ALU.add).then_inc(k_r, 1)

            def turn(k, par, has_front, has_back):
                if has_back:
                    back("K_yz", k - 1, 1 - par)
                if has_front:
                    front("F_xr", k + 1, 1 - par)
                for s in range(DS):
                    if s > 0 or not is_first(k):
                        dve.wait_ge(kept, k * DS + s)
                    for e in range(EK):
                        dve.wait_ge(dA_ok, k * (DS * EK) + (s * EK + e + 1))
                        if e % 2 == 0:
                            dve.wait_ge(dB_ok, k * (2 * DS) + (2 * s + e // 2 + 1))
                        V.tensor_tensor_scan(H[:, e, :], dA[:, e, :], dB[:, e, :], ST[:, s, e:e + 1], ALU.mult, ALU.add).then_inc(scanned, 1)
                    for pair in range(2):
                        es = slice(2 * pair, 2 * pair + 2)
                        dve.wait_ge(scanned, k * (DS * EK) + (s * EK + 2 * pair + 2))
                        if not (is_first(k) and s == 0):
                            dve.wait_ge(g_read, k * (2 * DS) + (2 * s - 1 + pair))
                        V.tensor_tensor(G[:, es, :], H[:, es, :], BC[:, s % NBC, 1:2, :].to_broadcast([P, 2, CT]), ALU.mult).then_inc(g_ok, 1)
                    V.tensor_tensor(ST[:, s, :].bitcast(U32), H[:, :, CT - 1].bitcast(U32),
                                    mask[:, bass.ds(k + 1, 1)].to_broadcast([P, EK]), ALU.bitwise_and).then_inc(kept, 1)
                    items(s, k, par, has_front and s > 0, has_back, front, back)

            run(dve, turn, front, back)


def build(nc, x, gate, gate_b, b1, b2, w1, w2, mamba_w, mamba_c, out):
    ctx = ExitStack()
    with ctx:
        keep = buf_maker(nc, ctx, "keep")
        X = keep("X", [P, TT, D])
        C = {
            "whole": ctx, "sems": {},
            "ident": keep("ident", [P, P]), "upper": keep("upper", [P, P], BF16), "onesb": keep("onesb", [P, P], BF16),
            "gate": keep("gate", [P, DK, EXPERTS]), "gb": keep("gb", [P, EXPERTS]), "rank": keep("rank", [P, EXPERTS]),
            "region": keep("region", [P, EXPERTS]), "b1": keep("b1", [P, EXPERTS * FK]),
        }
        R = {"w": keep("w", [P, TOPK, TT]), "idx": keep("idx", [P, TOPK, TT], U32)}
        PS = ctx.enter_context(nc.psum_tensor("PS", [P, 8, 512], FP32))
        xrows = nc.dram_tensor("xrows", (ROWS, D), FP32, kind="Internal").ap()
        yrows = nc.dram_tensor("yrows", (ROWS, D), FP32, kind="Internal").ap()
        setup(nc, C, gate, gate_b, b1)
        route(nc, "r0", X, C, PS, R, xrows, x, True)
        experts(nc, "e0", C, PS, xrows, yrows, w1, w2, b2)
        combine(nc, "c0", C, X, R, yrows, None)
        bc_dram = nc.dram_tensor("bc_rows", (MCH, 2, DS, CT), FP32, kind="Internal").ap()
        mamba(nc, X, C, PS, mamba_w, mamba_c, bc_dram)
        clear(nc, C, ("r", "e", "c"))
        route(nc, "r1", X, C, PS, R, xrows, None, False)
        experts(nc, "e1", C, PS, xrows, yrows, w1, w2, b2)
        combine(nc, "c1", C, X, R, yrows, out)


def clear(nc, C, tags):
    numbers = sorted(h.num for name, h in C["sems"].items() if name.split("_")[0] in tags)
    with nc.Block() as block:
        @block.gpsimd
        def _(gp):
            start = 0
            for n in range(1, len(numbers) + 1):
                if n == len(numbers) or numbers[n] != numbers[n - 1] + 1:
                    gp.sem_clear(range(numbers[start], numbers[n - 1] + 1))
                    start = n


def setup(nc, C, gate, gate_b, b1):
    ctx = ExitStack()
    with ctx:
        sem = sem_maker(nc, C, "s")
        loaded, made = sem("loaded"), sem("made")
        ints = ctx.enter_context(nc.sbuf_tensor("ints", [P, 2, EXPERTS], mybir.dt.int32))
        block = ctx.enter_context(nc.Block())

        @block.sync
        def _(sp):
            sp.dma_start(C["gate"][:, :, :], gate).then_inc(loaded, 16)
            sp.dma_start(C["gb"][:, :], gate_b.to_broadcast([P, EXPERTS])).then_inc(loaded, 16)
            sp.dma_start(C["b1"][:, :], b1).then_inc(loaded, 16)
            sp.wait_ge(loaded, 48)

        @block.gpsimd
        def _(gp):
            G = nc.gpsimd
            G.memset(C["ident"][:, :], 0.0)
            G.memset(C["upper"][:, :], 1.0)
            G.memset(C["onesb"][:, :], 1.0)
            G.iota(ints[:, 0, :], pattern=[[-1, EXPERTS]], base=EXPERTS, channel_multiplier=0)
            G.iota(ints[:, 1, :], pattern=[[ROWS_E, EXPERTS]], base=0, channel_multiplier=0).then_inc(made, 1)
            gp.wait_ge(made, 1)
            G.affine_select(out=C["ident"][:, :], in_=C["ident"][:, :], compare_op=ALU.not_equal, fill=1.0,
                            base=0, pattern=[[-1, P]], channel_multiplier=1)
            G.affine_select(out=C["upper"][:, :], in_=C["upper"][:, :], compare_op=ALU.is_ge, fill=0.0,
                            base=0, pattern=[[1, P]], channel_multiplier=-1)
            G.tensor_copy(C["rank"][:, :], ints[:, 0, :])
            G.tensor_copy(C["region"][:, :], ints[:, 1, :]).then_inc(made, 1)


def kernel(**inputs):
    import numpy as np
    import concourse.bacc as bacc
    from concourse import mybir as _mybir
    from concourse.bass_utils import run_bass_kernel_spmd as run

    def g(name):
        return np.asarray(inputs[name])

    def tiles(a):
        return np.ascontiguousarray(a.reshape(-1, P, a.shape[1]).transpose(1, 0, 2))

    def block_of(a):
        t = tiles(a)
        return t.reshape(P, -1)

    dt_w = np.zeros((P, DI), np.float32)
    dt_w[:DR] = g("L0_attn_dt_proj_w").T
    arrays = {
        "x": g("L0_attn_x").reshape(TOKENS, D),
        "gate": tiles(g("L0_ffn_gate_w").T),
        "gate_b": g("L0_ffn_gate_b").reshape(1, EXPERTS),
        "b1": g("L0_ffn_b1").reshape(EXPERTS * FK, P).T,
        "b2": g("L0_ffn_b2").reshape(1, EXPERTS * D),
        "w1": g("L0_ffn_W1"),
        "w2": g("L0_ffn_W2"),
        "mamba_w": np.concatenate([
            block_of(g("L0_attn_in_proj_w").T), block_of(g("L0_attn_x_proj_w").T), dt_w,
            block_of(g("L0_attn_out_proj_w").T), block_of(g("L0_attn_c_fc_w").T), block_of(g("L0_attn_c_proj_w").T)], axis=1),
        "mamba_c": tiles(np.concatenate([
            g("L0_attn_conv_w"), g("L0_attn_conv_b")[:, None], g("L0_attn_dt_proj_b")[:, None], g("L0_attn_D")[:, None],
            g("L0_attn_A_log")], axis=1)),
    }
    nc = bacc.Bacc("TRN2", target_bir_lowering=False, num_devices=1)
    feed, args = {}, []
    for name, a in arrays.items():
        feed[name] = np.ascontiguousarray(a)
        args.append(nc.dram_tensor(name, a.shape, _mybir.dt.from_np(a.dtype), kind="ExternalInput").ap())
    args.append(nc.dram_tensor("out", (TOKENS, D), _mybir.dt.float32, kind="ExternalOutput").ap())
    build(nc, *args)
    r = run(nc, [feed], core_ids=[0])
    return r.results[0]["out"].reshape(BATCH, TOKENS // BATCH, D)
```

```python
import concourse.bass as bass
from concourse import mybir
from contextlib import ExitStack

FP32 = mybir.dt.float32
FP32R = mybir.dt.float32r
BF16 = mybir.dt.bfloat16
U32 = mybir.dt.uint32
ALU = mybir.AluOpType
ACT = mybir.ActivationFunctionType
AX = mybir.AxisListType

P = 128
TOKENS, D = 4096, 256
BATCH = 2
TT = TOKENS // P
DK = D // P
EXPERTS, FF, TOPK = 8, 1024, 2
CAP = 640
ROWS_E = TOPK * CAP
ROWS = EXPERTS * ROWS_E
CH = 256
CPE = ROWS_E // CH
CHT = CH // P
NCHUNK = EXPERTS * CPE
FK = FF // P
FP = FK // 2
DROPPED = 20000
LN_EPS = 1e-5
RMS_EPS = 1.1920928955078125e-07

DI, DS, DC, DR = 512, 16, 4, 64
EK = DI // P
CT = 512
CTT = CT // P
MCH = TOKENS // CT
XPR = DR + 2 * DS
W_IN, W_XP = 0, DK * 2 * DI
W_DT = W_XP + EK * XPR
W_OUT = W_DT + DI
W_FC = W_OUT + EK * D
W_PJ = W_FC + DK * 2 * D
W_ALL = W_PJ + EK * D
C_CW, C_CB, C_DB, C_D, C_AL, C_ALL = 0, 4, 5, 6, 7, 7 + DS


def sem_maker(nc, C, tag):
    def get(name, own=False):
        full = f"{tag}_{name}" if own else f"{tag[0]}_{name}"
        if full not in C["sems"]:
            C["sems"][full] = C["whole"].enter_context(nc.semaphore(full))
        return C["sems"][full]

    return get


def buf_maker(nc, ctx, tag):
    return lambda name, shape, dt=FP32: ctx.enter_context(nc.sbuf_tensor(f"{tag}_{name}", shape, dt))


def chain(eng, sem):
    count = [0]

    def link(instruction):
        count[0] += 1
        instruction.then_inc(sem, 1)
        eng.wait_ge(sem, count[0])

    return link


def route(nc, tag, X, C, PS, R, xrows, x_dram, zero_rows):
    ctx = ExitStack()
    with ctx:
        sem, sb = sem_maker(nc, C, tag), buf_maker(nc, ctx, tag)
        st = sb("stats", [P, TT, 6])
        small = sb("small", [P, 6, TT])
        mean, rstd, dif, mhalf = small[:, 0, :], small[:, 1, :], small[:, 2, :], small[:, 3, :]
        xn = sb("xn", [P, 2, 4, D])
        xnT = sb("xnT", [P, 2, DK, 4 * P])
        lg = sb("lg", [P, TT, EXPERTS])
        pr = sb("pr", [P, TT, EXPERTS])
        w1 = sb("w1", [P, TT, EXPERTS])
        w2 = sb("w2", [P, TT, EXPERTS])
        red = sb("red", [P, 4, TT])
        oh = sb("oh", [P, TOPK, TT, EXPERTS])
        ohb = sb("ohb", [P, TOPK, TT, EXPERTS], BF16)
        pos = sb("pos", [P, TOPK, TT, EXPERTS])
        tot = sb("tot", [P, TOPK, TT, EXPERTS])
        inc = sb("inc", [P, TOPK, TT, EXPERTS])
        zcol = sb("zcol", [P, TT])
        base = sb("base", [P, TOPK, EXPERTS])
        kept = sb("kept", [P, TOPK, EXPERTS])
        slot = sb("slot", [P, TOPK, TT])
        xs = sb("xs", [P, 4, D])
        ixs = sb("ixs", [P, 4, TOPK], U32)
        zrow = sb("zrow", [P, 2048])

        x_in = [sem(f"x_in{q}") for q in range(4)]
        zero_set, zeroed = sem("zero_set"), sem("zeroed")
        dch, var_ok, rstd_ok = sem("dch"), sem("var_ok"), sem("rstd_ok")
        xn_ok, tp_ok, xnT_ok, lgp_ok, lg_ok = sem("xn_ok"), sem("tp_ok"), sem("xnT_ok"), sem("lgp_ok"), sem("lg_ok")
        sh_ok, ex_ok, ohb_ok, cum_ok = sem("sh_ok"), sem("ex_ok"), sem("ohb_ok"), sem("cum_ok")
        xs_ok, turned = sem("xs_ok"), sem("turned")
        sent = [[sem(f"sent{b}_{c}", own=True) for c in range(TOPK)] for b in range(4)]
        block = ctx.enter_context(nc.Block())
        Q = TT // 4

        @block.sync
        def _(sp):
            if x_dram is not None:
                for q in range(4):
                    sp.dma_start(X[:, q * Q:(q + 1) * Q, :],
                                 x_dram[q * Q * P:(q + 1) * Q * P, :].rearrange("(t p) d -> p t d", p=P)).then_inc(x_in[q], 16)
            if zero_rows:
                sp.wait_ge(zero_set, 1)
                rows = 8 * P
                for r in range(ROWS // rows):
                    sp.dma_start(xrows[r * rows:(r + 1) * rows, :].rearrange("(p a) d -> p (a d)", p=P),
                                 zrow[:, :]).then_inc(zeroed, 16)

        @block.vector
        def _(dve):
            V = nc.vector
            link = chain(dve, dch)
            V.memset(zrow[:, :], 0.0).then_inc(zero_set, 1)
            V.memset(mhalf, -0.5)
            V.memset(zcol[:, :], 1.0)
            for q in range(4):
                if x_dram is not None:
                    dve.wait_ge(x_in[q], 16)
                with dve.Fori(q * Q, (q + 1) * Q, 1) as t:
                    V.bn_stats(st[:, bass.ds(t, 1), :].rearrange("p o s -> p (o s)"),
                               X[:, bass.ds(t, 1), :].rearrange("p o d -> p (o d)"))
            link(V.memset(red[:, 0, :], 0.0))
            link(V.tensor_tensor(mean, st[:, :, 1], st[:, :, 4], ALU.add))
            V.tensor_tensor(dif, st[:, :, 1], st[:, :, 4], ALU.subtract)
            link(V.tensor_tensor(rstd, st[:, :, 2], st[:, :, 5], ALU.add))
            link(V.tensor_scalar(mean, mean, 0.5, None, ALU.mult))
            link(V.tensor_tensor(dif, dif, dif, ALU.mult))
            link(V.tensor_scalar(dif, dif, 0.25, LN_EPS, ALU.mult, ALU.add))
            V.scalar_tensor_tensor(rstd, rstd, 1.0 / D, dif, ALU.mult, ALU.add).then_inc(var_ok, 1)
            dve.wait_ge(rstd_ok, 1)

            def normed(out, t):
                return V.tensor_scalar(out, X[:, bass.ds(t, 1), :].rearrange("p o d -> p (o d)"),
                                       mean[:, bass.ds(t, 1)], rstd[:, bass.ds(t, 1)], ALU.subtract, ALU.mult)

            with dve.Fori(0, TT // 8, 1) as i:
                for g in range(2):
                    for a in range(4):
                        last = normed(xn[:, g, a, :], i * 8 + (g * 4 + a))
                    last.then_inc(xn_ok, 1)
                for g in range(2):
                    dve.wait_ge(lgp_ok, i * 2 + (g + 1))
                    V.tensor_tensor(lg[:, bass.ds(i * 8 + g * 4, 4), :],
                                    PS[:, 4 + g, 0:4 * EXPERTS].rearrange("p (t e) -> p t e", e=EXPERTS),
                                    C["gb"][:, :].unsqueeze(1).to_broadcast([P, 4, EXPERTS]), ALU.add).then_inc(lg_ok, 1)
            dve.wait_ge(lg_ok, TT // 4)
            bc = lambda a: a.unsqueeze(2).to_broadcast([P, TT, EXPERTS])
            link(V.tensor_reduce(red[:, 0, :], lg[:, :, :], AX.X, ALU.max))
            V.tensor_tensor(lg[:, :, :], lg[:, :, :], bc(red[:, 0, :]), ALU.subtract).then_inc(sh_ok, 1)
            dve.wait_ge(ex_ok, 1)
            link(V.tensor_reduce(red[:, 1, :], lg[:, :, :], AX.X, ALU.add))
            link(V.reciprocal(red[:, 1, :], red[:, 1, :]))
            link(V.tensor_tensor(pr[:, :, :], lg[:, :, :], bc(red[:, 1, :]), ALU.mult))
            rank = C["rank"][:, :].unsqueeze(1).to_broadcast([P, TT, EXPERTS])
            for c in range(TOPK):
                wc = R["w"][:, c, :]
                link(V.tensor_reduce(wc, pr[:, :, :], AX.X, ALU.max))
                link(V.tensor_tensor(w1[:, :, :], pr[:, :, :], bc(wc), ALU.is_equal))
                link(V.tensor_tensor(w1[:, :, :], w1[:, :, :], rank, ALU.mult))
                link(V.tensor_reduce(red[:, 2, :], w1[:, :, :], AX.X, ALU.max))
                link(V.tensor_tensor(oh[:, c, :, :], w1[:, :, :], bc(red[:, 2, :]), ALU.is_equal))
                if c == 0:
                    link(V.scalar_tensor_tensor(pr[:, :, :], oh[:, 0, :, :], -2.0, pr[:, :, :], ALU.mult, ALU.add))
            V.tensor_copy(ohb[:, :, :, :], oh[:, :, :, :]).then_inc(ohb_ok, 1)
            dve.wait_ge(cum_ok, 1)
            f = lambda a: a[:, :, :, :].rearrange("p c t e -> p (c t e)")
            link(V.tensor_copy(f(tot), PS[:, 1, :]))
            for c in range(TOPK):
                for e in range(EXPERTS):
                    last = V.tensor_tensor_scan(inc[:, c, :, e], zcol[:, :], tot[:, c, :, e], 0.0, ALU.mult, ALU.add)
            link(last)
            link(V.tensor_tensor(f(pos), PS[:, 0, :], f(inc), ALU.add))
            link(V.scalar_tensor_tensor(f(pos), f(pos), -1.0, f(tot), ALU.add, ALU.subtract))
            link(V.scalar_tensor_tensor(f(oh), f(pos), float(CAP), f(oh), ALU.is_lt, ALU.mult))
            link(V.tensor_scalar(kept[:, :, :], inc[:, :, TT - 1, :], float(CAP), None, ALU.min))
            link(V.tensor_tensor(kept[:, 0, :], kept[:, 0, :], kept[:, 1, :], ALU.add))
            V.tensor_copy(R["rows"][:, :], kept[:, 0, :])
            V.tensor_scalar(base[:, 0, :], C["region"][:, :], -float(DROPPED), None, ALU.add)
            link(V.tensor_scalar(base[:, 1, :], inc[:, 0, TT - 1, :], float(CAP), -float(DROPPED), ALU.min, ALU.add))
            link(V.tensor_tensor(base[:, 1, :], base[:, 1, :], C["region"][:, :], ALU.add))
            for c in range(TOPK):
                link(V.tensor_tensor(w1[:, :, :], pos[:, c, :, :],
                                     base[:, c, :].unsqueeze(1).to_broadcast([P, TT, EXPERTS]), ALU.add))
                link(V.tensor_tensor(w1[:, :, :], w1[:, :, :], oh[:, c, :, :], ALU.mult))
                link(V.tensor_reduce(slot[:, c, :], w1[:, :, :], AX.X, ALU.add))
                V.tensor_reduce(red[:, 2 + c, :], oh[:, c, :, :], AX.X, ALU.add)
            link(V.tensor_scalar(slot[:, :, :], slot[:, :, :], float(DROPPED), None, ALU.add))
            link(V.tensor_copy(R["idx"][:, :, :], slot[:, :, :]))
            link(V.scalar_tensor_tensor(R["w"][:, :, :], R["w"][:, :, :], 0.5, red[:, 2:4, :], ALU.mult, ALU.mult))
            def fill(i, first=False):
                for b in range(4):
                    if not first:
                        for c in range(TOPK):
                            dve.wait_ge(sent[b][c], i * 16)
                    normed(xs[:, b, :], i * 4 + b)
                    V.tensor_copy(ixs[:, b, :], R["idx"][:, :, bass.ds(i * 4 + b, 1)].rearrange("p c o -> p (c o)")).then_inc(xs_ok, 1)

            fill(0, first=True)
            with dve.Fori(1, TT // 4, 1) as i:
                fill(i)

        @block.gpsimd
        def _(gp):
            G = nc.gpsimd
            gp.wait_ge(var_ok, 1)
            G.tensor_tensor(rstd, rstd, mhalf, ALU.pow).then_inc(rstd_ok, 1)
            bound = gp.to_reg(ROWS - 1)
            if zero_rows:
                gp.wait_ge(zeroed, 16 * (ROWS // (8 * P)))
            with gp.Fori(0, TT // 4, 1) as i:
                for b in range(4):
                    gp.wait_ge(xs_ok, i * 4 + (b + 1))
                    gp.sem_inc(turned, 1)
                    for c in range(TOPK):
                        G.indirect_dma_start(out=xrows, out_offset=bass.IndirectOffsetOnAxis(ap=ixs[:, b, c:c + 1], axis=0),
                                             in_=xs[:, b, :], in_offset=None, bounds_check=bound,
                                             oob_is_err=False).then_inc(sent[b][c], 16)
            for b in range(4):
                for c in range(TOPK):
                    gp.wait_ge(sent[b][c], 16 * (TT // 4))

        @block.scalar
        def _(act):
            with act.Fori(0, TT // 8, 1) as i:
                for g in range(2):
                    act.wait_ge(tp_ok, i * 2 + (g + 1))
                    nc.scalar.activation(xnT[:, g, :, :], PS[:, 2 * g:2 * g + 2, :], ACT.Copy).then_inc(xnT_ok, 1)
            act.wait_ge(sh_ok, 1)
            nc.scalar.activation(lg[:, :, :], lg[:, :, :], ACT.Exp).then_inc(ex_ok, 1)

        @block.tensor
        def _(pe):
            with pe.Fori(0, TT // 8, 1) as i:
                for g in range(2):
                    pe.wait_ge(xn_ok, i * 2 + (g + 1))
                    for k in range(DK):
                        for a in range(4):
                            last = nc.tensor.transpose(PS[:, 2 * g + k, a * P:(a + 1) * P], xn[:, g, a, k * P:(k + 1) * P],
                                                       C["ident"][:, :])
                    last.then_inc(tp_ok, 1)
                for g in range(2):
                    pe.wait_ge(xnT_ok, i * 2 + (g + 1))
                    for a in range(4):
                        for k in range(DK):
                            last = nc.tensor.matmul(PS[:, 4 + g, a * EXPERTS:(a + 1) * EXPERTS],
                                                    xnT[:, g, k, a * P:(a + 1) * P], C["gate"][:, k, :],
                                                    start=(k == 0), stop=(k == DK - 1))
                    last.then_inc(lgp_ok, 1)
            pe.wait_ge(lg_ok, TT // 4)
            pe.wait_ge(ohb_ok, 1)
            ohf = ohb[:, :, :, :].rearrange("p c t e -> p (c t e)")
            nc.tensor.matmul(PS[:, 0, :], C["upper"][:, :], ohf, start=True, stop=True)
            nc.tensor.matmul(PS[:, 1, :], C["onesb"][:, :], ohf, start=True, stop=True).then_inc(cum_ok, 1)


def experts(nc, tag, C, PS, R, xrows, yrows, W1, W2, b2):
    ctx = ExitStack()
    with ctx:
        sem, sb = sem_maker(nc, C, tag), buf_maker(nc, ctx, tag)
        raw = sb("raw", [P, 4, FF])
        wh = sb("wh", [P, 2, 4, FF], FP32R)
        wl = sb("wl", [P, 2, 4, FF], FP32R)
        xin = sb("xin", [P, 2, CHT, D])
        xh = sb("xh", [P, 2, DK, CH], FP32R)
        xl = sb("xl", [P, 2, DK, CH], FP32R)
        u = sb("u", [P, FP, 2, CH])
        hh = sb("hh", [P, 2, FK, CH], FP32R)
        hl = sb("hl", [P, 2, FK, CH], FP32R)
        ysb = sb("ysb", [P, 2, CHT, D])
        b2_all = sb("b2", [P, EXPERTS, D])
        b2_in = sem("b2_in")
        wraw = [sem(f"wraw{q}") for q in range(4)]
        wh_ok, wl_ok = sem("wh_ok"), sem("wl_ok")
        xin_ok = [sem(f"xin{b}") for b in range(2)]
        xT_ok, xh_ok, xl_ok = sem("xT_ok"), sem("xh_ok"), sem("xl_ok")
        s1_ok, u_ok, hh_ok, hl_ok = sem("s1_ok"), sem("u_ok"), sem("hh_ok"), sem("hl_ok")
        y_ok, yb_ok, passed = sem("y_ok"), sem("yb_ok"), sem("passed")
        stored, ysb_free = [sem(f"stored{b}", own=True) for b in range(2)], sem("ysb_free")
        block = ctx.enter_context(nc.Block())
        B_XT, B_S1, B_Y = 0, 1, 5
        TURN = 2 * CPE
        Y0, YB0, YF0 = 1, 2, 2

        def chunks(eng, step):
            with eng.Fori(0, EXPERTS // 2 - 1, 1) as i:
                for c in range(TURN):
                    step(i, c, False)
            for c in range(TURN):
                step(EXPERTS // 2 - 1, c, True)

        def rows_of(eng, i, e2):
            return eng.value_load(R["rows"][0:1, bass.ds(i * 2 + e2, 1)], min_val=0, max_val=ROWS_E)

        def if_taken(eng, rows, c, work, signal):
            j = c % CPE
            if j < 2:
                return work()
            eng.sem_inc(passed, 1)
            with eng.If(rows > j * CH):
                work()
            with eng.Else():
                for s, so_far, n in signal:
                    eng.wait_ge(s, so_far)
                    eng.sem_inc(s, n)

        @block.sync
        def _(sp):
            def load_x(i, c):
                sp.dma_start(xin[:, c % 2, :, :],
                             xrows[bass.ds(i * (TURN * CH) + c * CH, CH), :].rearrange("(t p) d -> p t d", p=P)).then_inc(xin_ok[c % 2], 16)

            def load_w(e, q):
                if q < 2:
                    src = W1[bass.ds(e, 1), q * P:(q + 1) * P, :].rearrange("o p f -> p (o f)")
                    sp.dma_start(raw[:, q, :], src).then_inc(wraw[q], 16)
                else:
                    src = W2[bass.ds(e, 1), (q - 2) * 4 * P:(q - 1) * 4 * P, :].rearrange("o (j p) d -> p (o j) d", p=P)
                    sp.dma_start(raw[:, q, :].rearrange("p (j d) -> p j d", d=D), src).then_inc(wraw[q], 16)

            load_x(0, 0)
            load_x(0, 1)
            for q in range(4):
                load_w(0, q)
            sp.dma_start(b2_all[:, :, :].rearrange("p e d -> p (e d)"), b2.to_broadcast([P, EXPERTS * D])).then_inc(b2_in, 16)

            def step(i, c, last):
                e2, j = divmod(c, CPE)
                if j < 4 and not (last and e2 == 1):
                    sp.wait_ge(wl_ok, i * 8 + (4 * e2 + j + 1))
                    load_w(i * 2 + (e2 + 1), j)
                if not (last and c + 2 >= TURN):
                    sp.wait_ge(xT_ok, i * TURN + (c + 1))
                    load_x(i, c + 2)

            chunks(sp, step)

        @block.gpsimd
        def _(gp):
            def step(i, c, last):
                gp.wait_ge(yb_ok, i * TURN + (c + 1 + YB0))
                gp.dma_start(yrows[bass.ds(i * (TURN * CH) + c * CH, CH), :].rearrange("(t p) d -> p t d", p=P),
                             ysb[:, c % 2, :, :]).then_inc(stored[c % 2], 16)
                gp.wait_ge(stored[c % 2], i * (16 * CPE) + 16 * (c // 2 + 1))
                gp.sem_inc(ysb_free, 1)

            chunks(gp, step)

        @block.tensor
        def _(pe):
            M = nc.tensor.matmul
            pe.sem_inc(y_ok, Y0)

            def turn(i, c, first=False):
                pe.wait_ge(xin_ok[c % 2], i * (16 * CPE) + 16 * (c // 2 + 1))
                if not first:
                    pe.wait_ge(xl_ok, i * TURN + c)
                for k in range(DK):
                    for t in range(CHT):
                        last = nc.tensor.transpose(PS[:, B_XT, k * CH + t * P:k * CH + (t + 1) * P],
                                                   xin[:, c % 2, t, k * P:(k + 1) * P], C["ident"][:, :])
                last.then_inc(xT_ok, 1)

            rows = [None]

            def up(i, c, first=False):
                e2, j = divmod(c, CPE)
                w = e2 % 2
                if j == 0:
                    pe.wait_ge(wl_ok, i * 8 + (4 * e2 + 2))
                pe.wait_ge(xl_ok, i * TURN + (c + 1))
                if_taken(pe, rows[0], c, lambda: up_products(i, c, w, first), [(s1_ok, i * (TURN * FP) + c * FP, FP)])

            def up_products(i, c, w, first):
                for pair in range(FP):
                    if not first:
                        pe.wait_ge(u_ok, i * (TURN * FP) + ((c - 1) * FP + pair + 1))
                    for m in range(2):
                        f = slice((2 * pair + m) * P, (2 * pair + m + 1) * P)
                        terms = [(wx[:, w, k, f], rx[:, c % 2, k, :]) for k in range(DK)
                                 for wx, rx in ((wh, xh), (wh, xl), (wl, xh))]
                        for n, (a, r) in enumerate(terms):
                            last = M(PS[:, B_S1 + pair, m * CH:(m + 1) * CH], a, r, start=(n == 0), stop=(n == len(terms) - 1))
                    last.then_inc(s1_ok, 1)

            def down(i, c):
                e2, j = divmod(c, CPE)
                w = e2 % 2
                if j == 0:
                    pe.wait_ge(wl_ok, i * 8 + (4 * e2 + 4))
                pe.wait_ge(hl_ok, i * (TURN * FP) + (c + 1) * FP)
                pe.wait_ge(yb_ok, i * TURN + (c - 1 + YB0))
                if_taken(pe, rows[0], c, lambda: down_products(c, w), [(y_ok, i * TURN + (c + Y0), 1)])

            def down_products(c, w):
                for t in range(CHT):
                    ts = slice(t * P, (t + 1) * P)
                    terms = [(hx[:, c % 2, f, ts], wx[:, w, 2 + f // 4, (f % 4) * D:(f % 4 + 1) * D])
                             for f in range(FK) for hx, wx in ((hh, wh), (hl, wh), (hh, wl))]
                    for n, (a, r) in enumerate(terms):
                        last = M(PS[:, B_Y + c % 2, t * D:(t + 1) * D], a, r, start=(n == 0), stop=(n == len(terms) - 1))
                last.then_inc(y_ok, 1)

            turn(0, 0, first=True)
            turn(0, 1)
            up(0, 0, first=True)

            def step(i, c, last):
                if c % CPE == 0:
                    rows[0] = rows_of(pe, i, c // CPE)
                if not (last and c + 2 >= TURN):
                    turn(*((i, c + 2) if c + 2 < TURN else (i + 1, c + 2 - TURN)))
                if not (last and c + 1 >= TURN):
                    up(*((i, c + 1) if c + 1 < TURN else (i + 1, c + 1 - TURN)))
                down(i, c)

            chunks(pe, step)

        @block.scalar
        def _(act):
            A = nc.scalar.activation

            def split_w(e2, i, q):
                act.wait_ge(wraw[q], i * 32 + 16 * (e2 + 1))
                A(wh[:, e2 % 2, q, :], raw[:, q, :], ACT.Copy).then_inc(wh_ok, 1)

            def rows(i, c):
                act.wait_ge(xT_ok, i * TURN + (c + 1))
                A(xh[:, c % 2, :, :].rearrange("p k c -> p (k c)"), PS[:, B_XT, :], ACT.Copy).then_inc(xh_ok, 1)

            taken = [None]

            def hidden(i, c):
                if_taken(act, taken[0], c, lambda: high(i, c), [(hh_ok, i * (TURN * FP) + c * FP, FP)])

            def high(i, c):
                for pair in range(FP):
                    act.wait_ge(u_ok, i * (TURN * FP) + (c * FP + pair + 1))
                    A(hh[:, c % 2, 2 * pair:2 * pair + 2, :], u[:, pair, :, :], ACT.Relu).then_inc(hh_ok, 1)

            rows(0, 0)
            rows(0, 1)
            for q in range(4):
                split_w(0, 0, q)
            hidden(0, 0)

            def step(i, c, last):
                e2, j = divmod(c, CPE)
                if j == 0:
                    taken[0] = rows_of(act, i, e2)
                if not (last and c + 2 >= TURN):
                    act.wait_ge(s1_ok, i * (TURN * FP) + (c + 1) * FP)
                    rows(*((i, c + 2) if c + 2 < TURN else (i + 1, c + 2 - TURN)))
                act.wait_ge(y_ok, i * TURN + (c + Y0))
                if not (last and c + 1 >= TURN):
                    hidden(*((i, c + 1) if c + 1 < TURN else (i + 1, c + 1 - TURN)))
                if j >= 1 and not (last and e2 == 1):
                    split_w(*((1, i) if e2 == 0 else (0, i + 1)), j - 1)

            chunks(act, step)

        @block.vector
        def _(dve):
            V = nc.vector
            dve.sem_inc(yb_ok, YB0)
            dve.sem_inc(ysb_free, YF0)

            def split_w(e2, i, q):
                dve.wait_ge(wh_ok, i * 8 + (4 * e2 + q + 1))
                V.tensor_tensor(wl[:, e2 % 2, q, :], raw[:, q, :], wh[:, e2 % 2, q, :].bitcast(FP32), ALU.subtract).then_inc(wl_ok, 1)

            def rows(i, c):
                dve.wait_ge(xh_ok, i * TURN + (c + 1))
                V.tensor_tensor(xl[:, c % 2, :, :].rearrange("p k c -> p (k c)"), PS[:, B_XT, :],
                                xh[:, c % 2, :, :].rearrange("p k c -> p (k c)").bitcast(FP32), ALU.subtract).then_inc(xl_ok, 1)

            taken = [None]

            def hidden(i, c):
                if_taken(dve, taken[0], c, lambda: bias_and_low(i, c),
                         [(u_ok, i * (TURN * FP) + c * FP, FP), (hl_ok, i * (TURN * FP) + c * FP, FP)])

            def bias_and_low(i, c):
                e2 = c // CPE

                def bias(pair):
                    dve.wait_ge(s1_ok, i * (TURN * FP) + (c * FP + pair + 1))
                    b1 = C["b1"][:, bass.ds(i * (2 * FK) + (e2 * FK + 2 * pair), 2)]
                    V.tensor_tensor(u[:, pair, :, :], PS[:, B_S1 + pair, :].rearrange("p (m c) -> p m c", m=2),
                                    b1.unsqueeze(2).to_broadcast([P, 2, CH]), ALU.add).then_inc(u_ok, 1)

                def low(pair):
                    dve.wait_ge(hh_ok, i * (TURN * FP) + (c * FP + pair + 1))
                    V.scalar_tensor_tensor(hl[:, c % 2, 2 * pair:2 * pair + 2, :], u[:, pair, :, :], 0.0,
                                           hh[:, c % 2, 2 * pair:2 * pair + 2, :].bitcast(FP32), ALU.max, ALU.subtract).then_inc(hl_ok, 1)

                bias(0)
                for pair in range(1, FP):
                    bias(pair)
                    low(pair - 1)
                low(FP - 1)

            def out(i, c):
                e2 = c // CPE
                dve.wait_ge(y_ok, i * TURN + (c + 1 + Y0))
                dve.wait_ge(ysb_free, i * TURN + (c - 1 + YF0))
                b2 = b2_all[:, bass.ds(i * 2 + e2, 1), :].rearrange("p o d -> p (o d)")
                V.tensor_tensor(ysb[:, c % 2, :, :], PS[:, B_Y + c % 2, :].rearrange("p (t d) -> p t d", t=CHT),
                                b2.unsqueeze(1).to_broadcast([P, CHT, D]), ALU.add).then_inc(yb_ok, 1)

            rows(0, 0)
            rows(0, 1)
            for q in range(4):
                split_w(0, 0, q)
            hidden(0, 0)
            dve.wait_ge(b2_in, 16)

            def step(i, c, last):
                e2, j = divmod(c, CPE)
                if j == 0:
                    taken[0] = rows_of(dve, i, e2)
                if not (last and c + 2 >= TURN):
                    dve.wait_ge(s1_ok, i * (TURN * FP) + (c + 1) * FP)
                    rows(*((i, c + 2) if c + 2 < TURN else (i + 1, c + 2 - TURN)))
                dve.wait_ge(y_ok, i * TURN + (c + Y0))
                if not (last and c + 1 >= TURN):
                    hidden(*((i, c + 1) if c + 1 < TURN else (i + 1, c + 1 - TURN)))
                out(i, c)
                if j >= 1 and not (last and e2 == 1):
                    split_w(*((1, i) if e2 == 0 else (0, i + 1)), j - 1)

            chunks(dve, step)


def combine(nc, tag, C, X, R, yrows, out_dram):
    ctx = ExitStack()
    with ctx:
        sem, sb = sem_maker(nc, C, tag), buf_maker(nc, ctx, tag)
        NB = 8
        got = sb("got", [P, NB, TOPK, D])
        ix = sb("ix", [P, NB, TOPK], U32)
        cleared, ix_ok, added, done, turned = sem("cleared"), sem("ix_ok"), sem("added"), sem("done"), sem("turned")
        landed = [[sem(f"landed{b}_{c}", own=True) for c in range(TOPK)] for b in range(NB)]
        block = ctx.enter_context(nc.Block())

        @block.gpsimd
        def _(gp):
            G = nc.gpsimd
            G.memset(got[:, :, :, :], 0.0).then_inc(cleared, 1)
            gp.wait_ge(cleared, 1)
            bound = gp.to_reg(ROWS - 1)
            with gp.Fori(0, TT // NB, 1) as i:
                for b in range(NB):
                    gp.wait_ge(added, i * NB + (b + 1))
                    G.tensor_copy(ix[:, b, :], R["idx"][:, :, bass.ds(i * NB + b, 1)].rearrange("p c o -> p (c o)")).then_inc(ix_ok, 1)
                    gp.wait_ge(ix_ok, i * NB + (b + 1))
                    gp.sem_inc(turned, 1)
                    for c in range(TOPK):
                        G.indirect_dma_start(out=got[:, b, c, :], out_offset=None, in_=yrows,
                                             in_offset=bass.IndirectOffsetOnAxis(ap=ix[:, b, c:c + 1], axis=0),
                                             bounds_check=bound, oob_is_err=False).then_inc(landed[b][c], 16)

        @block.vector
        def _(dve):
            V = nc.vector
            dve.sem_inc(added, NB)
            with dve.Fori(0, TT // NB, 1) as i:
                for b in range(NB):
                    x = X[:, bass.ds(i * NB + b, 1), :].rearrange("p o d -> p (o d)")
                    for c in range(TOPK):
                        dve.wait_ge(landed[b][c], i * 16 + 16)
                        w = R["w"][:, c, bass.ds(i * NB + b, 1)]
                        last = V.scalar_tensor_tensor(x, got[:, b, c, :], w, x, ALU.mult, ALU.add)
                        if c == 0:
                            last.then_inc(done, 1)
                            dve.wait_ge(done, i * NB + (b + 1))
                    last.then_inc(added, 1)

        if out_dram is not None:
            @block.sync
            def _(sp):
                stored = sem("stored")
                Q = TT // 4
                for q in range(4):
                    sp.wait_ge(added, NB + (q + 1) * Q)
                    sp.dma_start(out_dram[q * Q * P:(q + 1) * Q * P, :].rearrange("(t p) d -> p t d", p=P),
                                 X[:, q * Q:(q + 1) * Q, :]).then_inc(stored, 16)
                sp.wait_ge(stored, 64)


def mamba(nc, X, C, PS, mamba_w, mamba_c, bc_dram):
    ctx = ExitStack()
    with ctx:
        sem, sb = sem_maker(nc, C, "m"), buf_maker(nc, ctx, "m")
        MW = sb("MW", [P, W_ALL])
        mc = sb("mc", [P, EK, C_ALL])
        A = sb("A", [P, EK, DS])
        skip = sb("skip", [P, EK, P])
        mask = sb("mask", [P, MCH + 1], U32)
        st = sb("st", [P, TT, 6])
        tk = sb("tk", [P, 5, TT])
        mean, rstd, rrms, var, mhalf = (tk[:, n, :] for n in range(5))
        XI = sb("XI", [P, EK, DC - 1 + CT])
        U = sb("U", [P, EK, CT])
        T3 = sb("T3", [P, EK, CT])
        xrT = sb("xrT", [P, DK, CT])
        hT = sb("hT", [P, DK, CT])
        XR = sb("XR", [P, CTT, D])
        XP = sb("XP", [P, CTT, D])
        ssq = sb("ssq", [P, CTT])
        SZ = sb("SZ", [P, 2, EK, CT])
        DT = sb("DT", [P, 2, EK, CT])
        DTU = sb("DTU", [P, 2, EK, CT])
        dA = sb("dA", [P, EK, CT])
        dB = sb("dB", [P, EK, CT])
        H = sb("H", [P, EK, CT])
        G = sb("G", [P, 2, EK, CT])
        ST = sb("ST", [P, DS, EK])
        NBC = 2
        BC = sb("BC", [P, NBC, 2, CT])
        sp1 = sb("sp1", [P, EK, CT])
        XD = sb("XD", [P, CT])

        w_in, mc_in, dch, a_raw, a_ok, diag_ok = (sem(n) for n in ("w_in", "mc_in", "dch", "a_raw", "a_ok", "diag_ok"))
        var_ok, rstd_ok, ms_ok, rrms_ok = (sem(n) for n in ("var_ok", "rstd_ok", "ms_ok", "rrms_ok"))
        f_w, f_r = sem("f_w"), sem("f_r")
        k_w, k_r = sem("k_w"), sem("k_r")
        xr_ok, tail_ok, u_ok, sz_ok = sem("xr_ok"), sem("tail_ok"), sem("u_ok"), sem("sz_ok")
        tap0_ok, taps_ok = sem("tap0_ok"), sem("taps_ok")
        sp_abs, sp_exp, sp_ln, dt_ok, dtu_ok = (sem(n) for n in ("sp_abs", "sp_exp", "sp_ln", "dt_ok", "dtu_ok"))
        bc_out = sem("bc_out")
        b_in, c_in = ([sem(f"{n}_in{b}") for b in range(NBC)] for n in "bc")
        dA_ok, dB_ok, scanned, g_ok, g_read, kept = (sem(n) for n in ("dA_ok", "dB_ok", "scanned", "g_ok", "g_read", "kept"))
        yz_ok, xn_ok, sq_ok, v_ok, rs_ok, hr_ok, q_ok, xa_ok = (sem(n) for n in (
            "yz_ok", "xn_ok", "sq_ok", "v_ok", "rs_ok", "hr_ok", "q_ok", "xa_ok"))
        block = ctx.enter_context(nc.Block())

        B_F, B_K, B_Y = 0, 2, 4
        F_USE = {use: n for n, use in enumerate(
            [("T", 0), ("T", 1), ("x", 0), ("x", 1), ("x", 2), ("x", 3), ("z", 0), ("z", 1), ("z", 2), ("z", 3),
             ("xp", 0), ("dt", 0), ("dt", 1), ("dt", 2), ("dt", 3)])}
        K_USE = {use: n for n, use in enumerate(
            [("out", 0), ("out", 1), ("T", 0), ("T", 1), ("fc", 0), ("fc", 1), ("fc", 2), ("fc", 3), ("pj", 0), ("pj", 1)])}
        NF, NK = len(F_USE), len(K_USE)
        NTAP = EK * (DC - 1)
        KR0 = 2
        ON_PE, ON_ACT, ON_DVE, ON_POOL = range(4)
        FRONT = {
            "F_xr": (0, 0, -1, 0), "F_T": (0, 0, 0, 0), "F_x01": (1, 1, 1, 1), "F_x23": (2, 2, 2, 2),
            "F_c01": (2, 2, 2, 2), "F_c23": (3, 3, 3, 3), "F_z01": (3, 3, 3, 3), "F_z23": (4, 4, 4, 4),
            "F_silu": (5, 5, 5, 5), "F_xp": (7, 7, 7, 7), "F_dt": (9, 9, 9, 9), "F_du": (11, 11, 11, 11),
        }
        BACK = {
            "K_out0": (4, 4, 4, 4), "K_out1": (5, 5, 5, 5), "K_sq": (6, 6, 6, 6), "K_v": (7, 7, 7, 7),
            "K_hr": (8, 8, 8, 8), "K_T": (9, 9, 9, 9), "K_fc01": (10, 10, 10, 10), "K_fc23": (11, 11, 11, 11),
            "K_pj0": (12, 12, 12, 12), "K_pj1": (13, 13, 13, 13),
        }
        SEND_AT = 11

        def run(eng, turn, front, back):
            for p in FRONT:
                front(p, 0, 0)
            turn(0, 0, True, False)
            with eng.Fori(0, MCH // 2 - 1, 1) as i:
                turn(i * 2 + 1, 1, True, True)
                turn(i * 2 + 2, 0, True, True)
            turn(MCH - 1, 1, False, True)
            for p in ["K_yz"] + list(BACK):
                back(p, MCH - 1, 1)

        def items(engine, s, k, par, has_front, has_back, front, back):
            for p in FRONT:
                if FRONT[p][engine] == s and has_front:
                    front(p, k + 1, 1 - par)
            for p in BACK:
                if BACK[p][engine] == s and has_back:
                    back(p, k - 1, 1 - par)

        def is_first(k):
            return isinstance(k, int) and k == 0

        def f_bank(use, rows=P):
            return PS[0:rows, B_F + F_USE[use] % 2, :]

        def k_bank(use):
            return PS[:, B_K + K_USE[use] % 2, :]

        def weights(at, width, tile, lo, n):
            return MW[:, at + tile * width + lo:at + tile * width + lo + n]

        @block.sync
        def _(sp):
            sp.dma_start(mc[:, :, :], mamba_c).then_inc(mc_in, 16)
            sp.dma_start(MW[:, :], mamba_w).then_inc(w_in, 16)

            def load(k, s):
                for j, landed, used in ((0, b_in, dB_ok), (1, c_in, g_ok)):
                    if s >= NBC or not is_first(k):
                        sp.wait_ge(used, k * (2 * DS) + 2 * (s - NBC + 1))
                    src = bc_dram[bass.ds(k, 1), j, s:s + 1, :].rearrange("o q t -> (o q) t")
                    sp.dma_start(BC[:, s % NBC, j, :], src.to_broadcast([P, CT])).then_inc(landed[s % NBC], 16)

            def front(p, k, par):
                if p == "F_xp":
                    sp.wait_ge(f_r, k * NF + (F_USE["xp", 0] + 1))
                    sp.dma_start(bc_dram[bass.ds(k, 1), :, :, :].rearrange("o j s t -> (o j s) t"),
                                 XD[DR:XPR, :]).then_inc(bc_out, 16)

            def back(p, k, par):
                pass

            def turn(k, par, has_front, has_back):
                sp.wait_ge(bc_out, k * 16 + 16)
                for s in range(DS):
                    load(k, s)
                    if s == SEND_AT and has_front:
                        front("F_xp", k + 1, 1 - par)

            run(sp, turn, front, back)

        @block.tensor
        def _(pe):
            M = nc.tensor.matmul
            pe.sem_inc(k_r, KR0)
            pe.wait_ge(w_in, 16)
            pe.wait_ge(diag_ok, 1)

            def front(p, k, par):
                def bank_free(use):
                    if not (is_first(k) and F_USE[use] < 2):
                        pe.wait_ge(f_r, k * NF + max(F_USE[use] - 1, 0))

                if p == "F_T":
                    pe.wait_ge(xr_ok, k + 1)
                    for d in range(DK):
                        bank_free(("T", d))
                        for t in range(CTT):
                            last = nc.tensor.transpose(f_bank(("T", d))[:, t * P:(t + 1) * P], XR[:, t, d * P:(d + 1) * P], C["ident"][:, :])
                        last.then_inc(f_w, 1)
                elif p[:3] in ("F_x", "F_z") and p[3:] in ("01", "23"):
                    for n in (int(p[3]), int(p[4])):
                        use = (p[2], n)
                        pe.wait_ge(f_r, k * NF + 2)
                        bank_free(use)
                        for d in range(DK):
                            last = M(f_bank(use), weights(W_IN, 2 * DI, d, (0 if p[2] == "x" else DI) + n * P, P), xrT[:, d, :],
                                     start=(d == 0), stop=(d == DK - 1))
                        last.then_inc(f_w, 1)
                elif p == "F_xp":
                    use = ("xp", 0)
                    pe.wait_ge(u_ok, k + 1)
                    bank_free(use)
                    for e in range(EK):
                        last = M(f_bank(use, XPR), weights(W_XP, XPR, e, 0, XPR), U[:, e, :], start=(e == 0), stop=(e == EK - 1))
                    last.then_inc(f_w, 1)
                elif p == "F_dt":
                    pe.wait_ge(f_r, k * NF + (F_USE["xp", 0] + 1))
                    for n in range(EK):
                        bank_free(("dt", n))
                        M(f_bank(("dt", n)), MW[0:DR, W_DT + n * P:W_DT + (n + 1) * P], XD[0:DR, :], start=True, stop=True).then_inc(f_w, 1)

            def back(p, k, par):
                def bank_free(use):
                    pe.wait_ge(k_r, k * NK + (K_USE[use] - 1 + KR0))

                if p[:-1] in ("K_out", "K_pj"):
                    kind, at, ready = ("out", W_OUT, yz_ok) if p[:-1] == "K_out" else ("pj", W_PJ, q_ok)
                    a = int(p[-1])
                    pe.wait_ge(ready, k * 2 + 2)
                    bank_free((kind, a))
                    for t in (2 * a, 2 * a + 1):
                        for e in range(EK):
                            last = M(k_bank((kind, a))[:, (t % 2) * D:(t % 2 + 1) * D], T3[:, e, t * P:(t + 1) * P],
                                     weights(at, D, e, 0, D), start=(e == 0), stop=(e == EK - 1))
                    last.then_inc(k_w, 1)
                elif p == "K_T":
                    pe.wait_ge(hr_ok, k + 1)
                    for d in range(DK):
                        bank_free(("T", d))
                        for t in range(CTT):
                            last = nc.tensor.transpose(k_bank(("T", d))[:, t * P:(t + 1) * P], XR[:, t, d * P:(d + 1) * P], C["ident"][:, :])
                        last.then_inc(k_w, 1)
                elif p[:4] == "K_fc":
                    pe.wait_ge(k_r, k * NK + (K_USE["T", 1] + 1 + KR0))
                    for n in (int(p[4]), int(p[5])):
                        bank_free(("fc", n))
                        for d in range(DK):
                            last = M(k_bank(("fc", n)), weights(W_FC, 2 * D, d, n * P, P), hT[:, d, :], start=(d == 0), stop=(d == DK - 1))
                        last.then_inc(k_w, 1)

            def turn(k, par, has_front, has_back):
                for s in range(DS):
                    items(ON_PE, s, k, par, has_front, has_back, front, back)
                    if s == 0:
                        pe.wait_ge(u_ok, k + 1)
                        for e in range(EK):
                            if has_back:
                                pe.wait_ge(yz_ok, k * 2 + (e // 2 - 1))
                            M(PS[:, B_Y + e, :], skip[:, e, :], U[:, e, :], start=True, stop=False)
                    for pair in range(2):
                        pe.wait_ge(g_ok, k * (2 * DS) + (2 * s + pair + 1))
                        for e in (2 * pair, 2 * pair + 1):
                            last = M(PS[:, B_Y + e, :], C["ident"][:, :], G[:, s % 2, e, :], start=False, stop=(s == DS - 1))
                        last.then_inc(g_read, 1)

            run(pe, turn, front, back)

        @block.scalar
        def _(act):
            def F(out, in_, func, **kw):
                return nc.scalar.activation(out, in_, func, **kw)

            def exp_set():
                act.preload_act_table_set("natural_log_exp_and_others")

            act.wait_ge(mc_in, 16)
            exp_set()
            F(A[:, :, :], mc[:, :, C_AL:C_AL + DS], ACT.Exp).then_inc(a_raw, 1)
            act.wait_ge(a_ok, 1)

            def evac(use, k, out, **kw):
                act.wait_ge(f_w, k * NF + (F_USE[use] + 1))
                F(out, f_bank(use), kw.pop("func", ACT.Copy), **kw).then_inc(f_r, 1)

            def front(p, k, par):
                if p == "F_T":
                    for d in range(DK):
                        evac(("T", d), k, xrT[:, d, :])
                elif p in ("F_x01", "F_x23"):
                    act.wait_ge(tail_ok, k + 1)
                    for n in (int(p[3]), int(p[4])):
                        evac(("x", n), k, XI[:, n, DC - 1:])
                elif p in ("F_z01", "F_z23"):
                    if not (isinstance(k, int) and k < 2):
                        act.wait_ge(yz_ok, k * 2 - 2)
                    for n in (int(p[3]), int(p[4])):
                        evac(("z", n), k, SZ[:, par, n, :])
                elif p[:3] == "F_c":
                    if not is_first(k):
                        act.wait_ge(dtu_ok, k * 2)
                        act.wait_ge(g_read, (k - 1) * (2 * DS) + 1)
                    for n in (int(p[3]), int(p[4])):
                        act.wait_ge(f_r, k * NF + (F_USE["x", n] + 1))
                        F(U[:, n, :], XI[:, n, 0:CT], ACT.Identity, scale=mc[:, n, C_CW:C_CW + 1],
                          bias=mc[:, n, C_CB:C_CB + 1]).then_inc(tap0_ok, 1)
                elif p == "F_silu":
                    act.wait_ge(f_r, k * NF + (F_USE["z", 3] + 1))
                    act.wait_ge(taps_ok, k * NTAP + NTAP)
                    F(U[:, :, :], U[:, :, :], ACT.Silu).then_inc(u_ok, 1)
                    F(SZ[:, par, :, :], SZ[:, par, :, :], ACT.Silu).then_inc(sz_ok, 1)
                    exp_set()
                elif p == "F_xp":
                    if not is_first(k):
                        act.wait_ge(bc_out, k * 16)
                    act.wait_ge(f_w, k * NF + (F_USE["xp", 0] + 1))
                    F(XD[0:XPR, :], f_bank(("xp", 0), XPR), ACT.Copy).then_inc(f_r, 1)
                elif p == "F_dt":
                    if not is_first(k):
                        act.wait_ge(dt_ok, k * 2)
                    for n in range(EK):
                        act.wait_ge(f_w, k * NF + (F_USE["dt", n] + 1))
                        bias = mc[:, n, C_DB:C_DB + 1]
                        F(DT[:, par, n, :], f_bank(("dt", n)), ACT.Relu, bias=bias)
                        F(sp1[:, n, :], f_bank(("dt", n)), ACT.Abs, bias=bias).then_inc(f_r, 1)
                    for pair in range(2):
                        es = slice(2 * pair, 2 * pair + 2)
                        act.wait_ge(f_r, k * NF + (F_USE["dt", 2 * pair + 1] + 1))
                        F(sp1[:, es, :], sp1[:, es, :], ACT.Exp, scale=-1.0).then_inc(sp_exp, 1)
                    for pair in range(2):
                        es = slice(2 * pair, 2 * pair + 2)
                        act.wait_ge(sp_exp, k * 2 + (pair + 1))
                        F(sp1[:, es, :], sp1[:, es, :], ACT.Ln, bias=1.0).then_inc(sp_ln, 1)

            def back(p, k, par):
                if p == "K_sq":
                    act.wait_ge(k_r, k * NK + 2 + KR0)
                    for t in range(CTT):
                        last = F(XR[:, t, :], XP[:, t, :], ACT.Square, accum_out=ssq[:, t:t + 1])
                    last.then_inc(sq_ok, 1)
                elif p == "K_hr":
                    act.wait_ge(rs_ok, k + 1)
                    for t in range(CTT):
                        last = F(XR[:, t, :], XP[:, t, :], ACT.Copy, scale=ssq[:, t:t + 1])
                    last.then_inc(hr_ok, 1)
                elif p == "K_T":
                    for d in range(DK):
                        act.wait_ge(k_w, k * NK + (K_USE["T", d] + 1))
                        F(hT[:, d, :], k_bank(("T", d)), ACT.Copy).then_inc(k_r, 1)
                elif p[:4] == "K_fc":
                    for n in (int(p[4]), int(p[5])):
                        act.wait_ge(k_w, k * NK + (K_USE["fc", n] + 1))
                        F(T3[:, n, :], k_bank(("fc", n)), ACT.Relu).then_inc(k_r, 1)
                    act.wait_ge(k_r, k * NK + (K_USE["fc", n] + 1 + KR0))
                    F(T3[:, n - 1:n + 1, :], T3[:, n - 1:n + 1, :], ACT.Square).then_inc(q_ok, 1)

            def decay(k, par, s):
                if s == 0:
                    act.wait_ge(dt_ok, k * 2 + 2)
                for e in range(EK):
                    if not (is_first(k) and s == 0):
                        act.wait_ge(scanned, k * (DS * EK) + ((s - 1) * EK + e + 1))
                    F(dA[:, e, :], DT[:, par, e, :], ACT.Exp, scale=A[:, e, s:s + 1]).then_inc(dA_ok, 1)

            def turn(k, par, has_front, has_back):
                decay(k, par, 0)
                for s in range(DS):
                    if s + 1 < DS:
                        decay(k, par, s + 1)
                    items(ON_ACT, s, k, par, has_front, has_back, front, back)

            run(act, turn, front, back)

        @block.gpsimd
        def _(gp):
            G_ = nc.gpsimd
            gp.wait_ge(var_ok, 1)
            G_.tensor_tensor(rstd, rstd, mhalf, ALU.pow).then_inc(rstd_ok, 1)
            gp.wait_ge(ms_ok, 1)
            G_.tensor_tensor(rrms, rrms, mhalf, ALU.pow).then_inc(rrms_ok, 1)

            def front(p, k, par):
                if p == "F_du":
                    for pair in range(2):
                        es = slice(2 * pair, 2 * pair + 2)
                        gp.wait_ge(sp_ln, k * 2 + (pair + 1))
                        G_.tensor_tensor(DT[:, par, es, :], DT[:, par, es, :], sp1[:, es, :], ALU.add).then_inc(dt_ok, 1)

            def back(p, k, par):
                if p == "K_v":
                    gp.wait_ge(v_ok, k + 1)
                    G_.tensor_tensor(ssq[:, :], ssq[:, :], mhalf[:, 0:CTT], ALU.pow).then_inc(rs_ok, 1)

            def turn(k, par, has_front, has_back):
                gp.wait_ge(dtu_ok, k * 2 + 2)
                for s in range(DS):
                    gp.wait_ge(b_in[s % NBC], k * (16 * DS // NBC) + 16 * (s // NBC + 1))
                    for pair in range(2):
                        if not (is_first(k) and s == 0):
                            gp.wait_ge(scanned, k * (DS * EK) + ((s - 1) * EK + 2 * pair + 2))
                        es = slice(2 * pair, 2 * pair + 2)
                        G_.tensor_tensor(dB[:, es, :], DTU[:, par, es, :], BC[:, s % NBC, 0:1, :].to_broadcast([P, 2, CT]),
                                         ALU.mult).then_inc(dB_ok, 1)
                    items(ON_POOL, s, k, par, has_front, has_back, front, back)

            run(gp, turn, front, back)

        @block.vector
        def _(dve):
            V = nc.vector
            link = chain(dve, dch)
            V.memset(mhalf, -0.5)
            link(V.memset(mask[:, :].bitcast(mybir.dt.int32), -1))
            V.memset(ST[:, :, :], 0.0)
            V.memset(XI[:, :, 0:DC - 1], 0.0).then_inc(tail_ok, 1)
            with dve.Fori(0, TT, 1) as t:
                V.bn_stats(st[:, bass.ds(t, 1), :].rearrange("p o s -> p (o s)"),
                           X[:, bass.ds(t, 1), :].rearrange("p o d -> p (o d)"))
            for k in range(0, MCH, MCH // BATCH):
                link(V.memset(mask[:, k:k + 1].bitcast(mybir.dt.int32), 0))
            dve.wait_ge(mc_in, 16)
            for e in range(EK):
                last = V.tensor_scalar(skip[:, e, :], C["ident"][:, :], mc[:, e, C_D:C_D + 1], None, ALU.mult)
            last.then_inc(diag_ok, 1)
            link(V.tensor_tensor(mean, st[:, :, 1], st[:, :, 4], ALU.add))
            V.tensor_tensor(var, st[:, :, 1], st[:, :, 4], ALU.subtract)
            link(V.tensor_tensor(rstd, st[:, :, 2], st[:, :, 5], ALU.add))
            link(V.tensor_scalar(mean, mean, 0.5, None, ALU.mult))
            link(V.tensor_tensor(var, var, var, ALU.mult))
            link(V.tensor_scalar(var, var, 0.25, None, ALU.mult))
            link(V.scalar_tensor_tensor(var, rstd, 1.0 / D, var, ALU.mult, ALU.add))
            V.tensor_scalar(rstd, var, LN_EPS, None, ALU.add).then_inc(var_ok, 1)
            dve.wait_ge(a_raw, 1)
            V.tensor_scalar(A[:, :, :], A[:, :, :], -1.0, None, ALU.mult).then_inc(a_ok, 1)
            dve.wait_ge(rstd_ok, 1)
            link(V.tensor_tensor(rrms, rstd, rstd, ALU.mult))
            link(V.tensor_tensor(rrms, rrms, var, ALU.mult))
            V.tensor_scalar(rrms, rrms, RMS_EPS, None, ALU.add).then_inc(ms_ok, 1)
            dve.wait_ge(rrms_ok, 1)
            link(V.tensor_tensor(rrms, rrms, rstd, ALU.mult))

            def tile(k, t, n=1):
                x = X[:, bass.ds(k * CTT + t, n), :]
                return x.rearrange("p o d -> p (o d)") if n == 1 else x

            def col(a, k, t):
                return a[:, bass.ds(k * CTT + t, 1)]

            def front(p, k, par):
                if p == "F_xr":
                    for t in range(CTT):
                        last = V.tensor_scalar(XR[:, t, :], tile(k, t), col(mean, k, t), col(rrms, k, t), ALU.subtract, ALU.mult)
                    last.then_inc(xr_ok, 1)
                    if not is_first(k):
                        dve.wait_ge(taps_ok, k * NTAP)
                        dve.wait_ge(tap0_ok, k * EK)
                        V.tensor_tensor(XI[:, :, 0:DC - 1].bitcast(U32), XI[:, :, CT:].bitcast(U32),
                                        mask[:, bass.ds(k, 1)].unsqueeze(2).to_broadcast([P, EK, DC - 1]),
                                        ALU.bitwise_and).then_inc(tail_ok, 1)
                elif p[:3] == "F_c":
                    lo = int(p[3])
                    for tap in range(1, DC):
                        for n in (lo, lo + 1):
                            if tap == 1:
                                dve.wait_ge(tap0_ok, k * EK + (n + 1))
                            else:
                                dve.wait_ge(taps_ok, k * NTAP + (lo * (DC - 1) + 2 * (tap - 2) + (n - lo) + 1))
                            V.scalar_tensor_tensor(U[:, n, :], XI[:, n, tap:tap + CT], mc[:, n, C_CW + tap:C_CW + tap + 1],
                                                   U[:, n, :], ALU.mult, ALU.add).then_inc(taps_ok, 1)
                elif p == "F_du":
                    for pair in range(2):
                        es = slice(2 * pair, 2 * pair + 2)
                        dve.wait_ge(dt_ok, k * 2 + (pair + 1))
                        V.tensor_tensor(DTU[:, par, es, :], DT[:, par, es, :], U[:, es, :], ALU.mult).then_inc(dtu_ok, 1)

            def back(p, k, par):
                if p == "K_yz":
                    dve.wait_ge(sz_ok, k + 1)
                    for pair in range(2):
                        es = slice(2 * pair, 2 * pair + 2)
                        dve.wait_ge(g_read, k * (2 * DS) + (2 * DS - 1 + pair))
                        V.tensor_tensor(T3[:, es, :], PS[:, B_Y + 2 * pair:B_Y + 2 * pair + 2, :], SZ[:, par, es, :], ALU.mult).then_inc(yz_ok, 1)
                elif p[:-1] == "K_out":
                    a = int(p[-1])
                    for t in (2 * a, 2 * a + 1):
                        last = V.tensor_scalar(XP[:, t, :], tile(k, t), col(mean, k, t), col(rstd, k, t), ALU.subtract, ALU.mult)
                    last.then_inc(xn_ok, 1)
                    dve.wait_ge(xn_ok, k * 2 + (a + 1))
                    dve.wait_ge(k_w, k * NK + (K_USE["out", a] + 1))
                    xp = XP[:, 2 * a:2 * a + 2, :]
                    V.tensor_tensor(xp, xp, k_bank(("out", a)).rearrange("p (t d) -> p t d", t=2), ALU.add).then_inc(k_r, 1)
                elif p == "K_v":
                    dve.wait_ge(sq_ok, k + 1)
                    V.tensor_scalar(ssq[:, :], ssq[:, :], 1.0 / D, RMS_EPS, ALU.mult, ALU.add).then_inc(v_ok, 1)
                elif p[:-1] == "K_pj":
                    a = int(p[-1])
                    x = tile(k, 2 * a, 2)
                    V.tensor_tensor(x, x, XP[:, 2 * a:2 * a + 2, :], ALU.add).then_inc(xa_ok, 1)
                    dve.wait_ge(xa_ok, k * 2 + (a + 1))
                    dve.wait_ge(k_w, k * NK + (K_USE["pj", a] + 1))
                    V.tensor_tensor(x, x, k_bank(("pj", a)).rearrange("p (t d) -> p t d", t=2), ALU.add).then_inc(k_r, 1)

            def turn(k, par, has_front, has_back):
                items(ON_DVE, -1, k, par, has_front, has_back, front, back)
                for s in range(DS):
                    if s > 0 or not is_first(k):
                        dve.wait_ge(kept, k * DS + s)
                    for e in range(EK):
                        dve.wait_ge(dA_ok, k * (DS * EK) + (s * EK + e + 1))
                        if e % 2 == 0:
                            dve.wait_ge(dB_ok, k * (2 * DS) + (2 * s + e // 2 + 1))
                        V.tensor_tensor_scan(H[:, e, :], dA[:, e, :], dB[:, e, :], ST[:, s, e:e + 1], ALU.mult, ALU.add).then_inc(scanned, 1)
                    if s == 0 and has_back:
                        back("K_yz", k - 1, 1 - par)
                    dve.wait_ge(c_in[s % NBC], k * (16 * DS // NBC) + 16 * (s // NBC + 1))
                    for pair in range(2):
                        es = slice(2 * pair, 2 * pair + 2)
                        dve.wait_ge(scanned, k * (DS * EK) + (s * EK + 2 * pair + 2))
                        if not (is_first(k) and s < 2):
                            dve.wait_ge(g_read, k * (2 * DS) + (2 * s - 3 + pair))
                        V.tensor_tensor(G[:, s % 2, es, :], H[:, es, :], BC[:, s % NBC, 1:2, :].to_broadcast([P, 2, CT]), ALU.mult).then_inc(g_ok, 1)
                    V.tensor_tensor(ST[:, s, :].bitcast(U32), H[:, :, CT - 1].bitcast(U32),
                                    mask[:, bass.ds(k + 1, 1)].to_broadcast([P, EK]), ALU.bitwise_and).then_inc(kept, 1)
                    items(ON_DVE, s, k, par, has_front, has_back, front, back)

            run(dve, turn, front, back)


def build(nc, x, gate, gate_b, b1, b2, w1, w2, mamba_w, mamba_c, out):
    ctx = ExitStack()
    with ctx:
        keep = buf_maker(nc, ctx, "keep")
        X = keep("X", [P, TT, D])
        C = {
            "whole": ctx, "sems": {},
            "ident": keep("ident", [P, P]), "upper": keep("upper", [P, P], BF16), "onesb": keep("onesb", [P, P], BF16),
            "gate": keep("gate", [P, DK, EXPERTS]), "gb": keep("gb", [P, EXPERTS]), "rank": keep("rank", [P, EXPERTS]),
            "region": keep("region", [P, EXPERTS]), "b1": keep("b1", [P, EXPERTS * FK]),
        }
        R = {"w": keep("w", [P, TOPK, TT]), "idx": keep("idx", [P, TOPK, TT], U32), "rows": keep("rows", [P, EXPERTS], U32)}
        PS = ctx.enter_context(nc.psum_tensor("PS", [P, 8, 512], FP32))
        xrows = nc.dram_tensor("xrows", (ROWS, D), FP32, kind="Internal").ap()
        yrows = nc.dram_tensor("yrows", (ROWS, D), FP32, kind="Internal").ap()
        setup(nc, C, gate, gate_b, b1)
        route(nc, "r0", X, C, PS, R, xrows, x, True)
        experts(nc, "e0", C, PS, R, xrows, yrows, w1, w2, b2)
        combine(nc, "c0", C, X, R, yrows, None)
        bc_dram = nc.dram_tensor("bc_rows", (MCH, 2, DS, CT), FP32, kind="Internal").ap()
        mamba(nc, X, C, PS, mamba_w, mamba_c, bc_dram)
        clear(nc, C, ("r", "e", "c"))
        route(nc, "r1", X, C, PS, R, xrows, None, False)
        experts(nc, "e1", C, PS, R, xrows, yrows, w1, w2, b2)
        combine(nc, "c1", C, X, R, yrows, out)


def clear(nc, C, tags):
    numbers = sorted(h.num for name, h in C["sems"].items() if name.split("_")[0] in tags)
    with nc.Block() as block:
        @block.gpsimd
        def _(gp):
            start = 0
            for n in range(1, len(numbers) + 1):
                if n == len(numbers) or numbers[n] != numbers[n - 1] + 1:
                    gp.sem_clear(range(numbers[start], numbers[n - 1] + 1))
                    start = n


def setup(nc, C, gate, gate_b, b1):
    ctx = ExitStack()
    with ctx:
        sem = sem_maker(nc, C, "s")
        loaded, made = sem("loaded"), sem("made")
        ints = ctx.enter_context(nc.sbuf_tensor("ints", [P, 2, EXPERTS], mybir.dt.int32))
        block = ctx.enter_context(nc.Block())

        @block.sync
        def _(sp):
            sp.dma_start(C["gate"][:, :, :], gate).then_inc(loaded, 16)
            sp.dma_start(C["gb"][:, :], gate_b.to_broadcast([P, EXPERTS])).then_inc(loaded, 16)
            sp.dma_start(C["b1"][:, :], b1).then_inc(loaded, 16)
            sp.wait_ge(loaded, 48)

        @block.gpsimd
        def _(gp):
            G = nc.gpsimd
            G.memset(C["ident"][:, :], 0.0)
            G.memset(C["upper"][:, :], 1.0)
            G.memset(C["onesb"][:, :], 1.0)
            G.iota(ints[:, 0, :], pattern=[[-1, EXPERTS]], base=EXPERTS, channel_multiplier=0)
            G.iota(ints[:, 1, :], pattern=[[ROWS_E, EXPERTS]], base=0, channel_multiplier=0).then_inc(made, 1)
            gp.wait_ge(made, 1)
            G.affine_select(out=C["ident"][:, :], in_=C["ident"][:, :], compare_op=ALU.not_equal, fill=1.0,
                            base=0, pattern=[[-1, P]], channel_multiplier=1)
            G.affine_select(out=C["upper"][:, :], in_=C["upper"][:, :], compare_op=ALU.is_ge, fill=0.0,
                            base=0, pattern=[[1, P]], channel_multiplier=-1)
            G.tensor_copy(C["rank"][:, :], ints[:, 0, :])
            G.tensor_copy(C["region"][:, :], ints[:, 1, :]).then_inc(made, 1)


def kernel(**inputs):
    import numpy as np
    import concourse.bacc as bacc
    from concourse import mybir as _mybir
    from concourse.bass_utils import run_bass_kernel_spmd as run

    def g(name):
        return np.asarray(inputs[name])

    def tiles(a):
        return np.ascontiguousarray(a.reshape(-1, P, a.shape[1]).transpose(1, 0, 2))

    def block_of(a):
        t = tiles(a)
        return t.reshape(P, -1)

    dt_w = np.zeros((P, DI), np.float32)
    dt_w[:DR] = g("L0_attn_dt_proj_w").T
    arrays = {
        "x": g("L0_attn_x").reshape(TOKENS, D),
        "gate": tiles(g("L0_ffn_gate_w").T),
        "gate_b": g("L0_ffn_gate_b").reshape(1, EXPERTS),
        "b1": g("L0_ffn_b1").reshape(EXPERTS * FK, P).T,
        "b2": g("L0_ffn_b2").reshape(1, EXPERTS * D),
        "w1": g("L0_ffn_W1"),
        "w2": g("L0_ffn_W2"),
        "mamba_w": np.concatenate([
            block_of(g("L0_attn_in_proj_w").T), block_of(g("L0_attn_x_proj_w").T), dt_w,
            block_of(g("L0_attn_out_proj_w").T), block_of(g("L0_attn_c_fc_w").T), block_of(g("L0_attn_c_proj_w").T)], axis=1),
        "mamba_c": tiles(np.concatenate([
            g("L0_attn_conv_w"), g("L0_attn_conv_b")[:, None], g("L0_attn_dt_proj_b")[:, None], g("L0_attn_D")[:, None],
            g("L0_attn_A_log")], axis=1)),
    }
    nc = bacc.Bacc("TRN2", target_bir_lowering=False, num_devices=1)
    feed, args = {}, []
    for name, a in arrays.items():
        feed[name] = np.ascontiguousarray(a)
        args.append(nc.dram_tensor(name, a.shape, _mybir.dt.from_np(a.dtype), kind="ExternalInput").ap())
    args.append(nc.dram_tensor("out", (TOKENS, D), _mybir.dt.float32, kind="ExternalOutput").ap())
    build(nc, *args)
    r = run(nc, [feed], core_ids=[0])
    return r.results[0]["out"].reshape(BATCH, TOKENS // BATCH, D)
```

```python
import concourse.bass as bass
from concourse import mybir
from contextlib import ExitStack

FP32 = mybir.dt.float32
FP32R = mybir.dt.float32r
BF16 = mybir.dt.bfloat16
U32 = mybir.dt.uint32
ALU = mybir.AluOpType
ACT = mybir.ActivationFunctionType
AX = mybir.AxisListType

P = 128
TOKENS, D = 4096, 256
BATCH = 2
TT = TOKENS // P
DK = D // P
EXPERTS, FF, TOPK = 8, 1024, 2
CAP = 640
ROWS_E = TOPK * CAP
BLOCKS = EXPERTS * ROWS_E // P
CH = 256
CPE = ROWS_E // CH
CHT = CH // P
NCHUNK = EXPERTS * CPE
FK = FF // P
FP = FK // 2
DROPPED = 20000
LN_EPS = 1e-5
RMS_EPS = 1.1920928955078125e-07

DI, DS, DC, DR = 512, 16, 4, 64
EK = DI // P
CT = 512
CTT = CT // P
MCH = TOKENS // CT
XPR = DR + 2 * DS
W_IN, W_XP = 0, DK * 2 * DI
W_DT = W_XP + EK * XPR
W_OUT = W_DT + DI
W_FC = W_OUT + EK * D
W_PJ = W_FC + DK * 2 * D
W_ALL = W_PJ + EK * D
C_CW, C_CB, C_DB, C_D, C_AL, C_ALL = 0, 4, 5, 6, 7, 7 + DS


def sem_maker(nc, C, tag):
    def get(name, own=False):
        full = f"{tag}_{name}" if own else f"{tag[0]}_{name}"
        if full not in C["sems"]:
            C["sems"][full] = C["whole"].enter_context(nc.semaphore(full))
        return C["sems"][full]

    return get


def buf_maker(nc, ctx, tag):
    return lambda name, shape, dt=FP32: ctx.enter_context(nc.sbuf_tensor(f"{tag}_{name}", shape, dt))


def chain(eng, sem, before=0):
    count = [0]

    def link(instruction):
        count[0] += 1
        instruction.then_inc(sem, 1)
        eng.wait_ge(sem, before + count[0])

    return link


def route(nc, tag, X, C, PS, R, raw, W1, W2, xrows, yrows, x_dram, zero_rows):
    ctx = ExitStack()
    with ctx:
        sem, sb = sem_maker(nc, C, tag), buf_maker(nc, ctx, tag)
        st = sb("stats", [P, TT, 6])
        small = sb("small", [P, 6, TT])
        mean, rstd, dif, mhalf = small[:, 0, :], small[:, 1, :], small[:, 2, :], small[:, 3, :]
        NX = 4
        xn = sb("xn", [P, NX, 4, D])
        xnT = sb("xnT", [P, 2, DK, 4 * P])
        lg = sb("lg", [P, TT, EXPERTS])
        pr = sb("pr", [P, TT, EXPERTS])
        w1 = sb("w1", [P, TT, EXPERTS])
        w2 = sb("w2", [P, TT, EXPERTS])
        red = sb("red", [P, 4, TT])
        oh = sb("oh", [P, TOPK, TT, EXPERTS])
        ohb = sb("ohb", [P, TOPK, TT, EXPERTS], BF16)
        pos = sb("pos", [P, TOPK, TT, EXPERTS])
        tot = sb("tot", [P, TOPK, TT, EXPERTS])
        inc = sb("inc", [P, TOPK, TT, EXPERTS])
        zcol = sb("zcol", [P, TT])
        base = sb("base", [P, TOPK, EXPERTS])
        kept = sb("kept", [P, TOPK, EXPERTS])
        slot = sb("slot", [P, TOPK, TT])
        count_i = sb("count_i", [P, P], mybir.dt.int32)
        number_i = sb("number_i", [P, TOPK, TT], mybir.dt.int32)
        part_i = sb("part_i", [P, 1], mybir.dt.int32)
        count = sb("count", [P, P])
        count_b = sb("count_b", [P, P], BF16)
        tile_no = sb("tile_no", [P, TOPK, TT])
        part_no = sb("part_no", [P, 1])
        slot_u = sb("slot_u", [P, TOPK, TT], U32)
        low_u = sb("low_u", [P, TOPK, TT], U32)
        low = sb("low", [P, TOPK, TT])
        high = sb("high", [P, TOPK, TT])
        masks = sb("masks", [P, 2, TOPK * TT], mybir.dt.int32)
        GT, NH = 4, 4
        inlow = sb("inlow", [P, NH, GT, TOPK, P], BF16)
        hot = sb("hot", [P, NH, TOPK, GT, BLOCKS])
        inblock = sb("inblock", [P, NH, TOPK, GT, 2, BLOCKS], BF16)
        tab = sb("tab", [P, 3, BLOCKS])
        zrow = sb("zrow", [P, 2048])

        x_in, x_ready, stat_ok = [sem(f"x_in{q}") for q in range(4)], sem("x_ready"), sem("stat_ok")
        zero_set, zeroed = sem("zero_set"), sem("zeroed")
        dch, var_ok, rstd_ok = sem("dch"), sem("var_ok"), sem("rstd_ok")
        xn_ok, tp_ok, xnT_ok, lgp_ok, lg_ok = sem("xn_ok"), sem("tp_ok"), sem("xnT_ok"), sem("lgp_ok"), sem("lg_ok")
        sh_ok, ex_ok, ohb_ok, cum_ok = sem("sh_ok"), sem("ex_ok"), sem("ohb_ok"), sem("cum_ok")
        xn_out, xn_free = [sem(f"xn_out{g}") for g in range(NX)], sem("xn_free")
        counted, place_ok, block_ok = sem("counted"), sem("place_ok"), sem("block_ok")
        apart_ok, abs_ok = sem("apart_ok"), sem("abs_ok")
        hot_ok, hot_used, tab_ok = sem("hot_ok"), sem("hot_used"), sem("tab_ok")
        XN0, HU0 = NX, NH
        TP0, LG0 = NX, 2
        block = ctx.enter_context(nc.Block())
        QUARTERS, HALVES = 4, 2
        Q = TT // QUARTERS

        @block.sync
        def _(sp):
            if x_dram is not None:
                for q in range(4):
                    sp.dma_start(X[:, q * Q:(q + 1) * Q, :],
                                 x_dram[q * Q * P:(q + 1) * Q * P, :].rearrange("(t p) d -> p t d", p=P)).then_inc(x_in[q], 16)
            def store(h):
                for g in range(NX):
                    sp.wait_ge(xn_ok, h * NX + (g + 1))
                    sp.dma_start(xrows[bass.ds(h * (NX * 4 * P) + g * 4 * P, 4 * P), :].rearrange("(t p) d -> p t d", p=P),
                                 xn[:, g, :, :]).then_inc(xn_out[g], 16)

            for h in range(HALVES):
                for q in (2 * h, 2 * h + 1):
                    if x_dram is not None:
                        sp.wait_ge(x_in[q], 16)
                        sp.sem_inc(x_ready, 1)
                if h > 0:
                    for g in range(NX):
                        sp.wait_ge(xn_out[g], h * 16)
                        sp.sem_inc(xn_free, 1)
                store(h)
            for g in range(NX):
                sp.wait_ge(xn_out[g], HALVES * 16)
            for q in range(4):
                load_quarter(sp, W1, W2, raw, 0, q).then_inc(sem_maker(nc, C, "e" + tag[1])(f"wraw{q}"), 16)
            if zero_rows:
                sp.wait_ge(zero_set, 1)
                rows = 8 * P
                for r in range(TOPK * TOKENS // rows):
                    sp.dma_start(yrows[r * rows:(r + 1) * rows, :].rearrange("(p a) d -> p (a d)", p=P),
                                 zrow[:, :]).then_inc(zeroed, 16)
                sp.wait_ge(zeroed, 16 * (TOPK * TOKENS // rows))

        @block.vector
        def _(dve):
            V = nc.vector
            link = chain(dve, dch)
            V.memset(zrow[:, :], 0.0).then_inc(zero_set, 1)
            V.memset(mhalf, -0.5)
            V.memset(zcol[:, :], 1.0)
            V.memset(masks[:, 0, :], P - 1)
            V.memset(masks[:, 1, :], TOKENS - 1)
            dve.sem_inc(xn_free, XN0)
            if x_dram is None:
                dve.sem_inc(x_ready, QUARTERS)
            link(V.memset(red[:, 0, :], 0.0))

            def normed(out, t):
                return V.tensor_scalar(out, X[:, bass.ds(t, 1), :].rearrange("p o d -> p (o d)"),
                                       mean[:, bass.ds(t, 1)], rstd[:, bass.ds(t, 1)], ALU.subtract, ALU.mult)

            def statistics(q):
                dve.wait_ge(x_ready, q + 1)
                for a in range(Q):
                    t = bass.ds(q * Q + a, 1)
                    last = V.bn_stats(st[:, t, :].rearrange("p o s -> p (o s)"), X[:, t, :].rearrange("p o d -> p (o d)"))
                LINKS = 6
                slink = chain(dve, stat_ok, q * LINKS)
                slink(last)
                qs = bass.ds(q * Q, Q)
                m, rs, df, s = mean[:, qs], rstd[:, qs], dif[:, qs], st[:, qs, :]
                V.tensor_tensor(m, s[:, :, 1], s[:, :, 4], ALU.add)
                V.tensor_tensor(df, s[:, :, 1], s[:, :, 4], ALU.subtract)
                slink(V.tensor_tensor(rs, s[:, :, 2], s[:, :, 5], ALU.add))
                slink(V.tensor_scalar(m, m, 0.5, None, ALU.mult))
                slink(V.tensor_tensor(df, df, df, ALU.mult))
                slink(V.tensor_scalar(df, df, 0.25, LN_EPS, ALU.mult, ALU.add))
                slink(V.scalar_tensor_tensor(rs, rs, 1.0 / D, df, ALU.mult, ALU.add))
                dve.sem_inc(var_ok, 1)

            def norm(h, quarter):
                dve.wait_ge(rstd_ok, h * 2 + (quarter + 1))
                for g in (2 * quarter, 2 * quarter + 1):
                    dve.wait_ge(xn_free, h * NX + (g + 1))
                    dve.wait_ge(tp_ok, h * NX + (g + 1))
                    for a in range(4):
                        last = normed(xn[:, g, a, :], h * (2 * Q) + (g * 4 + a))
                    last.then_inc(xn_ok, 1)

            with dve.Fori(0, HALVES, 1) as h:
                statistics(h * 2)
                statistics(h * 2 + 1)
                norm(h, 0)
                norm(h, 1)
            dve.wait_ge(lg_ok, TT // 4 + LG0)
            link(V.tensor_tensor(lg[:, :, :], lg[:, :, :], C["gb"][:, :].unsqueeze(1).to_broadcast([P, TT, EXPERTS]), ALU.add))
            bc = lambda a: a.unsqueeze(2).to_broadcast([P, TT, EXPERTS])
            link(V.tensor_reduce(red[:, 0, :], lg[:, :, :], AX.X, ALU.max))
            V.tensor_tensor(lg[:, :, :], lg[:, :, :], bc(red[:, 0, :]), ALU.subtract).then_inc(sh_ok, 1)
            dve.wait_ge(ex_ok, 1)
            link(V.tensor_reduce(red[:, 1, :], lg[:, :, :], AX.X, ALU.add))
            link(V.reciprocal(red[:, 1, :], red[:, 1, :]))
            link(V.tensor_tensor(pr[:, :, :], lg[:, :, :], bc(red[:, 1, :]), ALU.mult))
            rank = C["rank"][:, :].unsqueeze(1).to_broadcast([P, TT, EXPERTS])
            for c in range(TOPK):
                wc = R["w"][:, c, :]
                link(V.tensor_reduce(wc, pr[:, :, :], AX.X, ALU.max))
                link(V.tensor_tensor(w1[:, :, :], pr[:, :, :], bc(wc), ALU.is_equal))
                link(V.tensor_tensor(w1[:, :, :], w1[:, :, :], rank, ALU.mult))
                link(V.tensor_reduce(red[:, 2, :], w1[:, :, :], AX.X, ALU.max))
                link(V.tensor_tensor(oh[:, c, :, :], w1[:, :, :], bc(red[:, 2, :]), ALU.is_equal))
                if c == 0:
                    link(V.scalar_tensor_tensor(pr[:, :, :], oh[:, 0, :, :], -2.0, pr[:, :, :], ALU.mult, ALU.add))
            V.tensor_copy(ohb[:, :, :, :], oh[:, :, :, :]).then_inc(ohb_ok, 1)
            dve.wait_ge(cum_ok, 1)
            f = lambda a: a[:, :, :, :].rearrange("p c t e -> p (c t e)")
            link(V.tensor_copy(f(tot), PS[:, 1, :]))
            for c in range(TOPK):
                for e in range(EXPERTS):
                    last = V.tensor_tensor_scan(inc[:, c, :, e], zcol[:, :], tot[:, c, :, e], 0.0, ALU.mult, ALU.add)
            link(last)
            link(V.tensor_tensor(f(pos), PS[:, 0, :], f(inc), ALU.add))
            link(V.scalar_tensor_tensor(f(pos), f(pos), -1.0, f(tot), ALU.add, ALU.subtract))
            link(V.scalar_tensor_tensor(f(oh), f(pos), float(CAP), f(oh), ALU.is_lt, ALU.mult))
            link(V.tensor_scalar(kept[:, :, :], inc[:, :, TT - 1, :], float(CAP), None, ALU.min))
            link(V.tensor_tensor(kept[:, 0, :], kept[:, 0, :], kept[:, 1, :], ALU.add))
            V.tensor_copy(R["rows"][:, :], kept[:, 0, :])
            link(V.tensor_scalar(base[:, 0, :], C["region"][:, :], -float(DROPPED), None, ALU.add))
            link(V.tensor_scalar(base[:, 1, :], inc[:, 0, TT - 1, :], float(CAP), -float(DROPPED), ALU.min, ALU.add))
            link(V.tensor_tensor(base[:, 1, :], base[:, 1, :], C["region"][:, :], ALU.add))
            for c in range(TOPK):
                link(V.tensor_tensor(w1[:, :, :], pos[:, c, :, :],
                                     base[:, c, :].unsqueeze(1).to_broadcast([P, TT, EXPERTS]), ALU.add))
                link(V.tensor_tensor(w1[:, :, :], w1[:, :, :], oh[:, c, :, :], ALU.mult))
                link(V.tensor_reduce(slot[:, c, :], w1[:, :, :], AX.X, ALU.add))
                V.tensor_reduce(red[:, 2 + c, :], oh[:, c, :, :], AX.X, ALU.add)
            link(V.tensor_scalar(slot[:, :, :], slot[:, :, :], float(DROPPED), None, ALU.add))
            V.scalar_tensor_tensor(R["w"][:, :, :], R["w"][:, :, :], 0.5, red[:, 2:4, :], ALU.mult, ALU.mult)
            link(V.tensor_copy(slot_u[:, :, :], slot[:, :, :]))
            flat = lambda a: a[:, :, :].rearrange("p c t -> p (c t)")
            link(V.tensor_tensor(flat(low_u), flat(slot_u), masks[:, 0, :].bitcast(U32), ALU.bitwise_and))
            link(V.tensor_copy(low[:, :, :], low_u[:, :, :]))
            link(V.tensor_tensor(high[:, :, :], slot[:, :, :], low[:, :, :], ALU.subtract))
            link(V.tensor_scalar(high[:, :, :], high[:, :, :], 1.0 / P, None, ALU.mult))
            dve.sem_inc(place_ok, 1)
            dve.wait_ge(counted, 2)
            with dve.Fori(0, TT // (NH * GT), 1) as i:
                for g in range(NH):
                    dve.wait_ge(hot_used, i * NH + (g + 1))
                    for a in range(GT):
                        for c in range(TOPK):
                            t = bass.ds(i * (NH * GT) + (g * GT + a), 1)
                            last = V.tensor_scalar(inlow[:, g, a, c, :], count_b[:, :], low[:, c, t], None, ALU.is_equal)
                    dve.wait_ge(abs_ok, i * (2 * NH) + (2 * g + 2))
                    for c in range(TOPK):
                        no = tile_no[:, c, bass.ds(i * (NH * GT) + g * GT, GT)]
                        last = V.tensor_tensor(inblock[:, g, c, :, 0, :], hot[:, g, c, :, :],
                                               no.unsqueeze(2).to_broadcast([P, GT, BLOCKS]), ALU.mult)
                    last.then_inc(hot_ok, 1)
            dve.wait_ge(tab_ok, 1)
            link(V.tensor_copy(tab[:, 2, :], PS[:, 2, BLOCKS:2 * BLOCKS]))
            link(V.scalar_tensor_tensor(tab[:, 2, :], PS[:, 2, 0:BLOCKS], float(P), tab[:, 2, :], ALU.mult, ALU.add))
            link(V.tensor_scalar(tab[:, 0, :], PS[:, 2, 0:BLOCKS], 0.0, float(DROPPED), ALU.is_equal, ALU.mult))
            link(V.scalar_tensor_tensor(tab[:, 1, :], tab[:, 2, :], -float(P), tab[:, 0, :], ALU.add, ALU.add))
            link(V.tensor_copy(R["dest"][:, :], tab[:, 1, :]))
            both = masks[:, 1, 0:1].bitcast(U32).to_broadcast([P, BLOCKS])
            V.tensor_tensor(R["token"][:, :], R["dest"][:, :], both, ALU.bitwise_and)

        @block.gpsimd
        def _(gp):
            G = nc.gpsimd
            G.iota(count_i[:, :], pattern=[[1, P]], base=0, channel_multiplier=0)
            G.iota(part_i[:, :], pattern=[[0, 1]], base=0, channel_multiplier=1)
            G.iota(number_i[:, :, :], pattern=[[TT, TOPK], [1, TT]], base=1, channel_multiplier=0).then_inc(counted, 1)
            gp.wait_ge(counted, 1)
            G.tensor_copy(count[:, :], count_i[:, :])
            G.tensor_copy(count_b[:, :], count_i[:, :])
            G.tensor_copy(part_no[:, :], part_i[:, :])
            G.tensor_copy(tile_no[:, :, :], number_i[:, :, :]).then_inc(counted, 1)
            with gp.Fori(0, QUARTERS, 1) as q:
                gp.wait_ge(var_ok, q + 1)
                rs = rstd[:, bass.ds(q * Q, Q)]
                G.tensor_tensor(rs, rs, mhalf[:, 0:Q], ALU.pow).then_inc(rstd_ok, 1)
            gp.wait_ge(place_ok, 1)
            with gp.Fori(0, TT // (NH * GT), 1) as i:
                for g in range(NH):
                    gp.wait_ge(hot_used, i * NH + (g + 1))
                    for c in range(TOPK):
                        t = bass.ds(i * (NH * GT) + g * GT, GT)
                        last = G.tensor_tensor(hot[:, g, c, :, :], count[:, 0:BLOCKS].unsqueeze(1).to_broadcast([P, GT, BLOCKS]),
                                               high[:, c, t].unsqueeze(2).to_broadcast([P, GT, BLOCKS]), ALU.subtract)
                    last.then_inc(apart_ok, 1)

        @block.scalar
        def _(act):
            with act.Fori(0, HALVES, 1) as h:
                for pair in range(0, NX, 2):
                    for g in range(2):
                        act.wait_ge(tp_ok, h * NX + (pair + g + 1 + TP0))
                        nc.scalar.activation(xnT[:, g, :, :], PS[:, 2 * g:2 * g + 2, :], ACT.Copy).then_inc(xnT_ok, 1)
                    for g in range(2):
                        act.wait_ge(lgp_ok, h * NX + (pair + g + 1))
                        nc.scalar.activation(lg[:, bass.ds(h * (NX * 4) + (pair + g) * 4, 4), :],
                                             PS[:, 4 + g, 0:4 * EXPERTS].rearrange("p (t e) -> p t e", e=EXPERTS),
                                             ACT.Copy).then_inc(lg_ok, 1)
            act.wait_ge(sh_ok, 1)
            nc.scalar.activation(lg[:, :, :], lg[:, :, :], ACT.Exp).then_inc(ex_ok, 1)
            with act.Fori(0, TT // (NH * GT), 1) as i:
                for g in range(NH):
                    act.wait_ge(apart_ok, i * NH + (g + 1))
                    one = hot[:, g, :, :, :].rearrange("p c a s -> p (c a) s")
                    nc.scalar.activation(one, one, ACT.Abs).then_inc(abs_ok, 1)
                    act.wait_ge(abs_ok, i * (2 * NH) + (2 * g + 1))
                    nc.scalar.activation(one, one, ACT.Relu, scale=-1.0, bias=1.0).then_inc(abs_ok, 1)
                    act.wait_ge(abs_ok, i * (2 * NH) + (2 * g + 2))
                    nc.scalar.activation(inblock[:, g, :, :, 1, :].rearrange("p c a s -> p (c a) s"), one, ACT.Copy,
                                         scale=part_no[:, :]).then_inc(block_ok, 1)

        @block.tensor
        def _(pe):
            pe.sem_inc(tp_ok, TP0)
            pe.sem_inc(lg_ok, LG0)
            with pe.Fori(0, HALVES, 1) as h:
                for pair in range(0, NX, 2):
                    for g in range(2):
                        pe.wait_ge(xn_ok, h * NX + (pair + g + 1))
                        for k in range(DK):
                            for a in range(4):
                                last = nc.tensor.transpose(PS[:, 2 * g + k, a * P:(a + 1) * P],
                                                           xn[:, pair + g, a, k * P:(k + 1) * P], C["ident"][:, :])
                        last.then_inc(tp_ok, 1)
                    for g in range(2):
                        pe.wait_ge(xnT_ok, h * NX + (pair + g + 1))
                        pe.wait_ge(lg_ok, h * NX + (pair + g + 1))
                        for a in range(4):
                            for k in range(DK):
                                last = nc.tensor.matmul(PS[:, 4 + g, a * EXPERTS:(a + 1) * EXPERTS],
                                                        xnT[:, g, k, a * P:(a + 1) * P], C["gate"][:, k, :],
                                                        start=(k == 0), stop=(k == DK - 1))
                        last.then_inc(lgp_ok, 1)
            pe.wait_ge(ohb_ok, 1)
            ohf = ohb[:, :, :, :].rearrange("p c t e -> p (c t e)")
            nc.tensor.matmul(PS[:, 0, :], C["upper"][:, :], ohf, start=True, stop=True)
            nc.tensor.matmul(PS[:, 1, :], C["onesb"][:, :], ohf, start=True, stop=True).then_inc(cum_ok, 1)
            pe.sem_inc(hot_used, HU0)
            both = PS[:, 2, 0:2 * BLOCKS]
            edge = lambda **flags: nc.tensor.matmul(both, zrow[:, 0:P], zrow[:, 0:2 * BLOCKS], **flags)
            edge(start=True, stop=False)
            with pe.Fori(0, TT // (NH * GT), 1) as i:
                for g in range(NH):
                    pe.wait_ge(hot_ok, i * NH + (g + 1))
                    pe.wait_ge(block_ok, i * NH + (g + 1))
                    for a in range(GT):
                        for c in range(TOPK):
                            last = nc.tensor.matmul(both, inlow[:, g, a, c, :], inblock[:, g, c, a, :, :].rearrange("p n s -> p (n s)"),
                                                    start=False, stop=False)
                    last.then_inc(hot_used, 1)
            edge(start=False, stop=True).then_inc(tab_ok, 1)


def load_quarter(sp, W1, W2, raw, e, q):
    if q < 2:
        return sp.dma_start(raw[:, q, :], W1[bass.ds(e, 1), q * P:(q + 1) * P, :].rearrange("o p f -> p (o f)"))
    src = W2[bass.ds(e, 1), (q - 2) * 4 * P:(q - 1) * 4 * P, :].rearrange("o (j p) d -> p (o j) d", p=P)
    return sp.dma_start(raw[:, q, :].rearrange("p (j d) -> p j d", d=D), src)


def experts(nc, tag, C, PS, R, raw, xrows, yrows, W1, W2, b2):
    ctx = ExitStack()
    with ctx:
        sem, sb = sem_maker(nc, C, tag), buf_maker(nc, ctx, tag)
        wh = sb("wh", [P, 2, 4, FF], FP32R)
        wl = sb("wl", [P, 2, 4, FF], FP32R)
        xin = sb("xin", [P, 2, CHT, D])
        xh = sb("xh", [P, 2, DK, CH], FP32R)
        xl = sb("xl", [P, 2, DK, CH], FP32R)
        u = sb("u", [P, FP, 2, CH])
        hh = sb("hh", [P, 2, FK, CH], FP32R)
        hl = sb("hl", [P, 2, FK, CH], FP32R)
        ysb = sb("ysb", [P, 2, CHT, D])
        gix = sb("gix", [P, 2, CHT], U32)
        six = sb("six", [P, 2, CHT], U32)
        b2_all = sb("b2", [P, EXPERTS, D])
        b2_in = sem("b2_in")
        wraw = [sem(f"wraw{q}") for q in range(4)]
        wh_ok, wl_ok = sem("wh_ok"), sem("wl_ok")
        xin_ok = [sem(f"xin{b}", own=True) for b in range(2)]
        gx_ok, sx_ok, carried = sem("gx_ok"), sem("sx_ok"), sem("carried")
        xT_ok, xh_ok, xl_ok = sem("xT_ok"), sem("xh_ok"), sem("xl_ok")
        s1_ok, u_ok, hh_ok, hl_ok = sem("s1_ok"), sem("u_ok"), sem("hh_ok"), sem("hl_ok")
        y_ok, yb_ok, passed = sem("y_ok"), sem("yb_ok"), sem("passed")
        stored, ysb_free = [sem(f"stored{b}", own=True) for b in range(2)], sem("ysb_free")
        block = ctx.enter_context(nc.Block())
        B_XT, B_S1, B_Y = 0, 1, 5
        TURN = 2 * CPE
        Y0, YB0, YF0 = 1, 2, 2

        def chunks(eng, step):
            with eng.Fori(0, EXPERTS // 2 - 1, 1) as i:
                for c in range(TURN):
                    step(i, c, False)
            for c in range(TURN):
                step(EXPERTS // 2 - 1, c, True)

        def rows_of(eng, i, e2):
            return eng.value_load(R["rows"][0:1, bass.ds(i * 2 + e2, 1)], min_val=0, max_val=ROWS_E)

        def if_taken(eng, rows, c, work, signal):
            j = c % CPE
            if j < 2:
                return work()
            eng.sem_inc(passed, 1)
            with eng.If(rows > j * CH):
                work()
            with eng.Else():
                for s, so_far, n in signal:
                    eng.wait_ge(s, so_far)
                    eng.sem_inc(s, n)

        @block.sync
        def _(sp):
            def load_w(e, q):
                load_quarter(sp, W1, W2, raw, e, q).then_inc(wraw[q], 16)

            sp.dma_start(b2_all[:, :, :].rearrange("p e d -> p (e d)"), b2.to_broadcast([P, EXPERTS * D])).then_inc(b2_in, 16)

            def step(i, c, last):
                e2, j = divmod(c, CPE)
                if j < 4 and not (last and e2 == 1):
                    sp.wait_ge(wl_ok, i * 8 + (4 * e2 + j + 1))
                    load_w(i * 2 + (e2 + 1), j)

            chunks(sp, step)

        @block.gpsimd
        def _(gp):
            G = nc.gpsimd
            last_token, last_dest = gp.to_reg(TOKENS - 1), gp.to_reg(TOPK * TOKENS - 1)

            def indices(i, c, buffer, table, done):
                G.tensor_copy(buffer[:, c % 2, :], R[table][:, bass.ds(i * (TURN * CHT) + c * CHT, CHT)]).then_inc(done, 1)
                gp.wait_ge(done, i * TURN + (c + 1))
                gp.sem_inc(carried, 1)

            def gather(i, c):
                indices(i, c, gix, "token", gx_ok)
                for t in range(CHT):
                    G.indirect_dma_start(out=xin[:, c % 2, t, :], out_offset=None, in_=xrows,
                                         in_offset=bass.IndirectOffsetOnAxis(ap=gix[:, c % 2, t:t + 1], axis=0),
                                         bounds_check=last_token, oob_is_err=False).then_inc(xin_ok[c % 2], 16)

            def scatter(i, c):
                indices(i, c, six, "dest", sx_ok)
                for t in range(CHT):
                    G.indirect_dma_start(out=yrows, out_offset=bass.IndirectOffsetOnAxis(ap=six[:, c % 2, t:t + 1], axis=0),
                                         in_=ysb[:, c % 2, t, :], in_offset=None, bounds_check=last_dest,
                                         oob_is_err=False).then_inc(stored[c % 2], 16)

            def step(i, c, first=False, last=False):
                if not (last and c + 3 >= TURN):
                    gp.wait_ge(xT_ok, i * TURN + (c + 2))
                    gather(i, c + 3)
                if not first:
                    gp.wait_ge(stored[(c - 1) % 2], i * (16 * CHT * CPE) + 16 * CHT * ((c - 1) // 2 + 1))
                    gp.sem_inc(ysb_free, 1)
                gp.wait_ge(yb_ok, i * TURN + (c + 1 + YB0))
                scatter(i, c)

            gather(0, 0)
            gather(0, 1)
            gp.wait_ge(xT_ok, 1)
            gather(0, 2)
            step(0, 0, first=True)
            with gp.Fori(0, EXPERTS // 2 - 1, 1) as i:
                for c in range(1, TURN + 1):
                    step(i, c)
            for c in range(1, TURN):
                step(EXPERTS // 2 - 1, c, last=True)
            gp.wait_ge(stored[(NCHUNK - 1) % 2], 16 * CHT * (NCHUNK // 2))

        @block.tensor
        def _(pe):
            M = nc.tensor.matmul
            pe.sem_inc(y_ok, Y0)

            def turn(i, c, first=False):
                pe.wait_ge(xin_ok[c % 2], i * (16 * CHT * CPE) + 16 * CHT * (c // 2 + 1))
                if not first:
                    pe.wait_ge(xl_ok, i * TURN + c)
                for k in range(DK):
                    for t in range(CHT):
                        last = nc.tensor.transpose(PS[:, B_XT, k * CH + t * P:k * CH + (t + 1) * P],
                                                   xin[:, c % 2, t, k * P:(k + 1) * P], C["ident"][:, :])
                last.then_inc(xT_ok, 1)

            rows = [None]

            def up(i, c, first=False):
                e2, j = divmod(c, CPE)
                w = e2 % 2
                if j == 0:
                    pe.wait_ge(wl_ok, i * 8 + (4 * e2 + 2))
                pe.wait_ge(xl_ok, i * TURN + (c + 1))
                if_taken(pe, rows[0], c, lambda: up_products(i, c, w, first), [(s1_ok, i * (TURN * FP) + c * FP, FP)])

            def up_products(i, c, w, first):
                for pair in range(FP):
                    if not first:
                        pe.wait_ge(u_ok, i * (TURN * FP) + ((c - 1) * FP + pair + 1))
                    for m in range(2):
                        f = slice((2 * pair + m) * P, (2 * pair + m + 1) * P)
                        terms = [(wx[:, w, k, f], rx[:, c % 2, k, :]) for k in range(DK)
                                 for wx, rx in ((wh, xh), (wh, xl), (wl, xh))]
                        for n, (a, r) in enumerate(terms):
                            last = M(PS[:, B_S1 + pair, m * CH:(m + 1) * CH], a, r, start=(n == 0), stop=(n == len(terms) - 1))
                    last.then_inc(s1_ok, 1)

            def down(i, c):
                e2, j = divmod(c, CPE)
                w = e2 % 2
                if j == 0:
                    pe.wait_ge(wl_ok, i * 8 + (4 * e2 + 4))
                pe.wait_ge(hl_ok, i * (TURN * FP) + (c + 1) * FP)
                pe.wait_ge(yb_ok, i * TURN + (c - 1 + YB0))
                if_taken(pe, rows[0], c, lambda: down_products(c, w), [(y_ok, i * TURN + (c + Y0), 1)])

            def down_products(c, w):
                for t in range(CHT):
                    ts = slice(t * P, (t + 1) * P)
                    terms = [(hx[:, c % 2, f, ts], wx[:, w, 2 + f // 4, (f % 4) * D:(f % 4 + 1) * D])
                             for f in range(FK) for hx, wx in ((hh, wh), (hl, wh), (hh, wl))]
                    for n, (a, r) in enumerate(terms):
                        last = M(PS[:, B_Y + c % 2, t * D:(t + 1) * D], a, r, start=(n == 0), stop=(n == len(terms) - 1))
                last.then_inc(y_ok, 1)

            turn(0, 0, first=True)
            turn(0, 1)
            up(0, 0, first=True)

            def step(i, c, last):
                if c % CPE == 0:
                    rows[0] = rows_of(pe, i, c // CPE)
                if not (last and c + 2 >= TURN):
                    turn(*((i, c + 2) if c + 2 < TURN else (i + 1, c + 2 - TURN)))
                if not (last and c + 1 >= TURN):
                    up(*((i, c + 1) if c + 1 < TURN else (i + 1, c + 1 - TURN)))
                down(i, c)

            chunks(pe, step)

        @block.scalar
        def _(act):
            A = nc.scalar.activation

            def split_w(e2, i, q):
                act.wait_ge(wraw[q], i * 32 + 16 * (e2 + 1))
                A(wh[:, e2 % 2, q, :], raw[:, q, :], ACT.Copy).then_inc(wh_ok, 1)

            def rows(i, c):
                act.wait_ge(xT_ok, i * TURN + (c + 1))
                A(xh[:, c % 2, :, :].rearrange("p k c -> p (k c)"), PS[:, B_XT, :], ACT.Copy).then_inc(xh_ok, 1)

            taken = [None]

            def hidden(i, c):
                if_taken(act, taken[0], c, lambda: high(i, c), [(hh_ok, i * (TURN * FP) + c * FP, FP)])

            def high(i, c):
                for pair in range(FP):
                    act.wait_ge(u_ok, i * (TURN * FP) + (c * FP + pair + 1))
                    A(hh[:, c % 2, 2 * pair:2 * pair + 2, :], u[:, pair, :, :], ACT.Relu).then_inc(hh_ok, 1)

            for q in range(4):
                split_w(0, 0, q)
            rows(0, 0)
            rows(0, 1)
            hidden(0, 0)

            def step(i, c, last):
                e2, j = divmod(c, CPE)
                if j == 0:
                    taken[0] = rows_of(act, i, e2)
                if not (last and c + 2 >= TURN):
                    act.wait_ge(s1_ok, i * (TURN * FP) + (c + 1) * FP)
                    rows(*((i, c + 2) if c + 2 < TURN else (i + 1, c + 2 - TURN)))
                act.wait_ge(y_ok, i * TURN + (c + Y0))
                if not (last and c + 1 >= TURN):
                    hidden(*((i, c + 1) if c + 1 < TURN else (i + 1, c + 1 - TURN)))
                if j >= 1 and not (last and e2 == 1):
                    split_w(*((1, i) if e2 == 0 else (0, i + 1)), j - 1)

            chunks(act, step)

        @block.vector
        def _(dve):
            V = nc.vector
            dve.sem_inc(yb_ok, YB0)
            dve.sem_inc(ysb_free, YF0)

            def split_w(e2, i, q):
                dve.wait_ge(wh_ok, i * 8 + (4 * e2 + q + 1))
                V.tensor_tensor(wl[:, e2 % 2, q, :], raw[:, q, :], wh[:, e2 % 2, q, :].bitcast(FP32), ALU.subtract).then_inc(wl_ok, 1)

            def rows(i, c):
                dve.wait_ge(xh_ok, i * TURN + (c + 1))
                V.tensor_tensor(xl[:, c % 2, :, :].rearrange("p k c -> p (k c)"), PS[:, B_XT, :],
                                xh[:, c % 2, :, :].rearrange("p k c -> p (k c)").bitcast(FP32), ALU.subtract).then_inc(xl_ok, 1)

            taken = [None]

            def hidden(i, c):
                if_taken(dve, taken[0], c, lambda: bias_and_low(i, c),
                         [(u_ok, i * (TURN * FP) + c * FP, FP), (hl_ok, i * (TURN * FP) + c * FP, FP)])

            def bias_and_low(i, c):
                e2 = c // CPE

                def bias(pair):
                    dve.wait_ge(s1_ok, i * (TURN * FP) + (c * FP + pair + 1))
                    b1 = C["b1"][:, bass.ds(i * (2 * FK) + (e2 * FK + 2 * pair), 2)]
                    V.tensor_tensor(u[:, pair, :, :], PS[:, B_S1 + pair, :].rearrange("p (m c) -> p m c", m=2),
                                    b1.unsqueeze(2).to_broadcast([P, 2, CH]), ALU.add).then_inc(u_ok, 1)

                def low(pair):
                    dve.wait_ge(hh_ok, i * (TURN * FP) + (c * FP + pair + 1))
                    V.scalar_tensor_tensor(hl[:, c % 2, 2 * pair:2 * pair + 2, :], u[:, pair, :, :], 0.0,
                                           hh[:, c % 2, 2 * pair:2 * pair + 2, :].bitcast(FP32), ALU.max, ALU.subtract).then_inc(hl_ok, 1)

                bias(0)
                for pair in range(1, FP):
                    bias(pair)
                    low(pair - 1)
                low(FP - 1)

            def out(i, c):
                e2 = c // CPE
                dve.wait_ge(y_ok, i * TURN + (c + 1 + Y0))
                dve.wait_ge(ysb_free, i * TURN + (c - 1 + YF0))
                b2 = b2_all[:, bass.ds(i * 2 + e2, 1), :].rearrange("p o d -> p (o d)")
                V.tensor_tensor(ysb[:, c % 2, :, :], PS[:, B_Y + c % 2, :].rearrange("p (t d) -> p t d", t=CHT),
                                b2.unsqueeze(1).to_broadcast([P, CHT, D]), ALU.add).then_inc(yb_ok, 1)

            for q in range(4):
                split_w(0, 0, q)
            rows(0, 0)
            rows(0, 1)
            hidden(0, 0)
            dve.wait_ge(b2_in, 16)

            def step(i, c, last):
                e2, j = divmod(c, CPE)
                if j == 0:
                    taken[0] = rows_of(dve, i, e2)
                if not (last and c + 2 >= TURN):
                    dve.wait_ge(s1_ok, i * (TURN * FP) + (c + 1) * FP)
                    rows(*((i, c + 2) if c + 2 < TURN else (i + 1, c + 2 - TURN)))
                dve.wait_ge(y_ok, i * TURN + (c + Y0))
                if not (last and c + 1 >= TURN):
                    hidden(*((i, c + 1) if c + 1 < TURN else (i + 1, c + 1 - TURN)))
                out(i, c)
                if j >= 1 and not (last and e2 == 1):
                    split_w(*((1, i) if e2 == 0 else (0, i + 1)), j - 1)

            chunks(dve, step)


def combine(nc, tag, C, X, R, yrows, out_dram):
    ctx = ExitStack()
    with ctx:
        sem, sb = sem_maker(nc, C, tag), buf_maker(nc, ctx, tag)
        NB, GT = 4, 4
        got = sb("got", [P, NB, TOPK, GT, D])
        landed = [sem(f"landed{b}") for b in range(NB)]
        added, done, stored = sem("added"), sem("done"), sem("stored")
        block = ctx.enter_context(nc.Block())
        GROUPS = TT // GT

        @block.sync
        def _(sp):
            with sp.Fori(0, GROUPS // NB, 1) as i:
                for b in range(NB):
                    sp.wait_ge(added, i * NB + (b + 1))
                    for c in range(TOPK):
                        src = yrows[bass.ds(i * (NB * GT * P) + (b * GT * P + c * TOKENS), GT * P), :]
                        sp.dma_start(got[:, b, c, :, :], src.rearrange("(t p) d -> p t d", p=P)).then_inc(landed[b], 16)

        @block.vector
        def _(dve):
            V = nc.vector
            dve.sem_inc(added, NB)
            with dve.Fori(0, GROUPS // NB, 1) as i:
                for b in range(NB):
                    dve.wait_ge(landed[b], i * (16 * TOPK) + 16 * TOPK)
                    for c in range(TOPK):
                        if c > 0:
                            dve.wait_ge(done, i * NB + (b + 1))
                        for a in range(GT):
                            t = bass.ds(i * (NB * GT) + (b * GT + a), 1)
                            x = X[:, t, :].rearrange("p o d -> p (o d)")
                            last = V.scalar_tensor_tensor(x, got[:, b, c, a, :], R["w"][:, c, t], x, ALU.mult, ALU.add)
                        last.then_inc(done if c == 0 else added, 1)

        @block.scalar
        def _(act):
            for q in range(GROUPS):
                act.wait_ge(added, NB + (q + 1))
                act.dma_start(out_dram[q * GT * P:(q + 1) * GT * P, :].rearrange("(t p) d -> p t d", p=P),
                              X[:, q * GT:(q + 1) * GT, :]).then_inc(stored, 16)
            act.wait_ge(stored, 16 * GROUPS)


def mamba(nc, X, C, PS, R, yrows, mamba_w, mamba_c, bc_dram):
    ctx = ExitStack()
    with ctx:
        sem, sb = sem_maker(nc, C, "m"), buf_maker(nc, ctx, "m")
        MW = sb("MW", [P, W_ALL])
        mc = sb("mc", [P, EK, C_ALL])
        A = sb("A", [P, EK, DS])
        skip = sb("skip", [P, EK, P])
        mask = sb("mask", [P, MCH + 1], U32)
        st = sb("st", [P, 2 * CTT, 6])
        tk = sb("tk", [P, 3, TT])
        mean, rstd, rrms = (tk[:, n, :] for n in range(3))
        var = sb("var", [P, 2, 2 * CTT])
        mhalf = sb("mhalf", [P, 2, 2 * CTT])
        XI = sb("XI", [P, EK, DC - 1 + CT])
        U = sb("U", [P, EK, CT])
        T3 = sb("T3", [P, EK, CT])
        xrT = sb("xrT", [P, DK, CT])
        hT = sb("hT", [P, DK, CT])
        XR = sb("XR", [P, CTT, D])
        XP = sb("XP", [P, CTT, D])
        ssq = sb("ssq", [P, CTT])
        SZ = sb("SZ", [P, 2, EK, CT])
        DT = sb("DT", [P, 2, EK, CT])
        DTU = sb("DTU", [P, 2, EK, CT])
        dA = sb("dA", [P, EK, CT])
        dB = sb("dB", [P, EK, CT])
        H = sb("H", [P, EK, CT])
        G = sb("G", [P, 2, EK, CT])
        ST = sb("ST", [P, DS, EK])
        NBC = 2
        BC = sb("BC", [P, NBC, 2, CT])
        sp1 = sb("sp1", [P, EK, CT])
        XD = sb("XD", [P, CT])

        w_in, mc_in, dch, a_raw, a_ok, diag_ok = (sem(n) for n in ("w_in", "mc_in", "dch", "a_raw", "a_ok", "diag_ok"))
        var_ok, pow_ok, stat_ok, w_in2 = (sem(n) for n in ("var_ok", "pow_ok", "stat_ok", "w_in2"))
        landed, joined, join_ch, stat_ch = [sem(f"landed{b}") for b in range(2)], sem("joined"), sem("join_ch"), sem("stat_ch")
        f_w, f_r = sem("f_w"), sem("f_r")
        k_w, k_r = sem("k_w"), sem("k_r")
        xr_ok, tail_ok, u_ok, sz_ok = sem("xr_ok"), sem("tail_ok"), sem("u_ok"), sem("sz_ok")
        tap0_ok, taps_ok = sem("tap0_ok"), sem("taps_ok")
        sp_exp, sp_ln, dt_ok, dtu_ok = (sem(n) for n in ("sp_exp", "sp_ln", "dt_ok", "dtu_ok"))
        bc_out = sem("bc_out")
        b_in, c_in = ([sem(f"{n}_in{b}") for b in range(NBC)] for n in "bc")
        dA_ok, dB_ok, scanned, g_ok, g_read, kept = (sem(n) for n in ("dA_ok", "dB_ok", "scanned", "g_ok", "g_read", "kept"))
        yz_ok, xn_ok, sq_ok, v_ok, rs_ok, hr_ok, q_ok, xa_ok = (sem(n) for n in (
            "yz_ok", "xn_ok", "sq_ok", "v_ok", "rs_ok", "hr_ok", "q_ok", "xa_ok"))
        block = ctx.enter_context(nc.Block())

        B_F, B_K, B_Y = 0, 2, 4
        F_USE = {use: n for n, use in enumerate(
            [("T", 0), ("T", 1), ("x", 0), ("x", 1), ("x", 2), ("x", 3), ("z", 0), ("z", 1), ("z", 2), ("z", 3),
             ("xp", 0), ("dt", 0), ("dt", 1), ("dt", 2), ("dt", 3)])}
        K_USE = {use: n for n, use in enumerate(
            [("out", 0), ("out", 1), ("T", 0), ("T", 1), ("fc", 0), ("fc", 1), ("fc", 2), ("fc", 3), ("pj", 0), ("pj", 1)])}
        NF, NK = len(F_USE), len(K_USE)
        NTAP = EK * (DC - 1)
        KR0 = 2
        ON_PE, ON_ACT, ON_DVE, ON_POOL = range(4)
        FRONT = {
            "F_xr": (0, 0, -1, 0), "F_T": (0, 0, 0, 0), "F_x01": (1, 1, 1, 1), "F_x23": (1, 2, 1, 1),
            "F_c01": (3, 3, 3, 3), "F_c23": (3, 3, 3, 3), "F_z01": (3, 3, 3, 3), "F_z23": (4, 4, 4, 4),
            "F_silu": (5, 4, 5, 5), "F_xp": (6, 7, 8, 7), "F_dt": (9, 9, 9, 9), "F_du": (11, 11, 11, 11),
        }
        BACK = {
            "K_out0": (2, 3, 4, 3), "K_out1": (5, 5, 5, 5), "K_sq": (6, 6, 5, 6), "K_v": (7, 7, 6, 7),
            "K_hr": (8, 8, 8, 8), "K_T": (10, 9, 10, 11), "K_fc01": (11, 11, 11, 11), "K_fc23": (12, 12, 12, 12),
            "K_pj0": (13, 13, 13, 13), "K_pj1": (15, 15, 15, 15),
        }
        SEND_AT = 9

        def run(eng, turn, front, back):
            for p in FRONT:
                front(p, 0, 0)
            turn(0, 0, True, False)
            with eng.Fori(0, MCH // 2 - 1, 1) as i:
                turn(i * 2 + 1, 1, True, True)
                turn(i * 2 + 2, 0, True, True)
            turn(MCH - 1, 1, False, True)
            for p in ["K_yz"] + list(BACK):
                back(p, MCH - 1, 1)

        def items(engine, s, k, par, has_front, has_back, front, back):
            for p in FRONT:
                if FRONT[p][engine] == s and has_front:
                    front(p, k + 1, 1 - par)
            for p in BACK:
                if BACK[p][engine] == s and has_back:
                    back(p, k - 1, 1 - par)

        def outputs(b):
            return G[:, b, :, :].rearrange("p e (h d) -> p (e h) d", d=D)

        def is_first(k):
            return isinstance(k, int) and k == 0

        def f_bank(use, rows=P):
            return PS[0:rows, B_F + F_USE[use] % 2, :]

        def k_bank(use):
            return PS[:, B_K + K_USE[use] % 2, :]

        def weights(at, width, tile, lo, n):
            return MW[:, at + tile * width + lo:at + tile * width + lo + n]

        @block.sync
        def _(sp):
            def load_outputs(m, b):
                for c in range(TOPK):
                    src = yrows[bass.ds(m * (2 * CT) + (b * CT + c * TOKENS), CT), :]
                    sp.dma_start(outputs(b)[:, c * CTT:(c + 1) * CTT, :], src.rearrange("(t p) d -> p t d", p=P)).then_inc(landed[b], 16)

            load_outputs(0, 0)
            sp.dma_start(MW[:, 0:W_XP], mamba_w[:, 0:W_XP]).then_inc(w_in, 16)
            sp.dma_start(mc[:, :, :], mamba_c).then_inc(mc_in, 16)
            load_outputs(0, 1)
            sp.dma_start(MW[:, W_XP:], mamba_w[:, W_XP:]).then_inc(w_in2, 16)
            with sp.Fori(1, MCH // 2, 1) as m:
                for b in range(2):
                    sp.wait_ge(joined, m * 2 + (b - 1))
                    load_outputs(m, b)

            def load(k, s):
                for j, landed, used in ((0, b_in, dB_ok), (1, c_in, g_ok)):
                    if s >= NBC or not is_first(k):
                        sp.wait_ge(used, k * (2 * DS) + 2 * (s - NBC + 1))
                    src = bc_dram[bass.ds(k, 1), j, s:s + 1, :].rearrange("o q t -> (o q) t")
                    sp.dma_start(BC[:, s % NBC, j, :], src.to_broadcast([P, CT])).then_inc(landed[s % NBC], 16)

            def front(p, k, par):
                if p == "F_xp":
                    sp.wait_ge(f_r, k * NF + (F_USE["xp", 0] + 1))
                    sp.dma_start(bc_dram[bass.ds(k, 1), :, :, :].rearrange("o j s t -> (o j s) t"),
                                 XD[DR:XPR, :]).then_inc(bc_out, 16)

            def back(p, k, par):
                pass

            def turn(k, par, has_front, has_back):
                sp.wait_ge(bc_out, k * 16 + 16)
                for s in range(DS):
                    load(k, s)
                    if s == SEND_AT and has_front:
                        front("F_xp", k + 1, 1 - par)

            run(sp, turn, front, back)

        @block.tensor
        def _(pe):
            M = nc.tensor.matmul
            pe.sem_inc(k_r, KR0)
            pe.wait_ge(w_in, 16)

            def front(p, k, par):
                def bank_free(use):
                    if not (is_first(k) and F_USE[use] < 2):
                        pe.wait_ge(f_r, k * NF + max(F_USE[use] - 1, 0))

                if p == "F_T":
                    pe.wait_ge(xr_ok, k + 1)
                    for d in range(DK):
                        bank_free(("T", d))
                        for t in range(CTT):
                            last = nc.tensor.transpose(f_bank(("T", d))[:, t * P:(t + 1) * P], XR[:, t, d * P:(d + 1) * P], C["ident"][:, :])
                        last.then_inc(f_w, 1)
                elif p[:3] in ("F_x", "F_z") and p[3:] in ("01", "23"):
                    for n in (int(p[3]), int(p[4])):
                        use = (p[2], n)
                        pe.wait_ge(f_r, k * NF + 2)
                        bank_free(use)
                        for d in range(DK):
                            last = M(f_bank(use), weights(W_IN, 2 * DI, d, (0 if p[2] == "x" else DI) + n * P, P), xrT[:, d, :],
                                     start=(d == 0), stop=(d == DK - 1))
                        last.then_inc(f_w, 1)
                elif p == "F_xp":
                    use = ("xp", 0)
                    pe.wait_ge(w_in2, 16)
                    pe.wait_ge(u_ok, k + 1)
                    bank_free(use)
                    for e in range(EK):
                        last = M(f_bank(use, XPR), weights(W_XP, XPR, e, 0, XPR), U[:, e, :], start=(e == 0), stop=(e == EK - 1))
                    last.then_inc(f_w, 1)
                elif p == "F_dt":
                    pe.wait_ge(f_r, k * NF + (F_USE["xp", 0] + 1))
                    for n in range(EK):
                        bank_free(("dt", n))
                        M(f_bank(("dt", n)), MW[0:DR, W_DT + n * P:W_DT + (n + 1) * P], XD[0:DR, :], start=True, stop=True).then_inc(f_w, 1)

            def back(p, k, par):
                def bank_free(use):
                    pe.wait_ge(k_r, k * NK + (K_USE[use] - 1 + KR0))

                if p[:-1] in ("K_out", "K_pj"):
                    kind, at, ready = ("out", W_OUT, yz_ok) if p[:-1] == "K_out" else ("pj", W_PJ, q_ok)
                    a = int(p[-1])
                    pe.wait_ge(ready, k * 2 + 2)
                    bank_free((kind, a))
                    for t in (2 * a, 2 * a + 1):
                        for e in range(EK):
                            last = M(k_bank((kind, a))[:, (t % 2) * D:(t % 2 + 1) * D], T3[:, e, t * P:(t + 1) * P],
                                     weights(at, D, e, 0, D), start=(e == 0), stop=(e == EK - 1))
                    last.then_inc(k_w, 1)
                elif p == "K_T":
                    pe.wait_ge(hr_ok, k + 1)
                    for d in range(DK):
                        bank_free(("T", d))
                        for t in range(CTT):
                            last = nc.tensor.transpose(k_bank(("T", d))[:, t * P:(t + 1) * P], XR[:, t, d * P:(d + 1) * P], C["ident"][:, :])
                        last.then_inc(k_w, 1)
                elif p[:4] == "K_fc":
                    pe.wait_ge(k_r, k * NK + (K_USE["T", 1] + 1 + KR0))
                    for n in (int(p[4]), int(p[5])):
                        bank_free(("fc", n))
                        for d in range(DK):
                            last = M(k_bank(("fc", n)), weights(W_FC, 2 * D, d, n * P, P), hT[:, d, :], start=(d == 0), stop=(d == DK - 1))
                        last.then_inc(k_w, 1)

            def turn(k, par, has_front, has_back):
                for s in range(DS):
                    items(ON_PE, s, k, par, has_front, has_back, front, back)
                    if s == 0:
                        pe.wait_ge(diag_ok, 1)
                        pe.wait_ge(u_ok, k + 1)
                        for e in range(EK):
                            if has_back:
                                pe.wait_ge(yz_ok, k * 2 + (e // 2 - 1))
                            M(PS[:, B_Y + e, :], skip[:, e, :], U[:, e, :], start=True, stop=False)
                    for pair in range(2):
                        pe.wait_ge(g_ok, k * (2 * DS) + (2 * s + pair + 1))
                        for e in (2 * pair, 2 * pair + 1):
                            last = M(PS[:, B_Y + e, :], C["ident"][:, :], G[:, s % 2, e, :], start=False, stop=(s == DS - 1))
                        last.then_inc(g_read, 1)

            run(pe, turn, front, back)

        @block.scalar
        def _(act):
            def F(out, in_, func, **kw):
                return nc.scalar.activation(out, in_, func, **kw)

            def exp_set():
                act.preload_act_table_set("natural_log_exp_and_others")

            act.wait_ge(mc_in, 16)
            exp_set()
            F(A[:, :, :], mc[:, :, C_AL:C_AL + DS], ACT.Exp).then_inc(a_raw, 1)

            def evac(use, k, out, **kw):
                act.wait_ge(f_w, k * NF + (F_USE[use] + 1))
                F(out, f_bank(use), kw.pop("func", ACT.Copy), **kw).then_inc(f_r, 1)

            def front(p, k, par):
                if p == "F_T":
                    for d in range(DK):
                        evac(("T", d), k, xrT[:, d, :])
                elif p in ("F_x01", "F_x23"):
                    act.wait_ge(tail_ok, k + 1)
                    for n in (int(p[3]), int(p[4])):
                        evac(("x", n), k, XI[:, n, DC - 1:])
                elif p in ("F_z01", "F_z23"):
                    if not (isinstance(k, int) and k < 2):
                        act.wait_ge(yz_ok, k * 2 - 2)
                    for n in (int(p[3]), int(p[4])):
                        evac(("z", n), k, SZ[:, par, n, :])
                elif p[:3] == "F_c":
                    if not is_first(k):
                        act.wait_ge(dtu_ok, k * 2)
                        act.wait_ge(g_read, (k - 1) * (2 * DS) + 1)
                    for n in (int(p[3]), int(p[4])):
                        act.wait_ge(f_r, k * NF + (F_USE["x", n] + 1))
                        F(U[:, n, :], XI[:, n, 0:CT], ACT.Identity, scale=mc[:, n, C_CW:C_CW + 1],
                          bias=mc[:, n, C_CB:C_CB + 1]).then_inc(tap0_ok, 1)
                elif p == "F_silu":
                    act.wait_ge(f_r, k * NF + (F_USE["z", 3] + 1))
                    act.wait_ge(taps_ok, k * NTAP + NTAP)
                    F(U[:, :, :], U[:, :, :], ACT.Silu).then_inc(u_ok, 1)
                    F(SZ[:, par, :, :], SZ[:, par, :, :], ACT.Silu).then_inc(sz_ok, 1)
                    exp_set()
                elif p == "F_xp":
                    if not is_first(k):
                        act.wait_ge(bc_out, k * 16)
                    act.wait_ge(f_w, k * NF + (F_USE["xp", 0] + 1))
                    F(XD[0:XPR, :], f_bank(("xp", 0), XPR), ACT.Copy).then_inc(f_r, 1)
                elif p == "F_dt":
                    if not is_first(k):
                        act.wait_ge(dt_ok, k * 2)
                    for n in range(EK):
                        act.wait_ge(f_w, k * NF + (F_USE["dt", n] + 1))
                        bias = mc[:, n, C_DB:C_DB + 1]
                        F(DT[:, par, n, :], f_bank(("dt", n)), ACT.Relu, bias=bias)
                        F(sp1[:, n, :], f_bank(("dt", n)), ACT.Abs, bias=bias).then_inc(f_r, 1)
                    for pair in range(2):
                        es = slice(2 * pair, 2 * pair + 2)
                        act.wait_ge(f_r, k * NF + (F_USE["dt", 2 * pair + 1] + 1))
                        F(sp1[:, es, :], sp1[:, es, :], ACT.Exp, scale=-1.0).then_inc(sp_exp, 1)
                    for pair in range(2):
                        es = slice(2 * pair, 2 * pair + 2)
                        act.wait_ge(sp_exp, k * 2 + (pair + 1))
                        F(sp1[:, es, :], sp1[:, es, :], ACT.Ln, bias=1.0).then_inc(sp_ln, 1)

            def back(p, k, par):
                if p == "K_sq":
                    act.wait_ge(k_r, k * NK + 2 + KR0)
                    for t in range(CTT):
                        last = F(XR[:, t, :], XP[:, t, :], ACT.Square, accum_out=ssq[:, t:t + 1])
                    last.then_inc(sq_ok, 1)
                elif p == "K_hr":
                    act.wait_ge(rs_ok, k + 1)
                    for t in range(CTT):
                        last = F(XR[:, t, :], XP[:, t, :], ACT.Copy, scale=ssq[:, t:t + 1])
                    last.then_inc(hr_ok, 1)
                elif p == "K_T":
                    for d in range(DK):
                        act.wait_ge(k_w, k * NK + (K_USE["T", d] + 1))
                        F(hT[:, d, :], k_bank(("T", d)), ACT.Copy).then_inc(k_r, 1)
                elif p[:4] == "K_fc":
                    for n in (int(p[4]), int(p[5])):
                        act.wait_ge(k_w, k * NK + (K_USE["fc", n] + 1))
                        F(T3[:, n, :], k_bank(("fc", n)), ACT.Relu).then_inc(k_r, 1)
                    act.wait_ge(k_r, k * NK + (K_USE["fc", n] + 1 + KR0))
                    F(T3[:, n - 1:n + 1, :], T3[:, n - 1:n + 1, :], ACT.Square).then_inc(q_ok, 1)

            def decay(k, par, s):
                if s == 0:
                    act.wait_ge(a_ok, 1)
                    act.wait_ge(dt_ok, k * 2 + 2)
                for e in range(EK):
                    if not (is_first(k) and s == 0):
                        act.wait_ge(scanned, k * (DS * EK) + ((s - 1) * EK + e + 1))
                    F(dA[:, e, :], DT[:, par, e, :], ACT.Exp, scale=A[:, e, s:s + 1]).then_inc(dA_ok, 1)

            def turn(k, par, has_front, has_back):
                decay(k, par, 0)
                for s in range(DS):
                    if s + 1 < DS:
                        decay(k, par, s + 1)
                    items(ON_ACT, s, k, par, has_front, has_back, front, back)

            run(act, turn, front, back)

        @block.gpsimd
        def _(gp):
            G_ = nc.gpsimd
            def factors(call, n, chunks):
                sl = bass.ds(n * CTT, chunks * CTT)
                gp.wait_ge(var_ok, call + 1)
                G_.tensor_tensor(tk[:, 1:3, sl], tk[:, 1:3, sl], mhalf[:, :, 0:chunks * CTT], ALU.pow).then_inc(pow_ok, 1)
                gp.wait_ge(pow_ok, call + 1)
                G_.tensor_tensor(rrms[:, sl], rrms[:, sl], rstd[:, sl], ALU.mult).then_inc(stat_ok, chunks)

            factors(0, 0, 1)
            factors(1, 1, 1)
            with gp.Fori(1, MCH // 2, 1) as m:
                factors(m + 1, m * 2, 2)

            def front(p, k, par):
                if p == "F_du":
                    for pair in range(2):
                        es = slice(2 * pair, 2 * pair + 2)
                        gp.wait_ge(sp_ln, k * 2 + (pair + 1))
                        G_.tensor_tensor(DT[:, par, es, :], DT[:, par, es, :], sp1[:, es, :], ALU.add).then_inc(dt_ok, 1)

            def back(p, k, par):
                if p == "K_v":
                    gp.wait_ge(v_ok, k + 1)
                    G_.tensor_tensor(ssq[:, :], ssq[:, :], mhalf[:, 0, 0:CTT], ALU.pow).then_inc(rs_ok, 1)

            def turn(k, par, has_front, has_back):
                gp.wait_ge(dtu_ok, k * 2 + 2)
                for s in range(DS):
                    gp.wait_ge(b_in[s % NBC], k * (16 * DS // NBC) + 16 * (s // NBC + 1))
                    for pair in range(2):
                        if not (is_first(k) and s == 0):
                            gp.wait_ge(scanned, k * (DS * EK) + ((s - 1) * EK + 2 * pair + 2))
                        es = slice(2 * pair, 2 * pair + 2)
                        G_.tensor_tensor(dB[:, es, :], DTU[:, par, es, :], BC[:, s % NBC, 0:1, :].to_broadcast([P, 2, CT]),
                                         ALU.mult).then_inc(dB_ok, 1)
                    items(ON_POOL, s, k, par, has_front, has_back, front, back)

            run(gp, turn, front, back)

        @block.vector
        def _(dve):
            V = nc.vector
            link = chain(dve, dch)
            V.memset(mhalf[:, :, :], -0.5)
            link(V.memset(mask[:, :].bitcast(mybir.dt.int32), -1))
            V.memset(ST[:, :, :], 0.0)
            V.memset(XI[:, :, 0:DC - 1], 0.0).then_inc(tail_ok, 1)
            for k in range(0, MCH, MCH // BATCH):
                link(V.memset(mask[:, k:k + 1].bitcast(mybir.dt.int32), 0))

            def tile(k, t, n=1):
                x = X[:, bass.ds(k * CTT + t, n), :]
                return x.rearrange("p o d -> p (o d)") if n == 1 else x

            def col(a, k, t):
                return a[:, bass.ds(k * CTT + t, 1)]

            def join(m, b):
                n = m * 2 + b
                jlink = chain(dve, join_ch, n * TOPK)
                dve.wait_ge(landed[b], m * (16 * TOPK) + 16 * TOPK)
                for c in range(TOPK):
                    for t in range(CTT):
                        last = V.scalar_tensor_tensor(tile(n, t), outputs(b)[:, c * CTT + t, :], R["w"][:, c, bass.ds(n * CTT + t, 1)],
                                                      tile(n, t), ALU.mult, ALU.add)
                    jlink(last)
                dve.sem_inc(joined, 1)

            LINKS = 10

            def statistics(call, n, chunks):
                slink = chain(dve, stat_ch, call * LINKS)
                for t in range(chunks * CTT):
                    last = V.bn_stats(st[:, t, :], tile(n, t))
                slink(last)
                w = chunks * CTT
                mn, rs, rr = (a[:, bass.ds(n * CTT, w)] for a in (mean, rstd, rrms))
                v, dif, s = var[:, 0, 0:w], var[:, 1, 0:w], st[:, 0:w, :]
                V.tensor_tensor(mn, s[:, :, 1], s[:, :, 4], ALU.add)
                V.tensor_tensor(dif, s[:, :, 1], s[:, :, 4], ALU.subtract)
                slink(V.tensor_tensor(v, s[:, :, 2], s[:, :, 5], ALU.add))
                slink(V.tensor_scalar(mn, mn, 0.5, None, ALU.mult))
                slink(V.tensor_tensor(dif, dif, dif, ALU.mult))
                slink(V.tensor_scalar(dif, dif, 0.25, None, ALU.mult))
                slink(V.scalar_tensor_tensor(v, v, 1.0 / D, dif, ALU.mult, ALU.add))
                slink(V.tensor_scalar(rs, v, LN_EPS, None, ALU.add))
                slink(V.reciprocal(rr, rs))
                slink(V.tensor_tensor(rr, rr, v, ALU.mult))
                slink(V.tensor_scalar(rr, rr, RMS_EPS, None, ALU.add))
                dve.sem_inc(var_ok, 1)

            def constants():
                dve.wait_ge(mc_in, 16)
                for e in range(EK):
                    last = V.tensor_scalar(skip[:, e, :], C["ident"][:, :], mc[:, e, C_D:C_D + 1], None, ALU.mult)
                last.then_inc(diag_ok, 1)
                dve.wait_ge(a_raw, 1)
                V.tensor_scalar(A[:, :, :], A[:, :, :], -1.0, None, ALU.mult).then_inc(a_ok, 1)

            join(0, 0)
            statistics(0, 0, 1)

            def front(p, k, par):
                if is_first(k) and p == "F_c01":
                    constants()
                    join(0, 1)
                    statistics(1, 1, 1)
                if is_first(k) and p == "F_du":
                    with dve.Fori(1, MCH // 2, 1) as m:
                        for b in range(2):
                            join(m, b)
                        statistics(m + 1, m * 2, 2)
                if p == "F_xr":
                    dve.wait_ge(stat_ok, k + 1)
                    for t in range(CTT):
                        last = V.tensor_scalar(XR[:, t, :], tile(k, t), col(mean, k, t), col(rrms, k, t), ALU.subtract, ALU.mult)
                    last.then_inc(xr_ok, 1)
                    if not is_first(k):
                        dve.wait_ge(taps_ok, k * NTAP)
                        dve.wait_ge(tap0_ok, k * EK)
                        V.tensor_tensor(XI[:, :, 0:DC - 1].bitcast(U32), XI[:, :, CT:].bitcast(U32),
                                        mask[:, bass.ds(k, 1)].unsqueeze(2).to_broadcast([P, EK, DC - 1]),
                                        ALU.bitwise_and).then_inc(tail_ok, 1)
                elif p[:3] == "F_c":
                    lo = int(p[3])
                    for tap in range(1, DC):
                        for n in (lo, lo + 1):
                            if tap == 1:
                                dve.wait_ge(tap0_ok, k * EK + (n + 1))
                            else:
                                dve.wait_ge(taps_ok, k * NTAP + (lo * (DC - 1) + 2 * (tap - 2) + (n - lo) + 1))
                            V.scalar_tensor_tensor(U[:, n, :], XI[:, n, tap:tap + CT], mc[:, n, C_CW + tap:C_CW + tap + 1],
                                                   U[:, n, :], ALU.mult, ALU.add).then_inc(taps_ok, 1)
                elif p == "F_du":
                    for pair in range(2):
                        es = slice(2 * pair, 2 * pair + 2)
                        dve.wait_ge(dt_ok, k * 2 + (pair + 1))
                        V.tensor_tensor(DTU[:, par, es, :], DT[:, par, es, :], U[:, es, :], ALU.mult).then_inc(dtu_ok, 1)

            def back(p, k, par):
                if p == "K_yz":
                    dve.wait_ge(sz_ok, k + 1)
                    for pair in range(2):
                        es = slice(2 * pair, 2 * pair + 2)
                        dve.wait_ge(g_read, k * (2 * DS) + (2 * DS - 1 + pair))
                        V.tensor_tensor(T3[:, es, :], PS[:, B_Y + 2 * pair:B_Y + 2 * pair + 2, :], SZ[:, par, es, :], ALU.mult).then_inc(yz_ok, 1)
                elif p[:-1] == "K_out":
                    a = int(p[-1])
                    for t in (2 * a, 2 * a + 1):
                        last = V.tensor_scalar(XP[:, t, :], tile(k, t), col(mean, k, t), col(rstd, k, t), ALU.subtract, ALU.mult)
                    last.then_inc(xn_ok, 1)
                    dve.wait_ge(xn_ok, k * 2 + (a + 1))
                    dve.wait_ge(k_w, k * NK + (K_USE["out", a] + 1))
                    xp = XP[:, 2 * a:2 * a + 2, :]
                    V.tensor_tensor(xp, xp, k_bank(("out", a)).rearrange("p (t d) -> p t d", t=2), ALU.add).then_inc(k_r, 1)
                elif p == "K_v":
                    dve.wait_ge(sq_ok, k + 1)
                    V.tensor_scalar(ssq[:, :], ssq[:, :], 1.0 / D, RMS_EPS, ALU.mult, ALU.add).then_inc(v_ok, 1)
                elif p[:-1] == "K_pj":
                    a = int(p[-1])
                    x = tile(k, 2 * a, 2)
                    V.tensor_tensor(x, x, XP[:, 2 * a:2 * a + 2, :], ALU.add).then_inc(xa_ok, 1)
                    dve.wait_ge(xa_ok, k * 2 + (a + 1))
                    dve.wait_ge(k_w, k * NK + (K_USE["pj", a] + 1))
                    V.tensor_tensor(x, x, k_bank(("pj", a)).rearrange("p (t d) -> p t d", t=2), ALU.add).then_inc(k_r, 1)

            def turn(k, par, has_front, has_back):
                items(ON_DVE, -1, k, par, has_front, has_back, front, back)
                for s in range(DS):
                    if s > 0 or not is_first(k):
                        dve.wait_ge(kept, k * DS + s)
                    for e in range(EK):
                        dve.wait_ge(dA_ok, k * (DS * EK) + (s * EK + e + 1))
                        if e % 2 == 0:
                            dve.wait_ge(dB_ok, k * (2 * DS) + (2 * s + e // 2 + 1))
                        V.tensor_tensor_scan(H[:, e, :], dA[:, e, :], dB[:, e, :], ST[:, s, e:e + 1], ALU.mult, ALU.add).then_inc(scanned, 1)
                    if s == 0 and has_back:
                        back("K_yz", k - 1, 1 - par)
                    dve.wait_ge(c_in[s % NBC], k * (16 * DS // NBC) + 16 * (s // NBC + 1))
                    for pair in range(2):
                        es = slice(2 * pair, 2 * pair + 2)
                        dve.wait_ge(scanned, k * (DS * EK) + (s * EK + 2 * pair + 2))
                        if not (is_first(k) and s < 2):
                            dve.wait_ge(g_read, k * (2 * DS) + (2 * s - 3 + pair))
                        V.tensor_tensor(G[:, s % 2, es, :], H[:, es, :], BC[:, s % NBC, 1:2, :].to_broadcast([P, 2, CT]), ALU.mult).then_inc(g_ok, 1)
                    V.tensor_tensor(ST[:, s, :].bitcast(U32), H[:, :, CT - 1].bitcast(U32),
                                    mask[:, bass.ds(k + 1, 1)].to_broadcast([P, EK]), ALU.bitwise_and).then_inc(kept, 1)
                    items(ON_DVE, s, k, par, has_front, has_back, front, back)

            run(dve, turn, front, back)


def build(nc, x, gate, gate_b, b1, b2, w1, w2, mamba_w, mamba_c, out):
    ctx = ExitStack()
    with ctx:
        keep = buf_maker(nc, ctx, "keep")
        X = keep("X", [P, TT, D])
        C = {
            "whole": ctx, "sems": {},
            "ident": keep("ident", [P, P]), "upper": keep("upper", [P, P], BF16), "onesb": keep("onesb", [P, P], BF16),
            "gate": keep("gate", [P, DK, EXPERTS]), "gb": keep("gb", [P, EXPERTS]), "rank": keep("rank", [P, EXPERTS]),
            "region": keep("region", [P, EXPERTS]), "b1": keep("b1", [P, EXPERTS * FK]),
        }
        PS = ctx.enter_context(nc.psum_tensor("PS", [P, 8, 512], FP32))
        xrows = nc.dram_tensor("xrows", (TOKENS, D), FP32, kind="Internal").ap()
        yrows = nc.dram_tensor("yrows", (TOPK * TOKENS, D), FP32, kind="Internal").ap()
        setup(nc, C, gate, gate_b, b1)
        R = {"w": keep("w", [P, TOPK, TT])}
        tokens_to_experts(nc, "0", X, C, PS, R, xrows, yrows, w1, w2, b2, x)
        bc_dram = nc.dram_tensor("bc_rows", (MCH, 2, DS, CT), FP32, kind="Internal").ap()
        mamba(nc, X, C, PS, R, yrows, mamba_w, mamba_c, bc_dram)
        clear(nc, C, ("r", "e"))
        tokens_to_experts(nc, "1", X, C, PS, R, xrows, yrows, w1, w2, b2, None)
        combine(nc, "c1", C, X, R, yrows, out)


def tokens_to_experts(nc, n, X, C, PS, R, xrows, yrows, w1, w2, b2, x_dram):
    ctx = ExitStack()
    with ctx:
        sb = buf_maker(nc, ctx, f"layer{n}")
        R = dict(R, token=sb("token", [P, BLOCKS], U32), dest=sb("dest", [P, BLOCKS], U32),
                 rows=sb("rows", [P, EXPERTS], U32))
        raw = sb("raw", [P, 4, FF])
        route(nc, "r" + n, X, C, PS, R, raw, w1, w2, xrows, yrows, x_dram, x_dram is not None)
        experts(nc, "e" + n, C, PS, R, raw, xrows, yrows, w1, w2, b2)


def clear(nc, C, tags):
    numbers = sorted(h.num for name, h in C["sems"].items() if name.split("_")[0] in tags)
    with nc.Block() as block:
        @block.gpsimd
        def _(gp):
            start = 0
            for n in range(1, len(numbers) + 1):
                if n == len(numbers) or numbers[n] != numbers[n - 1] + 1:
                    gp.sem_clear(range(numbers[start], numbers[n - 1] + 1))
                    start = n


def setup(nc, C, gate, gate_b, b1):
    ctx = ExitStack()
    with ctx:
        sem = sem_maker(nc, C, "s")
        loaded, made = sem("loaded"), sem("made")
        ints = ctx.enter_context(nc.sbuf_tensor("ints", [P, 2, EXPERTS], mybir.dt.int32))
        block = ctx.enter_context(nc.Block())

        @block.sync
        def _(sp):
            sp.dma_start(C["gate"][:, :, :], gate).then_inc(loaded, 16)
            sp.dma_start(C["gb"][:, :], gate_b.to_broadcast([P, EXPERTS])).then_inc(loaded, 16)
            sp.dma_start(C["b1"][:, :], b1).then_inc(loaded, 16)
            sp.wait_ge(loaded, 48)

        @block.gpsimd
        def _(gp):
            G = nc.gpsimd
            G.memset(C["ident"][:, :], 0.0)
            G.memset(C["upper"][:, :], 1.0)
            G.memset(C["onesb"][:, :], 1.0)
            G.iota(ints[:, 0, :], pattern=[[-1, EXPERTS]], base=EXPERTS, channel_multiplier=0)
            G.iota(ints[:, 1, :], pattern=[[ROWS_E, EXPERTS]], base=0, channel_multiplier=0).then_inc(made, 1)
            gp.wait_ge(made, 1)
            G.affine_select(out=C["ident"][:, :], in_=C["ident"][:, :], compare_op=ALU.not_equal, fill=1.0,
                            base=0, pattern=[[-1, P]], channel_multiplier=1)
            G.affine_select(out=C["upper"][:, :], in_=C["upper"][:, :], compare_op=ALU.is_ge, fill=0.0,
                            base=0, pattern=[[1, P]], channel_multiplier=-1)
            G.tensor_copy(C["rank"][:, :], ints[:, 0, :])
            G.tensor_copy(C["region"][:, :], ints[:, 1, :]).then_inc(made, 1)


def kernel(**inputs):
    import numpy as np
    import concourse.bacc as bacc
    from concourse import mybir as _mybir
    from concourse.bass_utils import run_bass_kernel_spmd as run

    def g(name):
        return np.asarray(inputs[name])

    def tiles(a):
        return np.ascontiguousarray(a.reshape(-1, P, a.shape[1]).transpose(1, 0, 2))

    def block_of(a):
        t = tiles(a)
        return t.reshape(P, -1)

    dt_w = np.zeros((P, DI), np.float32)
    dt_w[:DR] = g("L0_attn_dt_proj_w").T
    arrays = {
        "x": g("L0_attn_x").reshape(TOKENS, D),
        "gate": tiles(g("L0_ffn_gate_w").T),
        "gate_b": g("L0_ffn_gate_b").reshape(1, EXPERTS),
        "b1": g("L0_ffn_b1").reshape(EXPERTS * FK, P).T,
        "b2": g("L0_ffn_b2").reshape(1, EXPERTS * D),
        "w1": g("L0_ffn_W1"),
        "w2": g("L0_ffn_W2"),
        "mamba_w": np.concatenate([
            block_of(g("L0_attn_in_proj_w").T), block_of(g("L0_attn_x_proj_w").T), dt_w,
            block_of(g("L0_attn_out_proj_w").T), block_of(g("L0_attn_c_fc_w").T), block_of(g("L0_attn_c_proj_w").T)], axis=1),
        "mamba_c": tiles(np.concatenate([
            g("L0_attn_conv_w"), g("L0_attn_conv_b")[:, None], g("L0_attn_dt_proj_b")[:, None], g("L0_attn_D")[:, None],
            g("L0_attn_A_log")], axis=1)),
    }
    nc = bacc.Bacc("TRN2", target_bir_lowering=False, num_devices=1)
    feed, args = {}, []
    for name, a in arrays.items():
        feed[name] = np.ascontiguousarray(a)
        args.append(nc.dram_tensor(name, a.shape, _mybir.dt.from_np(a.dtype), kind="ExternalInput").ap())
    args.append(nc.dram_tensor("out", (TOKENS, D), _mybir.dt.float32, kind="ExternalOutput").ap())
    build(nc, *args)
    r = run(nc, [feed], core_ids=[0])
    return r.results[0]["out"].reshape(BATCH, TOKENS // BATCH, D)
```
